# Optimizing a Trainium2 kernel written in Bass

```python
import numpy as np
import jax
import jax.numpy as jnp

def _softmax(x, axis=-1):
    return jax.nn.softmax(x, axis=axis)

def _gelu(x):
    return jax.nn.gelu(x, approximate=True)

def _silu(x):
    return jax.nn.silu(x)

def _sigmoid(x):
    return jax.nn.sigmoid(x)

def _layernorm(x, axis=-1, eps=1e-05):
    m = jnp.mean(x, axis=axis, keepdims=True)
    v = jnp.var(x, axis=axis, keepdims=True)
    return (x - m) / jnp.sqrt(v + eps)

def _scatter_add(tgt, idx, src, axis=0):
    return tgt.at[idx].add(src)

def _segment_sum(src, seg, n):
    return jax.ops.segment_sum(src, seg, n)
kernel_name = 'mk_lm_tower_d1_tok_ids256_r4_d14c62'

def setup_inputs(seed: int=0):
    np.random.seed(seed)
    _w = jnp.asarray

    def _rec_inputs():
        import jax
        import jax.numpy as jnp
        _rk = jax.random.key(seed)
        x = jax.random.randint(jax.random.fold_in(_rk, 1), (64, 128), 0, 160, jnp.int32)
        mask_BS_i1_0 = jnp.where(jnp.ones((64, 128), dtype=bool), 1, 0).astype(jnp.int32)
        itok_BS_0_479 = jax.random.randint(jax.random.fold_in(_rk, 22), (64, 128), 0, 120, jnp.int32)
        mask_BS_b1_0 = jnp.ones((64, 128), dtype=bool)
        return (x, mask_BS_i1_0, itok_BS_0_479, mask_BS_b1_0)
    x, mask_BS_i1_0, itok_BS_0_479, mask_BS_b1_0 = _rec_inputs()

    def _L0_tok_setup():
        import jax, jax.numpy as jnp
        import numpy as np
        P_, H_, W_, D = (2, 120, 160, 64)
        B, N = (16, 4096)
        EPS = 1e-05

        def _layernorm(h, g, b):
            m = jnp.mean(h, axis=-1, keepdims=True)
            v = jnp.mean(jnp.square(h - m), axis=-1, keepdims=True)
            return (h - m) * jax.lax.rsqrt(v + EPS) * g + b
        key = jax.random.key(seed)
        ks = jax.random.split(key, 8)
        p = jax.random.randint(ks[0], (B, N), 0, P_, dtype=jnp.int64 if jax.config.jax_enable_x64 else jnp.int32)
        y = jax.random.randint(ks[1], (B, N), 0, H_, dtype=p.dtype)
        x = jax.random.randint(ks[2], (B, N), 0, W_, dtype=p.dtype)
        valid_mask = jax.random.randint(ks[3], (B, N), 0, 2) > 0
        d4, d2 = (D // 4, D // 2)
        W1 = jax.random.normal(ks[4], (3, d4), jnp.float32) / np.sqrt(3)
        W2 = jax.random.normal(ks[5], (d4, d2), jnp.float32) / np.sqrt(d4)
        W3 = jax.random.normal(ks[6], (d2, D), jnp.float32) / np.sqrt(d2)
        g1, b1 = (jnp.ones((d4,), jnp.float32), jnp.zeros((d4,), jnp.float32))
        g2, b2 = (jnp.ones((d2,), jnp.float32), jnp.zeros((d2,), jnp.float32))
        g3, b3 = (jnp.ones((D,), jnp.float32), jnp.zeros((D,), jnp.float32))
        return {'p': p, 'y': y, 'x': x, 'valid_mask': valid_mask, 'W1': W1, 'g1': g1, 'b1': b1, 'W2': W2, 'g2': g2, 'b2': b2, 'W3': W3, 'g3': g3, 'b3': b3}
    _L0_tok_all = _L0_tok_setup()
    _L0_tok_in = {k: v for k, v in _L0_tok_all.items() if k in ('W1', 'g1', 'b1', 'W2', 'g2', 'b2', 'W3', 'g3', 'b3')}
    del _L0_tok_all

    def _L0_attn_setup():
        import jax, jax.numpy as jnp
        import numpy as np
        D_ATT = 64
        D_GROUP = 32
        N_GROUP = D_ATT // D_GROUP
        key = jax.random.key(seed)
        ks = jax.random.split(key, 6)
        B, L = (4, 128)
        import math
        s = 1.0 / math.sqrt(D_ATT)
        return {'x': jax.random.normal(ks[0], (B, L, D_ATT), dtype=jnp.float32), 'Wq': jax.random.normal(ks[1], (D_ATT, D_ATT), dtype=jnp.float32) * s * 0.06, 'Wk': jax.random.normal(ks[2], (D_ATT, D_ATT), dtype=jnp.float32) * s * 0.06, 'Wv': jax.random.normal(ks[3], (D_ATT, D_ATT), dtype=jnp.float32) * s * 0.06, 'w_mlp': jax.random.normal(ks[4], (D_GROUP,), dtype=jnp.float32) * 0.1, 'b_mlp': jax.random.normal(ks[5], (1,), dtype=jnp.float32) * 0.1}
    _L0_attn_all = _L0_attn_setup()
    _L0_attn_in = {k: v for k, v in _L0_attn_all.items() if k in ('Wq', 'Wk', 'Wv', 'w_mlp', 'b_mlp')}
    del _L0_attn_all

    def _L0_ffn_setup():
        import jax, jax.numpy as jnp
        import numpy as np
        B, T, C = (64, 96, 64)
        NH, NKV = (4, 2)
        HD = C // NH
        NREP = NH // NKV
        NE, TOPK = (8, 2)
        HID = int(8 / 3 * C)
        EPS_RMS = 1e-06

        def _rope_tables(t_len):
            inv_freq = 1.0 / 10000.0 ** (np.arange(0, HD, 2, dtype=np.float32) / HD)
            t = np.arange(t_len, dtype=np.float32)
            freqs = np.outer(t, inv_freq)
            emb = np.concatenate([freqs, freqs], axis=-1)
            return (jnp.asarray(np.cos(emb)), jnp.asarray(np.sin(emb)))

        def _rotate_half(x):
            h = x.shape[-1] // 2
            return jnp.concatenate([-x[..., h:], x[..., :h]], axis=-1)

        def _rmsnorm(v, w):
            return v * jax.lax.rsqrt(jnp.mean(v * v, axis=-1, keepdims=True) + EPS_RMS) * w
        key = jax.random.key(seed)
        ks = jax.random.split(key, 10)
        s = lambda k, shape: jax.random.normal(k, shape, jnp.float32) * 0.02
        return {'x': jax.random.normal(ks[0], (B, T, C), jnp.float32), 'ln1_w': jnp.ones((C,), jnp.float32), 'ln2_w': jnp.ones((C,), jnp.float32), 'wq': s(ks[1], (NH * HD, C)), 'wk': s(ks[2], (NKV * HD, C)), 'wv': s(ks[3], (NKV * HD, C)), 'wo': s(ks[4], (C, C)), 'router_w': s(ks[5], (NE, C)), 'w1': s(ks[6], (NE, HID, C)), 'w2': s(ks[7], (NE, C, HID)), 'w3': s(ks[8], (NE, HID, C))}
    _L0_ffn_all = _L0_ffn_setup()
    _L0_ffn_in = {k: v for k, v in _L0_ffn_all.items() if k in ('ln1_w', 'ln2_w', 'wq', 'wk', 'wv', 'wo', 'router_w', 'w1', 'w2', 'w3')}
    del _L0_ffn_all
    return {'x': x, 'mask_BS_i1_0': mask_BS_i1_0, 'itok_BS_0_479': itok_BS_0_479, 'mask_BS_b1_0': mask_BS_b1_0, 'L0_tok_W1': _L0_tok_in['W1'], 'L0_tok_g1': _L0_tok_in['g1'], 'L0_tok_b1': _L0_tok_in['b1'], 'L0_tok_W2': _L0_tok_in['W2'], 'L0_tok_g2': _L0_tok_in['g2'], 'L0_tok_b2': _L0_tok_in['b2'], 'L0_tok_W3': _L0_tok_in['W3'], 'L0_tok_g3': _L0_tok_in['g3'], 'L0_tok_b3': _L0_tok_in['b3'], 'L0_attn_Wq': _L0_attn_in['Wq'], 'L0_attn_Wk': _L0_attn_in['Wk'], 'L0_attn_Wv': _L0_attn_in['Wv'], 'L0_attn_w_mlp': _L0_attn_in['w_mlp'], 'L0_attn_b_mlp': _L0_attn_in['b_mlp'], 'L0_ffn_ln1_w': _L0_ffn_in['ln1_w'], 'L0_ffn_ln2_w': _L0_ffn_in['ln2_w'], 'L0_ffn_wq': _L0_ffn_in['wq'], 'L0_ffn_wk': _L0_ffn_in['wk'], 'L0_ffn_wv': _L0_ffn_in['wv'], 'L0_ffn_wo': _L0_ffn_in['wo'], 'L0_ffn_router_w': _L0_ffn_in['router_w'], 'L0_ffn_w1': _L0_ffn_in['w1'], 'L0_ffn_w2': _L0_ffn_in['w2'], 'L0_ffn_w3': _L0_ffn_in['w3']}

def reference(x, mask_BS_i1_0, itok_BS_0_479, mask_BS_b1_0, L0_tok_W1, L0_tok_g1, L0_tok_b1, L0_tok_W2, L0_tok_g2, L0_tok_b2, L0_tok_W3, L0_tok_g3, L0_tok_b3, L0_attn_Wq, L0_attn_Wk, L0_attn_Wv, L0_attn_w_mlp, L0_attn_b_mlp, L0_ffn_ln1_w, L0_ffn_ln2_w, L0_ffn_wq, L0_ffn_wk, L0_ffn_wv, L0_ffn_wo, L0_ffn_router_w, L0_ffn_w1, L0_ffn_w2, L0_ffn_w3):
    import jax
    import jax.numpy as jnp

    def _L0_tok_ref(p, y, x, valid_mask, W1, g1, b1, W2, g2, b2, W3, g3, b3):
        import jax, jax.numpy as jnp
        import numpy as np
        P_, H_, W_, D = (2, 120, 160, 64)
        B, N = (16, 4096)
        EPS = 1e-05

        def _layernorm(h, g, b):
            m = jnp.mean(h, axis=-1, keepdims=True)
            v = jnp.mean(jnp.square(h - m), axis=-1, keepdims=True)
            return (h - m) * jax.lax.rsqrt(v + EPS) * g + b
        pf = p.astype(jnp.float32) * (2.0 / (P_ - 1)) - 1.0
        yf = y.astype(jnp.float32) * (2.0 / (H_ - 1)) - 1.0
        xf = x.astype(jnp.float32) * (2.0 / (W_ - 1)) - 1.0
        c = jnp.stack((xf, yf, pf), axis=2)
        c = c * valid_mask.astype(jnp.float32)[..., None]
        h = jax.nn.relu(_layernorm(c @ W1, g1, b1))
        h = jax.nn.relu(_layernorm(h @ W2, g2, b2))
        out = _layernorm(h @ W3, g3, b3)
        return out

    def _L0_attn_ref(x, Wq, Wk, Wv, w_mlp, b_mlp):
        import jax, jax.numpy as jnp
        import numpy as np
        D_ATT = 64
        D_GROUP = 32
        N_GROUP = D_ATT // D_GROUP
        B, L, d_att = x.shape
        G, Dg = (N_GROUP, D_GROUP)
        Q = x @ Wq.T
        K = x @ Wk.T
        V = x @ Wv.T
        Qg = Q.reshape(B, L, 1, G, Dg)
        Kg = K.reshape(B, 1, L, G, Dg)
        diff = Qg - Kg
        attn = jnp.einsum('bqkgd,d->bqkg', jax.nn.relu(diff), w_mlp) + b_mlp[0]
        attn = jax.nn.relu(attn)
        attn = jax.nn.softmax(attn, axis=2)
        Vg = V.reshape(B, L, Dg, G)
        out = jnp.einsum('bqkg,bkdg->bqdg', attn, Vg)
        return out.reshape(B, L, d_att)

    def _L0_ffn_ref(x, ln1_w, ln2_w, wq, wk, wv, wo, router_w, w1, w2, w3):
        import jax, jax.numpy as jnp
        import numpy as np
        B, T, C = (64, 96, 64)
        NH, NKV = (4, 2)
        HD = C // NH
        NREP = NH // NKV
        NE, TOPK = (8, 2)
        HID = int(8 / 3 * C)
        EPS_RMS = 1e-06

        def _rope_tables(t_len):
            inv_freq = 1.0 / 10000.0 ** (np.arange(0, HD, 2, dtype=np.float32) / HD)
            t = np.arange(t_len, dtype=np.float32)
            freqs = np.outer(t, inv_freq)
            emb = np.concatenate([freqs, freqs], axis=-1)
            return (jnp.asarray(np.cos(emb)), jnp.asarray(np.sin(emb)))

        def _rotate_half(x):
            h = x.shape[-1] // 2
            return jnp.concatenate([-x[..., h:], x[..., :h]], axis=-1)

        def _rmsnorm(v, w):
            return v * jax.lax.rsqrt(jnp.mean(v * v, axis=-1, keepdims=True) + EPS_RMS) * w
        Bx, Tx, Cx = x.shape
        h = _rmsnorm(x, ln1_w)
        q = (h @ wq.T).reshape(Bx, Tx, NH, HD).transpose(0, 2, 1, 3)
        k = (h @ wk.T).reshape(Bx, Tx, NKV, HD).transpose(0, 2, 1, 3)
        v = (h @ wv.T).reshape(Bx, Tx, NKV, HD).transpose(0, 2, 1, 3)
        cos, sin = _rope_tables(Tx)
        cos, sin = (cos[None, None], sin[None, None])
        q = q * cos + _rotate_half(q) * sin
        k = k * cos + _rotate_half(k) * sin
        k = jnp.repeat(k, NREP, axis=1)
        v = jnp.repeat(v, NREP, axis=1)
        scores = jnp.einsum('bhtd,bhsd->bhts', q, k) / jnp.sqrt(jnp.float32(HD))
        causal = jnp.tril(jnp.ones((Tx, Tx), dtype=bool))
        scores = jnp.where(causal[None, None], scores, jnp.float32(-1e+30))
        att = jax.nn.softmax(scores, axis=-1)
        y = jnp.einsum('bhts,bhsd->bhtd', att, v).transpose(0, 2, 1, 3).reshape(Bx, Tx, Cx)
        x = x + y @ wo.T
        flat = _rmsnorm(x, ln2_w).reshape(-1, Cx)
        probs = jax.nn.softmax(flat @ router_w.T, axis=-1)
        tp, ti = jax.lax.top_k(probs, TOPK)
        tp = tp / (jnp.sum(tp, axis=-1, keepdims=True) + 1e-09)
        weights = jnp.sum(tp[..., None] * jax.nn.one_hot(ti, NE, dtype=flat.dtype), axis=1)
        out = jnp.zeros_like(flat)
        for e in range(NE):
            hh = jax.nn.silu(flat @ w1[e].T) * (flat @ w3[e].T)
            out = out + weights[:, e:e + 1] * (hh @ w2[e].T)
        return x + out.reshape(Bx, Tx, Cx)
    h = _L0_tok_ref(mask_BS_i1_0, itok_BS_0_479, x, mask_BS_b1_0, L0_tok_W1, L0_tok_g1, L0_tok_b1, L0_tok_W2, L0_tok_g2, L0_tok_b2, L0_tok_W3, L0_tok_g3, L0_tok_b3)
    h = h + _L0_attn_ref(_layernorm(h, axis=-1), L0_attn_Wq, L0_attn_Wk, L0_attn_Wv, L0_attn_w_mlp, L0_attn_b_mlp)
    h = h + _L0_ffn_ref(_layernorm(h, axis=-1), L0_ffn_ln1_w, L0_ffn_ln2_w, L0_ffn_wq, L0_ffn_wk, L0_ffn_wv, L0_ffn_wo, L0_ffn_router_w, L0_ffn_w1, L0_ffn_w2, L0_ffn_w3)
    return h

_drawn_inputs = setup_inputs


def setup_inputs(seed=0):
    import zlib

    import numpy as np

    out = dict(_drawn_inputs(seed))
    spreads = {'L0_tok_g1': (1.0, 0.2),
     'L0_tok_b1': (0.0, 0.1),
     'L0_tok_g2': (1.0, 0.2),
     'L0_tok_b2': (0.0, 0.1),
     'L0_tok_g3': (1.0, 0.2),
     'L0_tok_b3': (0.0, 0.1),
     'L0_ffn_ln1_w': (1.0, 0.6),
     'L0_ffn_ln2_w': (1.0, 0.6)}
    factors = {'L0_attn_Wq': 8.0,
     'L0_attn_Wk': 8.0,
     'L0_attn_w_mlp': 29.388,
     'L0_ffn_wq': 8.0,
     'L0_ffn_wk': 8.0,
     'L0_ffn_wv': 6.564,
     'L0_ffn_wo': 5.647,
     'L0_ffn_router_w': 8.0,
     'L0_ffn_w1': 8.0,
     'L0_ffn_w2': 8.0,
     'L0_ffn_w3': 8.0}
    for name, (base, spread) in spreads.items():
        noise = np.random.default_rng([zlib.crc32(name.encode()), seed]).standard_normal(out[name].shape)
        drawn = base * np.exp(spread * noise) if base else spread * noise
        out[name] = jnp.asarray(drawn.astype(out[name].dtype))
    for name, factor in factors.items():
        out[name] = (out[name] * factor).astype(out[name].dtype)
    return out
```

```python
from contextlib import ExitStack

import numpy as np

import concourse.bass as bass
from concourse import mybir

ALU = mybir.AluOpType
ACT = mybir.ActivationFunctionType
AX = mybir.AxisListType.X
F32 = mybir.dt.float32
F16 = mybir.dt.float16
I32 = mybir.dt.int32
U8 = mybir.dt.uint8

P = 128
B, T, C = 64, 128, 64
PAIRS, GROUPS = B // 2, B // 4
G2, DG = 2, 32
BG = 4
D1, D2 = 16, 32
NH, NKV, HD = 4, 2, 16
HP = 32
NE, HID = 8, 170
NT = -(-NE * HID // P)
BIG = -1e30
LN_EPS, RMS_EPS, TOP_EPS = 1e-5, 1e-6, 1e-9

CH = 16
N_DVE = 64
N_POOL = 48
N_ACT = T - N_DVE - N_POOL
NP = N_POOL // CH

VW = DG + 1
KW = HD + 1


def columns(parts):
    at, out = 0, {}
    for name, width in parts:
        out[name] = (at, at + width)
        at += width
    return out, at


WCOL, WWIDTH = columns([
    ("qk", 256), ("v", 128), ("rope", 1024), ("vf", 64), ("wo", 128), ("router", NE),
    ("w2", NT * P), ("w_mlp", 1), ("b_mlp", 1), ("ln1", 1), ("ln2", 1), ("g1", 1), ("b1", 1),
    ("g2", 1), ("b2", 1), ("g3", C), ("b3", C), ("t1", D1), ("t2", D2), ("t3", C)])
KCOL, KWIDTH = columns([
    ("ident", 128), ("cos", 128), ("sin", 128), ("causal", 128), ("rank", NE), ("alpha", 1),
    ("scale", 1), ("bias", 1), ("m1", 8), ("m2", 8), ("m3", 4), ("eps", 1),
    ("ln_eps", 4), ("rms_eps", 4), ("mean", 4)])
HCOL, HWIDTH = columns([("ident", 128), ("sign_rows", 128), ("ones", 128), ("bg", BG)])


def first_expert(t):
    return min(P * t // HID, NE - 2)


def tower(nc, coords, valid, wts, w13, kf, kh, out):
    with ExitStack() as ctx:
        def sb(name, shape, dt=F32):
            return ctx.enter_context(nc.sbuf_tensor(name, shape, dt))

        def ps(name, shape, dt=F32):
            return ctx.enter_context(nc.psum_tensor(name, shape, dt))

        def sem(name):
            return ctx.enter_context(nc.semaphore(name))

        h0_dram = nc.dram_tensor("h0_scratch", (PAIRS, T, 2 * C), F32).ap()

        W = sb("W", [P, WWIDTH])
        K = sb("K", [P, KWIDTH])
        H = sb("H", [P, HWIDTH], F16)

        def w(name):
            return W[:, WCOL[name][0]:WCOL[name][1]]

        def k(name):
            return K[:, KCOL[name][0]:KCOL[name][1]]

        def hc(name):
            return H[:, HCOL[name][0]:HCOL[name][1]]

        w1h, w1l = sb("w1h", [P, NT, P], F16), sb("w1l", [P, NT, P], F16)
        w3h, w3l = sb("w3h", [P, NT, P], F16), sb("w3l", [P, NT, P], F16)
        wrh, wrl = sb("wrh", [P, NE], F16), sb("wrl", [P, NE], F16)
        half = sb("half", [P, 4])
        ind = [sb(f"ind{s}", [P, T, T], F16) for s in range(2)]
        dif = [sb(f"dif{s}", [P, CH, T]) for s in range(2)]
        hin = [sb(f"hin{s}", [P, 2, C]) for s in range(2)]
        h1 = sb("h1", [P, 4, C])
        stat = sb("stat", [P, 2, 6])
        mv = sb("mv", [P, 2, 2])
        ve = sb("ve", [P, 2])
        rstd = sb("rstd", [P, 2])
        xn = sb("xn", [P, 2, C])
        xT = sb("xT", [P, T])
        qk = [sb(f"qk{s}", [P, 2, T]) for s in range(2)]
        wh = sb("wh", [P, 2 * T], F16)
        wl = sb("wl", [P, 2 * T], F16)
        bd = [sb(f"bd{s}", [P, 2, T, 2, BG], F16) for s in range(2)]
        va = [sb(f"va{s}", [P, 2, G2, VW]) for s in range(2)]
        t2s = sb("t2s", [P, BG, T])
        t1s = sb("t1s", [P, BG, T])
        raw = sb("raw", [P, BG, T])
        att = sb("att", [P, BG, T])
        attT = sb("attT", [P, BG, T])
        mx = sb("mx", [P, BG])
        mb = sb("mb", [P, BG])
        nm = sb("nm", [P, BG])
        rden = sb("rden", [P, BG])
        add = sb("add", [P, 2, C])
        fstat = sb("fstat", [P, 4, 6])
        fmv = sb("fmv", [P, 4, 2])
        fv = sb("fv", [P, 4])
        fr = sb("fr", [P, 4])
        ft = sb("ft", [P, 4])
        fu = sb("fu", [P, 4])
        fq = sb("fq", [P, 4])
        fm = sb("fm", [P, 4])
        pause = sb("pause", [P, 1])
        frr = sb("frr", [P, 4])
        fx = sb("fx", [P, 4, C])
        fxr = sb("fxr", [P, 4, C])
        res = sb("res", [P, 4, C])
        fxT = sb("fxT", [P, 2, T])
        vf = sb("vf", [P, 4, NKV, KW])
        r1, r2 = sb("r1", [P, 4, T]), sb("r2", [P, 4, T])
        qe = sb("qe", [P, 4, T])
        ke = sb("ke", [P, 4, NH, T])
        sc = [sb(f"sc{s}", [P, NH, T]) for s in range(2)]
        fmx = [sb(f"fmx{s}", [P, NH]) for s in range(2)]
        fnm = [sb(f"fnm{s}", [P, NH]) for s in range(2)]
        fp = [sb(f"fp{s}", [P, NH, T]) for s in range(2)]
        fpT = [sb(f"fpT{s}", [P, NH, T]) for s in range(2)]
        frd = [sb(f"frd{s}", [P, NH]) for s in range(2)]
        y = sb("y", [P, 4, C])
        yT = sb("yT", [P, 2, T])
        x2 = sb("x2", [P, 4, C])
        ms = sb("ms", [P, 4])
        xf = sb("xf", [P, 4, C])
        xs = sb("xs", [P, 4, 2, C], F16)
        xsT = sb("xsT", [P, 4 * T], F16)
        lg = {n: sb("lg_" + n, [P, 4, NE]) for n in ("a", "e", "p", "eq", "c", "s1", "p2", "s2", "tp", "wt")}
        l1 = {n: sb("l1_" + n, [P, 4]) for n in ("mx", "z", "rz", "m1", "c1", "m2", "c2", "st", "de", "rd")}
        sg = [sb(f"sg{s}", [P, 512]) for s in range(2)]
        hh = sb("hh", [P, NT, 512])
        oe = [sb(f"oe{s}", [P, NE, C]) for s in range(2)]
        osum = [sb(f"osum{s}", [P, C]) for s in range(2)]
        fo = sb("fo", [P, 4, C])

        pT2 = ps("pT2", [P, 1024])
        pT1 = ps("pT1", [P, 1024])
        pA = ps("pA", [P, 512])
        pS = ps("pS", [P, 512])
        pF = [ps(f"pF{s}", [P, 512]) for s in range(2)]

        craw = ind[0][:, 0:16, :].rearrange("p a b -> p (a b)").bitcast(I32)
        vraw = ind[0][:, 16:20, :].rearrange("p a b -> p (a b)").bitcast(U8)
        cf = ind[0][:, 20:36, :].rearrange("p a b -> p (a b)").bitcast(F32)
        cT = ind[0][:, 36:52, :].rearrange("p a b -> p (a b)").bitcast(F32)
        h1T = ind[0][:, 52:68, :].rearrange("p a b -> p (a b)").bitcast(F32)
        w1bd = ind[0][:, 68:70, :].rearrange("p a b -> p (a b)").bitcast(F32)
        w2bd = ind[0][:, 70:74, :].rearrange("p a b -> p (a b)").bitcast(F32)
        w3bd = ind[0][:, 74:78, :].rearrange("p a b -> p (a b)").bitcast(F32)
        h2T = ind[1][:, 0:32, :].rearrange("p a b -> p (a b)").bitcast(F32)
        sq = [ind[1][:, 32 + 8 * i:40 + 8 * i, :].rearrange("p a b -> p (a b)").bitcast(F32) for i in range(2)]
        zn = [ind[1][:, 48 + 8 * i:56 + 8 * i, :].rearrange("p a b -> p (a b)").bitcast(F32) for i in range(2)]
        h3g = [ind[1][:, 64 + 8 * i:72 + 8 * i, :].rearrange("p a b -> p (a b)").bitcast(F32) for i in range(2)]
        h3o = [ind[1][:, 80 + 8 * i:88 + 8 * i, :].rearrange("p a b -> p (a b)").bitcast(F32) for i in range(2)]
        w13raw = hh[:, 0:6, :].rearrange("p a b -> p (a b)")
        pms = [sb(f"pms{i}", [P, 32]) for i in range(2)]
        psd = [sb(f"psd{i}", [P, 32]) for i in range(2)]
        prs = [sb(f"prs{i}", [P, 32]) for i in range(2)]
        wm = sb("wm", [P, 3])
        wn = sb("wn", [P, 3])
        wc = sb("wc", [P, D1 + D2 + C])

        names = """ld_w ld_w13 ld_k ld_c dve_pro pool_pro w_split wbd_ready c_ready
            w_ln z_mm z_sq z_ms z_sd z_rs z_zn z_tr z_hT z_gb z_st0 z_st1
            ld_a0 ld_a1 ld_r0 ld_r1 a_mv a_rstd a_xn a_tr a_xT a_mm a_qk a_v a_w a_wl a_bd
            i_dve i_dif i_sgn t2_mm t1_mm t2_s t1_s s_tp s_raw s_rl s_m s_p s_pt s_ptT s_pv s_h1
            dve_front dve_soft dve_value pool_a act_s
            dve_rope dve_heads dve_top dve_moe pool_f f_mv f_r f_x f_xo f_tr f_xT f_v f_va f_q f_qrope f_qe f_k f_krope f_ke
            f_sc f_scm f_nm f_p f_pt f_ptT f_pv f_y f_yt f_yT f_wo f_x2 f_ms f_rq f_xs f_xst f_xsT
            f_lg f_la f_le f_wt f_h13 f_sg f_hh f_e f_oe f_out st_out""".split()
        S = {n: sem(n) for n in names}
        block = ctx.enter_context(nc.Block())

        class Chain:

            def __init__(self, eng, name, idx, per):
                self.eng, self.sem, self.idx, self.per, self.n = eng, S[name], idx, per, 0

            def step(self, ins):
                self.n += 1
                return ins.then_inc(self.sem, 1)

            def wait(self):
                self.eng.wait_ge(self.sem, self.idx * self.per + self.n)

            def link(self, ins):
                self.step(ins)
                self.wait()

            def end(self):
                assert self.n == self.per, (self.sem, self.n)

        def nth(eng, name, idx, per, n):
            eng.wait_ge(S[name], idx * per + n)

        def before(eng, name, idx, per, back=1):
            if isinstance(idx, int) and idx < back:
                return
            eng.wait_ge(S[name], idx * per + per - back * per)

        def difs(s, c):
            return dif[(s * (NP) + c) % 2]

        def sequence(emit_step, emit_f, engine):
            emit_step("front", 0, 0, 0)
            emit_step("front", 1, 1, 0)
            emit_step("cmp0", 0, 0, 0)
            emit_step("cmp1", 0, 0, 0)

            def group(j, first, last):
                for s in range(2):
                    p = 2 * j + s
                    nxt = not (last and s == 1)
                    if nxt:
                        emit_step("cmp0", p + 1, 1 - s, j + s)
                    emit_step("sums", p, s, j)
                    if not first:
                        emit_f(("rope", "moe0")[s], j - 1)
                    emit_step("soft", p, s, j)
                    if nxt:
                        emit_step("cmp1", p + 1, 1 - s, j + s)
                    if not first:
                        emit_f(("heads", "moe1")[s], j - 1)
                    emit_step("value", p, s, j)
                    if not last:
                        emit_step("front", p + 2, s, j + 1)

            group(0, True, False)
            with engine.Fori(1, GROUPS - 1) as j:
                group(j, False, False)
            group(GROUPS - 1, False, True)
            for part in ("rope", "heads", "moe0", "moe1"):
                emit_f(part, GROUPS - 1)

        @block.sync
        def _(sp):
            sp.dma_start(craw[0:24, :], coords).then_inc(S["ld_c"], 16)
            sp.dma_start(vraw[0:24, :], valid).then_inc(S["ld_c"], 16)
            sp.dma_start(K[:], kf).then_inc(S["ld_k"], 16)
            sp.dma_start(W[:], wts).then_inc(S["ld_w"], 16)
            sp.dma_start(H[:], kh).then_inc(S["ld_k"], 16)
            sp.dma_start(w13raw[:, 0:2 * NT * P], w13).then_inc(S["ld_w13"], 16)
            for i in range(8):
                sp.wait_ge(S["z_gb"], i + 1)
                sp.dma_start(h0_dram.rearrange("(m i) t c -> i t m c", i=8)[i],
                             h3o[i % 2][:, 0:512].rearrange("p (m c) -> p m c", m=4)).then_inc(S[f"z_st{i % 2}"], 16)
            sp.wait_ge(S["z_st0"], 16 * 4)
            sp.wait_ge(S["z_st1"], 16 * 4)

            def load(p, s, g):
                before(sp, "a_xn", p, 1, 2)
                sp.dma_start(hin[s][:], h0_dram[p].rearrange("t (b c) -> t b c", b=2)).then_inc(S[f"ld_a{s}"], 16)
                before(sp, "f_xo", g, 1, 1)
                sp.dma_start(h1[:, 2 * s:2 * s + 2, :],
                             h0_dram[p].rearrange("t (b c) -> t b c", b=2)).then_inc(S[f"ld_r{s}"], 16)

            def store(g):
                nth(sp, "f_out", g, 4, 4)
                sp.dma_start(out[g].rearrange("b t c -> t b c"), fo[:]).then_inc(S["st_out"], 16)

            load(0, 0, 0)
            load(1, 1, 0)

            def residual(p, s, g):
                before(sp, "f_xo", g, 1, 1)
                sp.dma_start(h1[:, 2 * s:2 * s + 2, :],
                             h0_dram[p].rearrange("t (b c) -> t b c", b=2)).then_inc(S[f"ld_r{s}"], 16)

            def normed(p, s):
                before(sp, "a_xn", p, 1, 2)
                sp.dma_start(hin[s][:], h0_dram[p].rearrange("t (b c) -> t b c", b=2)).then_inc(S[f"ld_a{s}"], 16)

            normed(2, 0)
            normed(3, 1)
            with sp.Fori(1, GROUPS - 1) as j:
                residual(2 * j, 0, j)
                residual(2 * j + 1, 1, j)
                normed(2 * j + 2, 0)
                normed(2 * j + 3, 1)
                store(j - 1)
            residual(PAIRS - 2, 0, GROUPS - 1)
            residual(PAIRS - 1, 1, GROUPS - 1)
            store(GROUPS - 2)
            store(GROUPS - 1)
            sp.wait_ge(S["st_out"], 16 * GROUPS)

        @block.tensor
        def _(pe):
            zbank = [pT2[:, 0:512], pT2[:, 512:1024], pT1[:, 0:512], pT1[:, 512:1024]]
            tbank = [pA, pS]

            def mm(u):
                z = zbank[u % 4]
                if u >= 4:
                    pe.wait_ge(S["z_zn"], u - 3)
                if u < 2:
                    pe.wait_ge(S["c_ready"], 1)
                    pe.wait_ge(S["wbd_ready"], 1)
                    for c in range(4):
                        i = 4 * u + c
                        last = nc.tensor.matmul(z[:, 128 * c:128 * c + 128], cT[0:24, 128 * i:128 * i + 128],
                                                w1bd[0:24, :], start=True, stop=True)
                elif u < 6:
                    v = u - 2
                    pe.wait_ge(S["z_hT"], v // 2 + 1)
                    for c in range(2):
                        i = 2 * v + c
                        last = nc.tensor.matmul(z[:, 256 * c:256 * c + 256], h1T[:, 128 * i:128 * i + 128],
                                                w2bd[:, :], start=True, stop=True)
                else:
                    i = u - 6
                    pe.wait_ge(S["z_hT"], 2 + i // 2 + 1)
                    for hf in range(2):
                        last = nc.tensor.matmul(z[:, 256 * hf:256 * hf + 256],
                                                h2T[:, 1024 * hf + 128 * i:1024 * hf + 128 * i + 128],
                                                w3bd[:, :], start=True, stop=True)
                last.then_inc(S["z_mm"], 1)

            def tr(u):
                pe.wait_ge(S["z_zn"], u + 1)
                if u >= 2:
                    pe.wait_ge(S["z_hT"], u - 1)
                for c in range(4):
                    last = nc.tensor.transpose(tbank[u % 2][:, 128 * c:128 * c + 128],
                                               zn[u % 2][:, 128 * c:128 * c + 128], k("ident"))
                last.then_inc(S["z_tr"], 1)

            pe.wait_ge(S["ld_k"], 32)
            mm(0)
            mm(1)
            tr(0)
            mm(2)
            mm(3)
            tr(1)
            mm(4)
            mm(5)
            tr(2)
            mm(6)
            mm(7)
            tr(3)
            mm(8)
            mm(9)
            tr(4)
            tr(5)
            for u in range(10, 14):
                mm(u)
            pe.wait_ge(S["w_split"], 1)

            def step(part, p, s, g):
                if part == "front":
                    pe.wait_ge(S["a_xn"], p + 1)
                    before(pe, "a_qk", p, 1)
                    before(pe, "a_v", p, 1)
                    nc.tensor.transpose(pA[:, 384:512], xn[:].rearrange("p b c -> p (b c)"),
                                        k("ident")).then_inc(S["a_tr"], 1)
                    pe.wait_ge(S["a_xT"], p + 1)
                    nc.tensor.matmul(pA[:, 0:128], w("qk")[:, 0:128], xT[:], start=True, stop=True)
                    nc.tensor.matmul(pA[:, 128:256], w("qk")[:, 128:256], xT[:], start=True, stop=True)
                    nc.tensor.matmul(pA[:, 256:384], xT[:], w("v"), start=True, stop=True).then_inc(S["a_mm"], 1)
                elif part == "sums":
                    pe.wait_ge(S["i_dve"], p + 1)
                    nth(pe, "i_sgn", p, NP, NP)
                    pe.wait_ge(S["a_bd"], p + 1)
                    before(pe, "t2_s", p, 1)
                    for hf in range(2):
                        col = 512 * hf
                        tok = T // 2 * hf
                        nc.tensor.matmul(pT2[:, col:col + 512], hc("sign_rows"),
                                         bd[s][:, 1, tok:tok + T // 2, :, :].rearrange("p a b c -> p (a b c)"),
                                         start=True, stop=False)
                        for i in range(T // 2):
                            last = nc.tensor.matmul(
                                pT2[:, col + 8 * i:col + 8 * i + 8], ind[s][:, :, tok + i],
                                bd[s][:, 1, tok + i, :, :].rearrange("p b c -> p (b c)"),
                                start=False, stop=i == T // 2 - 1)
                    last.then_inc(S["t2_mm"], 1)
                    before(pe, "t1_s", p, 1)
                    for hf in range(2):
                        col = 512 * hf
                        tok = T // 2 * hf
                        signs = tok >= N_DVE
                        if signs:
                            nc.tensor.matmul(pT1[:, col:col + 512], hc("ones"),
                                             bd[s][:, 0, tok:tok + T // 2, :, :].rearrange("p a b c -> p (a b c)"),
                                             start=True, stop=False)
                        for i in range(T // 2):
                            last = nc.tensor.matmul(
                                pT1[:, col + 8 * i:col + 8 * i + 8], ind[s][:, tok + i, :],
                                bd[s][:, 0, tok + i, :, :].rearrange("p b c -> p (b c)"),
                                start=not signs, stop=not signs or i == T // 2 - 1)
                    last.then_inc(S["t1_mm"], 1)
                elif part == "soft":
                    pe.wait_ge(S["t1_s"], p + 1)
                    before(pe, "s_h1", p, 1)
                    for b in range(BG):
                        last = nc.tensor.transpose(pS[:, 128 * b:128 * b + 128], t1s[:, b, :], k("ident"))
                    last.then_inc(S["s_tp"], 1)
                elif part == "value":
                    pe.wait_ge(S["s_p"], p + 1)
                    pe.wait_ge(S["s_raw"], p + 1)
                    for b in range(BG):
                        last = nc.tensor.transpose(pS[:, 128 * b:128 * b + 128], att[:, b, :], k("ident"))
                    last.then_inc(S["s_pt"], 1)
                    pe.wait_ge(S["s_ptT"], p + 1)
                    for b in range(BG):
                        last = nc.tensor.matmul(pS[:, VW * b:VW * b + VW], attT[:, b, :],
                                                va[s][:, b // G2, b % G2, :], start=True, stop=True)
                    last.then_inc(S["s_pv"], 1)

            def ffn(part, g):
                if part == "rope":
                    pe.wait_ge(S["f_x"], g + 1)
                    before(pe, "f_out", g, 4)
                    for i in range(2):
                        last = nc.tensor.transpose(pF[1][:, 128 * i:128 * i + 128],
                                                   fxr[:, 2 * i:2 * i + 2, :].rearrange("p b c -> p (b c)"),
                                                   k("ident"))
                    last.then_inc(S["f_tr"], 1)
                    pe.wait_ge(S["f_xT"], g + 1)
                    for i in range(2):
                        last = nc.tensor.matmul(pF[1][:, 256 + 64 * i:320 + 64 * i], fxT[:, i, :], w("vf"),
                                                start=True, stop=True)
                    last.then_inc(S["f_v"], 1)
                    ropew = w("rope").rearrange("p (m b o) -> p m b o", m=4, b=2)

                    def project(m, bank):
                        dst = bank[:].rearrange("p (i b t) -> p b i t", i=2, b=2)
                        for b in range(2):
                            last = nc.tensor.matmul(dst[:, b, :, :], ropew[:, m, b, :], fxT[:, :, :],
                                                    start=True, stop=True)
                        return last

                    project(0, pF[0])
                    pe.wait_ge(S["f_va"], g + 1)
                    project(1, pF[1]).then_inc(S["f_q"], 1)
                    pe.wait_ge(S["f_qrope"], g + 1)
                    project(2, pF[0])
                    project(3, pF[1]).then_inc(S["f_k"], 1)
                    pe.wait_ge(S["f_krope"], g + 1)
                elif part == "heads":
                    pe.wait_ge(S["f_qe"], g + 1)
                    pe.wait_ge(S["f_ke"], g + 1)

                    def scores(b):
                        if b >= 2:
                            nth(pe, "f_y", g, 4, b - 1)
                        nc.tensor.matmul(pF[b % 2][:], qe[:, b, :], ke[:, b, :, :].rearrange("p h t -> p (h t)"),
                                         start=True, stop=True).then_inc(S["f_sc"], 1)

                    def turn(b):
                        nth(pe, "f_p", g, 4, b + 1)
                        for h in range(NH):
                            last = nc.tensor.transpose(pF[b % 2][:, 128 * h:128 * h + 128], fp[b % 2][:, h, :],
                                                       k("ident"))
                        last.then_inc(S["f_pt"], 1)

                    def values(b):
                        nth(pe, "f_ptT", g, 4, b + 1)
                        for h in range(NH):
                            last = nc.tensor.matmul(pF[b % 2][:, KW * h:KW * h + KW], fpT[b % 2][:, h, :],
                                                    vf[:, b, h * NKV // NH, :], start=True, stop=True)
                        last.then_inc(S["f_pv"], 1)

                    for b in range(0, 4, 2):
                        scores(b)
                        scores(b + 1)
                        turn(b)
                        turn(b + 1)
                        values(b)
                        values(b + 1)
                    nth(pe, "f_y", g, 4, 4)
                    for i in range(2):
                        last = nc.tensor.transpose(pF[0][:, 128 * i:128 * i + 128],
                                                   y[:, 2 * i:2 * i + 2, :].rearrange("p b c -> p (b c)"), k("ident"))
                    last.then_inc(S["f_yt"], 1)
                    pe.wait_ge(S["f_yT"], g + 1)
                    for i in range(2):
                        last = nc.tensor.matmul(pF[0][:, 256 + 128 * i:384 + 128 * i], yT[:, i, :], w("wo"),
                                                start=True, stop=True)
                    last.then_inc(S["f_wo"], 1)
                    pe.wait_ge(S["f_xs"], g + 1)
                    for b in range(4):
                        last = nc.tensor.transpose(pF[1][:].bitcast(F16)[:, 128 * b:128 * b + 128],
                                                   xs[:, b, :, :].rearrange("p a c -> p (a c)"), hc("ident"))
                    last.then_inc(S["f_xst"], 1)
                    pe.wait_ge(S["f_xsT"], g + 1)
                    for b in range(4):
                        dst = pF[0][:, NE * b:NE * b + NE]
                        nc.tensor.matmul(dst, xsT[:, 128 * b:128 * b + 128], wrh[:], start=True, stop=False)
                        last = nc.tensor.matmul(dst, xsT[:, 128 * b:128 * b + 128], wrl[:], start=False, stop=True)
                    last.then_inc(S["f_lg"], 1)
                    pe.wait_ge(S["f_la"], g + 1)
                else:
                    lo, hi = (0, NT // 2) if part == "moe0" else (NT // 2, NT)
                    for t in range(lo, hi):
                        if t > 0:
                            nth(pe, "f_sg", g, NT, t)
                        nc.tensor.matmul(pF[0][:], w1h[:, t, :], xsT[:], start=True, stop=False)
                        nc.tensor.matmul(pF[0][:], w1l[:, t, :], xsT[:], start=False, stop=True)
                        if t > 0:
                            nth(pe, "f_hh", g, NT, t)
                        nc.tensor.matmul(pF[1][:], w3h[:, t, :], xsT[:], start=True, stop=False)
                        nc.tensor.matmul(pF[1][:], w3l[:, t, :], xsT[:], start=False,
                                         stop=True).then_inc(S["f_h13"], 1)
                    if part == "moe1":
                        nth(pe, "f_hh", g, NT, NT)
                        for b in range(4):
                            if b >= 2:
                                nth(pe, "f_oe", g, 4, b - 1)
                            for t in range(NT):
                                e0 = first_expert(t)
                                last = nc.tensor.matmul(pF[b % 2][:, C * e0:C * e0 + 2 * C],
                                                        hh[:, t, 128 * b:128 * b + 128],
                                                        w("w2")[:, P * t:P * t + P], start=t == 0, stop=t == NT - 1,
                                                        skip_group_check=True)
                            last.then_inc(S["f_e"], 1)

            sequence(step, ffn, pe)

        @block.scalar
        def _(act):
            zbank = [pT2[:, 0:512], pT2[:, 512:1024], pT1[:, 0:512], pT1[:, 512:1024]]
            tbank = [pA, pS]

            def square(u):
                act.wait_ge(S["z_mm"], u + 1)
                if u >= 2:
                    act.wait_ge(S["z_ms"], u - 1)
                nc.scalar.activation(sq[u % 2][:, 0:512], zbank[u % 4], ACT.Square).then_inc(S["z_sq"], 1)

            def root(u):
                width = D1 if u < 2 else D2 if u < 6 else C
                act.wait_ge(S["z_ms"], u + 1)
                if u >= 2:
                    act.wait_ge(S["z_zn"], u - 1)
                nc.scalar.activation(psd[u % 2][:, 0:512 // width], pms[u % 2][:, 0:512 // width], ACT.Sqrt,
                                     bias=k("eps"), scale=1.0 / width).then_inc(S["z_sd"], 1)

            def evac(u):
                act.wait_ge(S["z_tr"], u + 1)
                if u < 2:
                    nc.scalar.activation(h1T[:, 512 * u:512 * u + 512], tbank[u % 2][:], ACT.Relu,
                                         bias=w("b1"), scale=w("g1")).then_inc(S["z_hT"], 1)
                else:
                    v = u - 2
                    dst = h2T[:, :].rearrange("p (h i t) -> p i h t", h=2, t=T)[:, 2 * v:2 * v + 2, :, :]
                    nc.scalar.activation(dst, tbank[u % 2][:].rearrange("p (i h t) -> p i h t", i=2, h=2), ACT.Relu,
                                         bias=w("b2"), scale=w("g2")).then_inc(S["z_hT"], 1)

            act.wait_ge(S["ld_w"], 16)
            act.wait_ge(S["ld_k"], 32)
            square(0)
            square(1)
            root(0)
            root(1)
            evac(0)
            square(2)
            square(3)
            evac(1)
            root(2)
            root(3)
            square(4)
            square(5)
            evac(2)
            root(4)
            root(5)
            square(6)
            square(7)
            evac(3)
            root(6)
            root(7)
            square(8)
            square(9)
            evac(4)
            root(8)
            root(9)
            square(10)
            square(11)
            evac(5)
            root(10)
            root(11)
            square(12)
            square(13)
            root(12)
            root(13)
            act.wait_ge(S["pool_pro"], 1)
            act.wait_ge(S["z_st0"], 16 * 4)
            act.wait_ge(S["z_st1"], 16 * 4)
            act.wait_ge(S["z_mm"], 14)

            def step(part, p, s, g):
                if part == "front":
                    act.wait_ge(S["a_tr"], p + 1)
                    nc.scalar.activation(xT[:], pA[:, 384:512], ACT.Copy).then_inc(S["a_xT"], 1)
                    act.wait_ge(S["a_mm"], p + 1)
                    before(act, "i_dve", p, 1, 2)
                    before(act, "i_sgn", p, NP, 2)
                    nc.scalar.activation(qk[s][:].rearrange("p a t -> p (a t)"), pA[:, 0:256],
                                         ACT.Copy).then_inc(S["a_qk"], 1)
                    before(act, "s_pv", p, 1, 2)
                    nc.scalar.activation(va[s][:, :, :, 0:DG], pA[:, 256:384].rearrange(
                        "p (b d g) -> p b g d", b=2, g=G2), ACT.Copy).then_inc(S["a_v"], 1)
                elif part == "cmp0":
                    before(act, "t1_mm", p, 1, 2)
                    before(act, "t2_mm", p, 1, 2)
                    act.wait_ge(S["a_qk"], p + 1)
                    for i in range(N_ACT):
                        q = N_DVE + N_POOL + i
                        nc.scalar.activation(ind[s][:, q, :], qk[s][:, 1, :], ACT.Sign, bias=qk[s][:, 0, q:q + 1],
                                             scale=-1.0)
                    for c in range(NP - 1):
                        sign(p, s, c)
                elif part == "cmp1":
                    sign(p, s, NP - 1)
                elif part == "soft":
                    act.wait_ge(S["s_raw"], p + 1)
                    nc.scalar.activation(att[:].rearrange("p b t -> p (b t)"), raw[:].rearrange("p b t -> p (b t)"),
                                         ACT.Relu, bias=w("b_mlp"), scale=k("alpha")).then_inc(S["act_s"], 1)
                    act.wait_ge(S["act_s"], p + 1)
                    act.wait_ge(S["s_m"], p + 1)
                    for b in range(BG):
                        last = nc.scalar.activation(att[:, b, :], att[:, b, :], ACT.Exp, bias=nm[:, b:b + 1])
                    last.then_inc(S["s_p"], 1)
                elif part == "value":
                    act.wait_ge(S["s_pt"], p + 1)
                    nc.scalar.activation(attT[:].rearrange("p b t -> p (b t)"), pS[:], ACT.Copy).then_inc(S["s_ptT"], 1)

            def sign(p, s, c):
                nth(act, "i_dif", p, NP, c + 1)
                n = N_DVE + CH * c
                nc.scalar.activation(ind[s][:, n:n + CH, :], difs(s, c)[:], ACT.Sign).then_inc(S["i_sgn"], 1)

            def ffn(part, g):
                if part == "rope":
                    act.wait_ge(S["f_tr"], g + 1)
                    nc.scalar.activation(fxT[:].rearrange("p i t -> p (i t)"), pF[1][:, 0:256],
                                         ACT.Copy).then_inc(S["f_xT"], 1)
                    act.wait_ge(S["f_v"], g + 1)
                    nc.scalar.activation(vf[:, :, :, 0:HD], pF[1][:, 256:384].rearrange(
                        "p (b v d) -> p b v d", b=4, v=NKV), ACT.Copy).then_inc(S["f_va"], 1)
                elif part == "heads":
                    def exps(b):
                        nth(act, "f_nm", g, 4, b + 1)
                        for h in range(NH):
                            last = nc.scalar.activation(fp[b % 2][:, h, :], sc[b % 2][:, h, :], ACT.Exp,
                                                        bias=fnm[b % 2][:, h:h + 1], scale=HD ** -0.5)
                        last.then_inc(S["f_p"], 1)

                    def turned(b):
                        nth(act, "f_pt", g, 4, b + 1)
                        nc.scalar.activation(fpT[b % 2][:].rearrange("p h t -> p (h t)"), pF[b % 2][:],
                                             ACT.Copy).then_inc(S["f_ptT"], 1)

                    for b in range(0, 4, 2):
                        exps(b)
                        exps(b + 1)
                        turned(b)
                        turned(b + 1)
                    act.wait_ge(S["f_yt"], g + 1)
                    nc.scalar.activation(yT[:].rearrange("p i t -> p (i t)"), pF[0][:, 0:256],
                                         ACT.Copy).then_inc(S["f_yT"], 1)
                    act.wait_ge(S["f_x2"], g + 1)
                    for b in range(4):
                        last = nc.scalar.activation(sg[0][:, 64 * b:64 * b + 64], x2[:, b, :], ACT.Square,
                                                    accum_out=ms[:, b:b + 1])
                    last.then_inc(S["f_ms"], 1)
                    act.wait_ge(S["f_xst"], g + 1)
                    nc.scalar.activation(xsT[:], pF[1][:].bitcast(F16)[:, 0:512], ACT.Copy).then_inc(S["f_xsT"], 1)
                    act.wait_ge(S["f_la"], g + 1)
                    nc.scalar.activation(lg["e"][:].rearrange("p b e -> p (b e)"),
                                         lg["a"][:].rearrange("p b e -> p (b e)"), ACT.Exp).then_inc(S["f_le"], 1)
                else:
                    lo, hi = (0, NT // 2) if part == "moe0" else (NT // 2, NT)
                    for t in range(lo, hi):
                        nth(act, "f_h13", g, NT, t + 1)
                        if t >= 2:
                            nth(act, "f_hh", g, NT, t - 1)
                        elif t == 0:
                            nth(act, "f_ms", g, 1, 1)
                        nc.scalar.activation(sg[t % 2][:], pF[0][:], ACT.Silu).then_inc(S["f_sg"], 1)

            sequence(step, ffn, act)

        @block.gpsimd
        def _(pool):
            nc.gpsimd.memset(half[:], -0.5)
            for s in range(2):
                nc.gpsimd.memset(va[s][:], 1.0)
            nc.gpsimd.memset(vf[:], 1.0).then_inc(S["pool_pro"], 1)
            pool.wait_ge(S["ld_w"], 16)
            for i in range(8):
                pool.wait_ge(S["z_zn"], 6 + i + 1)
                if i >= 2:
                    pool.wait_ge(S[f"z_st{i % 2}"], 16 * (i // 2))
                z, g, o = zn[i % 2][:, 0:512], h3g[i % 2][:, 0:512], h3o[i % 2][:, 0:512]
                g3 = w("g3").unsqueeze(1).to_broadcast([P, 8, C])
                b3 = w("b3").unsqueeze(1).to_broadcast([P, 8, C])
                nc.gpsimd.tensor_tensor(g.rearrange("p (a c) -> p a c", c=C), z.rearrange("p (a c) -> p a c", c=C), g3,
                                        ALU.mult).then_inc(S["pool_pro"], 1)
                pool.wait_ge(S["pool_pro"], i + 2)
                nc.gpsimd.tensor_tensor(o.rearrange("p (a c) -> p a c", c=C), g.rearrange("p (a c) -> p a c", c=C), b3,
                                        ALU.add).then_inc(S["z_gb"], 1)

            def diff(p, s, c):
                n = s * (NP) + c
                if not (isinstance(p, int) and p * (NP) + c < 2):
                    pool.wait_ge(S["i_sgn"], p * (NP) + c - 1)
                q = N_DVE + CH * c
                nc.gpsimd.tensor_tensor(dif[n % 2][:], qk[s][:, 0, q:q + CH].unsqueeze(2).to_broadcast([P, CH, T]),
                                        qk[s][:, 1, :].unsqueeze(1).to_broadcast([P, CH, T]),
                                        ALU.subtract).then_inc(S["i_dif"], 1)

            def step(part, p, s, g):
                if part == "front":
                    ch = Chain(pool, "pool_a", p, 1)
                    pool.wait_ge(S["a_mv"], p + 1)
                    ch.link(nc.gpsimd.tensor_tensor(ve[:], mv[:, :, 1], k("ln_eps")[:, 0:2], ALU.add))
                    ch.end()
                    nc.gpsimd.tensor_tensor(rstd[:], ve[:], half[:, 0:2], ALU.pow).then_inc(S["a_rstd"], 1)
                    pool.wait_ge(S["a_w"], p + 1)
                    before(pool, "t1_mm", p, 1, 2)
                    before(pool, "t2_mm", p, 1, 2)
                    for part2, src in ((0, wh), (1, wl)):
                        if part2 == 1:
                            pool.wait_ge(S["a_wl"], p + 1)
                        last = nc.gpsimd.tensor_tensor(
                            bd[s][:].rearrange("p a t r b -> p (a t) r b")[:, :, part2, :],
                            src[:].unsqueeze(2).to_broadcast([P, 2 * T, BG]),
                            hc("bg").unsqueeze(1).to_broadcast([P, 2 * T, BG]), ALU.mult)
                    last.then_inc(S["a_bd"], 1)
                elif part == "cmp0":
                    pool.wait_ge(S["a_qk"], p + 1)
                    for c in range(NP - 1):
                        diff(p, s, c)
                elif part == "cmp1":
                    diff(p, s, NP - 1)

            def ffn(part, g):
                if part == "rope":
                    ch = Chain(pool, "pool_f", g, 5)
                    pool.wait_ge(S["f_mv"], g + 1)
                    var = fmv[:, :, 1]
                    ch.link(nc.gpsimd.tensor_tensor(fv[:], var, k("ln_eps"), ALU.add))
                    ch.link(nc.gpsimd.tensor_tensor(fr[:], fv[:], half[:], ALU.pow))
                    ch.link(nc.gpsimd.tensor_tensor(ft[:], fr[:], fr[:], ALU.mult))
                    ch.link(nc.gpsimd.tensor_tensor(ft[:], ft[:], var, ALU.mult))
                    ch.link(nc.gpsimd.tensor_tensor(ft[:], ft[:], k("rms_eps"), ALU.add))
                    ch.end()
                    nc.gpsimd.tensor_tensor(fu[:], ft[:], half[:], ALU.pow).then_inc(S["f_r"], 1)
                    pool.wait_ge(S["f_x"], g + 1)
                    before(pool, "f_out", g, 4)
                    nc.gpsimd.tensor_tensor(res[:], h1[:], fx[:], ALU.add).then_inc(S["f_xo"], 1)
                    pool.wait_ge(S["f_qrope"], g + 1)
                    nc.gpsimd.tensor_tensor(qe[:], r1[:], r2[:], ALU.add).then_inc(S["f_qe"], 1)
                elif part == "heads":
                    pool.wait_ge(S["f_ms"], g + 1)
                    nc.gpsimd.tensor_tensor(fm[:], ms[:], k("mean"), ALU.mult).then_inc(S["f_rq"], 1)
                    nth(pool, "f_rq", g, 3, 1)
                    nc.gpsimd.tensor_tensor(fv[:], fm[:], k("rms_eps"), ALU.add).then_inc(S["f_rq"], 1)
                    nth(pool, "f_rq", g, 3, 2)
                    nc.gpsimd.tensor_tensor(fq[:], fv[:], half[:], ALU.pow).then_inc(S["f_rq"], 1)

            sequence(step, ffn, pool)

        @block.vector
        def _(dve):
            ch = Chain(dve, "dve_pro", 0, 10)
            nc.vector.memset(ke[:], 0.0)
            dve.wait_ge(S["ld_c"], 32)
            dve.wait_ge(S["ld_k"], 32)
            ch.link(nc.vector.tensor_scalar(cf[0:24, :], craw[0:24, :], k("scale")[0:24, :], -1.0, ALU.mult, ALU.add))
            nc.vector.tensor_tensor(cT[0:24, :], cf[0:24, :], vraw[0:24, :], ALU.mult).then_inc(S["c_ready"], 1)
            dve.wait_ge(S["ld_w"], 16)
            srcs = [(w("t1"), 0, D1), (w("t2"), D1, D2), (w("t3"), D1 + D2, C)]
            for i, (src, at, n) in enumerate(srcs):
                ch.step(nc.vector.tensor_reduce(wm[:, i:i + 1], src, AX, ALU.add))
            ch.wait()
            for i, (src, at, n) in enumerate(srcs):
                ch.step(nc.vector.tensor_scalar(wn[:, i:i + 1], wm[:, i:i + 1], -1.0 / n, None, ALU.mult))
            ch.wait()
            for i, (src, at, n) in enumerate(srcs):
                ch.step(nc.vector.tensor_scalar(wc[:, at:at + n], src, wn[:, i:i + 1], None, ALU.add))
            ch.wait()
            ch.end()
            for dst, mask, nb, at, n in ((w1bd, "m1", 8, 0, D1), (w2bd, "m2", 8, D1, D2), (w3bd, "m3", 4, D1 + D2, C)):
                last = nc.vector.tensor_tensor(dst[:, 0:nb * n].rearrange("p (b n) -> p b n", b=nb),
                                               wc[:, at:at + n].unsqueeze(1).to_broadcast([P, nb, n]),
                                               k(mask).unsqueeze(2).to_broadcast([P, nb, n]), ALU.mult)
            last.then_inc(S["wbd_ready"], 1)
            nc.vector.tensor_scalar(w("rope"), w("rope"), w("ln1"), None, ALU.mult)
            nc.vector.tensor_scalar(w("vf"), w("vf"), w("ln1"), None, ALU.mult)

            def mean_square(u):
                width = D1 if u < 2 else D2 if u < 6 else C
                dve.wait_ge(S["z_sq"], u + 1)
                if u >= 2:
                    dve.wait_ge(S["z_sd"], u - 1)
                nc.vector.tensor_reduce(pms[u % 2][:, 0:512 // width],
                                        sq[u % 2][:, 0:512].rearrange("p (a c) -> p a c", c=width),
                                        AX, ALU.add).then_inc(S["z_ms"], 1)

            def normalise(u):
                width = D1 if u < 2 else D2 if u < 6 else C
                n = 512 // width
                z = [pT2[:, 0:512], pT2[:, 512:1024], pT1[:, 0:512], pT1[:, 512:1024]][u % 4]
                dve.wait_ge(S["z_sd"], u + 1)
                nc.vector.reciprocal(prs[u % 2][:, 0:n], psd[u % 2][:, 0:n]).then_inc(S["z_rs"], 1)
                dve.wait_ge(S["z_rs"], u + 1)
                if 2 <= u < 8:
                    dve.wait_ge(S["z_tr"], u - 1)
                elif u >= 8:
                    dve.wait_ge(S["z_gb"], u - 7)
                nc.vector.tensor_tensor(zn[u % 2][:, 0:512].rearrange("p (a c) -> p a c", c=width),
                                        z.rearrange("p (a c) -> p a c", c=width),
                                        prs[u % 2][:, 0:n].unsqueeze(2).to_broadcast([P, n, width]),
                                        ALU.mult).then_inc(S["z_zn"], 1)

            for u in range(0, 14, 2):
                mean_square(u)
                mean_square(u + 1)
                normalise(u)
                normalise(u + 1)
            dve.wait_ge(S["ld_w13"], 16)
            n13 = NT * P
            flat = lambda x: x[:].rearrange("p t n -> p (t n)")
            raw13 = w13raw[:, 0:2 * n13]
            nc.vector.tensor_scalar(raw13, raw13, w("ln2"), None, ALU.mult)
            nc.vector.tensor_scalar(w("router"), w("router"), w("ln2"), None, ALU.mult).then_inc(S["w_ln"], 1)
            dve.wait_ge(S["w_ln"], 1)
            nc.vector.tensor_copy(flat(w1h), raw13[:, 0:n13])
            nc.vector.tensor_copy(flat(w3h), raw13[:, n13:2 * n13])
            nc.vector.tensor_copy(wrh[:], w("router")).then_inc(S["w_ln"], 1)
            dve.wait_ge(S["w_ln"], 2)
            nc.vector.tensor_tensor(flat(w1l), raw13[:, 0:n13], flat(w1h), ALU.subtract)
            nc.vector.tensor_tensor(flat(w3l), raw13[:, n13:2 * n13], flat(w3h), ALU.subtract)
            nc.vector.tensor_tensor(wrl[:], w("router"), wrh[:], ALU.subtract).then_inc(S["w_split"], 1)
            dve.wait_ge(S["w_split"], 1)
            dve.wait_ge(S["z_st0"], 16 * 4)
            dve.wait_ge(S["z_st1"], 16 * 4)
            dve.wait_ge(S["z_mm"], 14)

            def compare(p, s, c):
                ins = nc.vector.tensor_tensor(ind[s][:, CH * c:CH * c + CH, :],
                                              qk[s][:, 1, :].unsqueeze(1).to_broadcast([P, CH, T]),
                                              qk[s][:, 0, CH * c:CH * c + CH].unsqueeze(2).to_broadcast([P, CH, T]),
                                              ALU.is_lt)
                return ins

            NC = N_DVE // CH

            def step(part, p, s, g):
                if part == "front":
                    ch = Chain(dve, "dve_front", p, 1)
                    nth(dve, f"ld_a{s}", g, 16, 16)
                    for b in range(2):
                        last = nc.vector.bn_stats(stat[:, b, :], hin[s][:, b, :])
                    ch.link(last)
                    ch.end()
                    nc.vector.memset(pause[:], 0.0)
                    for b in range(2):
                        last = nc.vector.bn_aggr(mv[:, b, :], stat[:, b, :])
                    last.then_inc(S["a_mv"], 1)
                    dve.wait_ge(S["a_rstd"], p + 1)
                    dve.wait_ge(S["a_mv"], p + 1)
                    before(dve, "a_tr", p, 1)
                    for b in range(2):
                        last = nc.vector.tensor_scalar(xn[:, b, :], hin[s][:, b, :], mv[:, b, 0:1], rstd[:, b:b + 1],
                                                       ALU.subtract, ALU.mult)
                    last.then_inc(S["a_xn"], 1)
                    dve.wait_ge(S["a_qk"], p + 1)
                    before(dve, "a_bd", p, 1)
                    flat2 = qk[s][:].rearrange("p a t -> p (a t)")
                    nc.vector.tensor_scalar(wh[:], flat2, w("w_mlp"), None, ALU.mult).then_inc(S["a_w"], 1)
                    dve.wait_ge(S["a_w"], p + 1)
                    nc.vector.scalar_tensor_tensor(wl[:], flat2, w("w_mlp"), wh[:], ALU.mult,
                                                   ALU.subtract).then_inc(S["a_wl"], 1)
                elif part == "cmp0":
                    before(dve, "t1_mm", p, 1, 2)
                    before(dve, "t2_mm", p, 1, 2)
                    dve.wait_ge(S["a_qk"], p + 1)
                    for c in range(NC // 2):
                        compare(p, s, c)
                elif part == "sums":
                    dve.wait_ge(S["t2_mm"], p + 1)
                    nc.vector.tensor_reduce(t2s[:], pT2[:].rearrange("p (k r b) -> p b k r", r=2, b=BG), AX, ALU.add,
                                            negate=True).then_inc(S["t2_s"], 1)
                    dve.wait_ge(S["t1_mm"], p + 1)
                    before(dve, "s_tp", p, 1)
                    nc.vector.tensor_reduce(t1s[:], pT1[:].rearrange("p (k r b) -> p b k r", r=2, b=BG), AX,
                                            ALU.add).then_inc(S["t1_s"], 1)
                elif part == "soft":
                    dve.wait_ge(S["s_tp"], p + 1)
                    dve.wait_ge(S["t2_s"], p + 1)
                    before(dve, "act_s", p, 1)
                    nc.vector.tensor_tensor(raw[:].rearrange("p b t -> p (b t)"), pS[:],
                                            t2s[:].rearrange("p b t -> p (b t)"), ALU.add).then_inc(S["s_raw"], 1)
                    dve.wait_ge(S["s_raw"], p + 1)
                    ch = Chain(dve, "dve_soft", p, 2)
                    ch.link(nc.vector.tensor_reduce(mx[:], raw[:], AX, ALU.max))
                    ch.link(nc.vector.tensor_scalar(mb[:], mx[:], k("alpha"), w("b_mlp"), ALU.mult, ALU.add))
                    ch.end()
                    before(dve, "s_p", p, 1)
                    nc.vector.tensor_scalar(nm[:], mb[:], 0.0, -1.0, ALU.max, ALU.mult).then_inc(S["s_m"], 1)
                elif part == "cmp1":
                    for c in range(NC // 2, NC):
                        last = compare(p, s, c)
                    last.then_inc(S["i_dve"], 1)
                elif part == "value":
                    dve.wait_ge(S["s_pv"], p + 1)
                    pv = pS[:, 0:BG * VW].rearrange("p (b v) -> p b v", v=VW)
                    ch = Chain(dve, "dve_value", p, 2)
                    ch.link(nc.vector.reciprocal(rden[:], pv[:, :, DG]))
                    ch.link(nc.vector.tensor_tensor(add[:].rearrange("p b (d g) -> p b g d", g=G2),
                                                    pv[:, :, 0:DG].rearrange("p (b g) d -> p b g d", g=G2),
                                                    rden[:].rearrange("p (b g) -> p b g", g=G2).unsqueeze(3)
                                                    .to_broadcast([P, 2, G2, DG]), ALU.mult))
                    ch.end()
                    nth(dve, f"ld_r{s}", g, 16, 16)
                    nc.vector.tensor_tensor(h1[:, 2 * s:2 * s + 2, :], h1[:, 2 * s:2 * s + 2, :], add[:],
                                            ALU.add).then_inc(S["s_h1"], 1)

            def ffn(part, g):
                if part == "rope":
                    dve.wait_ge(S["s_h1"], g * 2 + 2)
                    ch = Chain(dve, "dve_rope", g, 2)
                    for b in range(4):
                        last = nc.vector.bn_stats(fstat[:, b, :], h1[:, b, :])
                    ch.link(last)
                    nc.vector.memset(pause[:], 0.0)
                    for b in range(4):
                        last = nc.vector.bn_aggr(fmv[:, b, :], fstat[:, b, :])
                    last.then_inc(S["f_mv"], 1)
                    dve.wait_ge(S["f_mv"], g + 1)
                    dve.wait_ge(S["f_r"], g + 1)
                    ch.link(nc.vector.tensor_tensor(frr[:], fr[:], fu[:], ALU.mult))
                    for dst, r in ((fxr, frr), (fx, fr)):
                        for b in range(4):
                            last = nc.vector.tensor_scalar(dst[:, b, :], h1[:, b, :], fmv[:, b, 0:1], r[:, b:b + 1],
                                                           ALU.subtract, ALU.mult)
                    last.then_inc(S["f_x"], 1)

                    def rotate():
                        cos = k("cos").unsqueeze(1).to_broadcast([P, 4, T])
                        sin = k("sin").unsqueeze(1).to_broadcast([P, 4, T])
                        nc.vector.tensor_tensor(r1[:], pF[0][:].rearrange("p (b t) -> p b t", b=4), cos, ALU.mult)
                        return nc.vector.tensor_tensor(r2[:], pF[1][:].rearrange("p (b t) -> p b t", b=4), sin,
                                                       ALU.mult)

                    dve.wait_ge(S["f_q"], g + 1)
                    rotate().then_inc(S["f_qrope"], 1)
                    dve.wait_ge(S["f_k"], g + 1)
                    dve.wait_ge(S["f_qe"], g + 1)
                    rotate().then_inc(S["f_krope"], 1)
                    dve.wait_ge(S["f_krope"], g + 1)
                    for h in range(NH):
                        rows = slice(HP * h, HP * h + HP)
                        last = nc.vector.tensor_tensor(ke[rows, :, h, :], r1[rows], r2[rows], ALU.add)
                    last.then_inc(S["f_ke"], 1)
                    ch.end()
                elif part == "heads":
                    ch = Chain(dve, "dve_heads", g, 11)

                    def masked(b):
                        nth(dve, "f_sc", g, 4, b + 1)
                        if b >= 2:
                            nth(dve, "f_p", g, 4, b - 1)
                        nc.vector.tensor_tensor(sc[b % 2][:], pF[b % 2][:].rearrange("p (h t) -> p h t", h=NH),
                                                k("causal").unsqueeze(1).to_broadcast([P, NH, T]),
                                                ALU.add).then_inc(S["f_scm"], 1)
                        nth(dve, "f_scm", g, 4, b + 1)
                        ch.link(nc.vector.tensor_reduce(fmx[b % 2][:], sc[b % 2][:], AX, ALU.max))
                        nc.vector.tensor_scalar(fnm[b % 2][:], fmx[b % 2][:], -HD ** -0.5, None,
                                                ALU.mult).then_inc(S["f_nm"], 1)

                    def weigh(b):
                        nth(dve, "f_pv", g, 4, b + 1)
                        pv = pF[b % 2][:, 0:NH * KW].rearrange("p (h v) -> p h v", v=KW)
                        ch.link(nc.vector.reciprocal(frd[b % 2][:], pv[:, :, HD]))
                        nc.vector.tensor_tensor(y[:, b, :].rearrange("p (h d) -> p h d", h=NH), pv[:, :, 0:HD],
                                                frd[b % 2][:].unsqueeze(2).to_broadcast([P, NH, HD]),
                                                ALU.mult).then_inc(S["f_y"], 1)

                    for b in range(0, 4, 2):
                        masked(b)
                        masked(b + 1)
                        weigh(b)
                        weigh(b + 1)
                    dve.wait_ge(S["f_wo"], g + 1)
                    wo = pF[0][:, 256:512].rearrange("p (b c) -> p b c", b=4)
                    nc.vector.tensor_tensor(x2[:], fx[:], wo, ALU.add).then_inc(S["f_x2"], 1)
                    dve.wait_ge(S["f_xo"], g + 1)
                    ch.step(nc.vector.tensor_tensor(res[:], res[:], wo, ALU.add))
                    nth(dve, "f_rq", g, 3, 3)
                    dve.wait_ge(S["f_x2"], g + 1)
                    ch.link(nc.vector.tensor_tensor(xf[:], x2[:], fq[:].unsqueeze(2).to_broadcast([P, 4, C]),
                                                    ALU.mult))
                    before(dve, "f_xst", g, 1)
                    ch.link(nc.vector.tensor_copy(xs[:, :, 0, :], xf[:]))
                    nc.vector.tensor_tensor(xs[:, :, 1, :], xf[:], xs[:, :, 0, :], ALU.subtract).then_inc(S["f_xs"], 1)
                    dve.wait_ge(S["f_lg"], g + 1)
                    logits = pF[0][:, 0:4 * NE].rearrange("p (b e) -> p b e", b=4)
                    ch.end()
                    ct = Chain(dve, "dve_top", g, 21)
                    ct.link(nc.vector.tensor_reduce(l1["mx"][:], logits, AX, ALU.max))
                    nc.vector.tensor_tensor(lg["a"][:], logits, l1["mx"][:].unsqueeze(2).to_broadcast([P, 4, NE]),
                                            ALU.subtract).then_inc(S["f_la"], 1)
                else:
                    lo, hi = (0, NT // 2) if part == "moe0" else (NT // 2, NT)
                    if part == "moe0":
                        top2(g)
                    for t in range(lo, hi):
                        nth(dve, "f_sg", g, NT, t + 1)
                        nc.vector.tensor_tensor(hh[:, t, :], sg[t % 2][:], pF[1][:], ALU.mult).then_inc(S["f_hh"], 1)
                    if part == "moe1":
                        ch = Chain(dve, "dve_moe", g, 4)
                        for b in range(4):
                            nth(dve, "f_e", g, 4, b + 1)
                            nc.vector.tensor_tensor(oe[b % 2][:], pF[b % 2][:].rearrange("p (e c) -> p e c", e=NE),
                                                    lg["wt"][:, b, :].unsqueeze(2).to_broadcast([P, NE, C]),
                                                    ALU.mult).then_inc(S["f_oe"], 1)
                            nth(dve, "f_oe", g, 4, b + 1)
                            ch.link(nc.vector.tensor_reduce(osum[b % 2][:], oe[b % 2][:].rearrange("p e c -> p c e"),
                                                            AX, ALU.add))
                            if b == 0 and not (isinstance(g, int) and g == 0):
                                dve.wait_ge(S["st_out"], g * 16)
                            nc.vector.tensor_tensor(fo[:, b, :], res[:, b, :], osum[b % 2][:],
                                                    ALU.add).then_inc(S["f_out"], 1)
                        ch.end()

            def top2(g):
                ch = Chain(dve, "dve_top", g, 21)
                ch.n = 1
                v = nc.vector
                dve.wait_ge(S["f_le"], g + 1)
                ch.link(v.tensor_reduce(l1["z"][:], lg["e"][:], AX, ALU.add))

                def wide(x):
                    return x[:].unsqueeze(2).to_broadcast([P, 4, NE])

                rank = k("rank").unsqueeze(1).to_broadcast([P, 4, NE])
                ch.link(v.reciprocal(l1["rz"][:], l1["z"][:]))
                ch.link(v.tensor_tensor(lg["p"][:], lg["e"][:], wide(l1["rz"]), ALU.mult))

                def largest(probs, m, c, sel):
                    ch.link(v.tensor_reduce(l1[m][:], lg[probs][:], AX, ALU.max))
                    ch.link(v.tensor_tensor(lg["eq"][:], lg[probs][:], wide(l1[m]), ALU.is_equal))
                    ch.link(v.tensor_tensor(lg["c"][:], lg["eq"][:], rank, ALU.mult))
                    ch.link(v.tensor_reduce(l1[c][:], lg["c"][:], AX, ALU.max))
                    ch.link(v.tensor_tensor(lg[sel][:], lg["c"][:], wide(l1[c]), ALU.is_equal))

                largest("p", "m1", "c1", "s1")
                ch.link(v.scalar_tensor_tensor(lg["p2"][:], lg["s1"][:], -2.0, lg["p"][:], ALU.mult, ALU.add))
                largest("p2", "m2", "c2", "s2")
                ch.step(v.tensor_tensor(lg["eq"][:], lg["s1"][:], lg["s2"][:], ALU.add))
                ch.link(v.tensor_tensor(l1["st"][:], l1["m1"][:], l1["m2"][:], ALU.add))
                ch.step(v.tensor_tensor(lg["tp"][:], lg["p"][:], lg["eq"][:], ALU.mult))
                ch.link(v.tensor_scalar(l1["de"][:], l1["st"][:], 1.0, TOP_EPS, ALU.mult, ALU.add))
                ch.link(v.reciprocal(l1["rd"][:], l1["de"][:]))
                ch.link(v.tensor_tensor(lg["wt"][:], lg["tp"][:], wide(l1["rd"]), ALU.mult))
                ch.end()

            sequence(step, ffn, dve)


def _block_rows(a, n):
    r, c = a.shape
    out = np.zeros((n * r, n * c), a.dtype)
    for i in range(n):
        out[i * r:(i + 1) * r, i * c:(i + 1) * c] = a
    return out


def _pack(cols, width, parts, dtype):
    out = np.zeros((P, width), dtype)
    for name, a in parts.items():
        lo, hi = cols[name]
        out[:a.shape[0], lo:hi] = a.reshape(a.shape[0], -1)
    return out


def _tokens(a):
    return a.reshape(4, 8, 2, T).transpose(0, 2, 1, 3).reshape(8, 1, 8 * T)


def _rope_rows(wm, perm):
    heads = wm.shape[0] // HD
    rows = np.zeros((NH, HP, C), wm.dtype)
    for h in range(NH):
        rows[h, :HD] = wm.reshape(heads, HD, C)[h * heads // NH][perm]
    return rows.reshape(P, C).T


def _weights(x):
    f = lambda n: np.asarray(x[n])
    col = lambda a, n: np.tile(a, n)[:, None]
    same, swap = np.arange(HD), (np.arange(HD) + HD // 2) % HD
    rope = np.zeros((2, C, 4, 2, P), np.float32)
    for m, (name, perm) in enumerate((("L0_ffn_wq", same), ("L0_ffn_wq", swap), ("L0_ffn_wk", same),
                                      ("L0_ffn_wk", swap))):
        for b in range(2):
            rope[b, :, m, b] = _rope_rows(f(name), perm)
    w2 = np.zeros((P, NT, 2, C), np.float32)
    for e in range(NE):
        for i in range(HID):
            n = e * HID + i
            w2[n % P, n // P, e - first_expert(n // P)] = f("L0_ffn_w2")[e, :, i]
    parts = {
        "qk": np.concatenate([_block_rows(f("L0_attn_Wq").T, 2), _block_rows(f("L0_attn_Wk").T, 2)], 1),
        "v": _block_rows(f("L0_attn_Wv").T, 2),
        "rope": rope.reshape(P, -1), "vf": _block_rows(f("L0_ffn_wv").T, 2), "wo": _block_rows(f("L0_ffn_wo").T, 2),
        "router": np.tile(f("L0_ffn_router_w").T, (2, 1)), "w2": w2,
        "w_mlp": col(f("L0_attn_w_mlp"), 4), "b_mlp": col(f("L0_attn_b_mlp"), P),
        "ln1": col(f("L0_ffn_ln1_w"), 2), "ln2": col(f("L0_ffn_ln2_w"), 2),
        "g1": col(f("L0_tok_g1"), 8), "b1": col(f("L0_tok_b1"), 8), "g2": col(f("L0_tok_g2"), 4),
        "b2": col(f("L0_tok_b2"), 4), "g3": np.tile(f("L0_tok_g3"), (P, 1)), "b3": np.tile(f("L0_tok_b3"), (P, 1)),
        "t1": np.tile(f("L0_tok_W1"), (8, 1)), "t2": np.tile(f("L0_tok_W2"), (8, 1)),
        "t3": np.tile(f("L0_tok_W3"), (4, 1)),
    }
    w13 = np.zeros((2, C, 2, NT * P), np.float32)
    w13[:, :, 0, :NE * HID] = f("L0_ffn_w1").reshape(NE * HID, C).T
    w13[:, :, 1, :NE * HID] = f("L0_ffn_w3").reshape(NE * HID, C).T
    return _pack(WCOL, WWIDTH, parts, np.float32), w13.reshape(P, -1)


def _constants():
    inv_freq = 1.0 / 10000.0 ** (np.arange(0, HD, 2, dtype=np.float32) / HD)
    freqs = np.outer(np.arange(T, dtype=np.float32), inv_freq)
    emb = np.concatenate([freqs, freqs], axis=-1)
    cos, sin = np.zeros((NH, HP, T), np.float32), np.zeros((NH, HP, T), np.float32)
    cos[:, :HD] = np.cos(emb).T
    sin[:, :HD] = np.sin(emb).T * np.where(np.arange(HD) < HD // 2, -1.0, 1.0)[:, None]
    q, key = np.arange(P)[:, None], np.arange(T)[None, :]
    sizes = np.array([160, 120, 2], np.float32)
    parts = {
        "ident": np.eye(P), "cos": cos.reshape(P, T), "sin": sin.reshape(P, T),
        "causal": np.where(key <= q, 0.0, BIG), "rank": np.tile(np.arange(NE, 0, -1), (P, 1)),
        "alpha": np.where(q < N_DVE, 1.0, 0.5), "scale": np.tile((2.0 / (sizes - 1))[:, None], (8, 1)),
        "bias": np.full((P, 1), -1.0), "m1": np.arange(P)[:, None] // 3 == np.arange(8),
        "m2": q // D1 == np.arange(8), "m3": q // D2 == np.arange(4), "eps": np.full((P, 1), LN_EPS),
        "ln_eps": np.full((P, 4), LN_EPS), "rms_eps": np.full((P, 4), RMS_EPS), "mean": np.full((P, 4), 1.0 / C),
    }
    half = {"ident": np.eye(P), "sign_rows": np.ones((P, 1)) * (key >= N_DVE), "ones": np.ones((P, P)),
            "bg": q // DG == np.arange(BG)}
    return _pack(KCOL, KWIDTH, parts, np.float32), _pack(HCOL, HWIDTH, half, np.float16)


def kernel(**inputs):
    import concourse.bacc as bacc
    from concourse.bass_utils import run_bass_kernel_spmd

    tok = [np.asarray(inputs[n]) for n in ("x", "itok_BS_0_479", "mask_BS_i1_0")]
    valid = np.asarray(inputs["mask_BS_b1_0"]).view(np.uint8)
    wts, w13 = _weights(inputs)
    kf, kh = _constants()
    arrays = {
        "coords": np.concatenate([_tokens(a) for a in tok], 1).reshape(24, 8 * T),
        "valid": np.concatenate([_tokens(valid)] * 3, 1).reshape(24, 8 * T),
        "wts": wts, "w13": w13, "kf": kf, "kh": kh,
    }
    nc = bacc.Bacc("TRN2", target_bir_lowering=False, num_devices=1)
    args = [nc.dram_tensor(n, a.shape, mybir.dt.from_np(a.dtype), kind="ExternalInput").ap()
            for n, a in arrays.items()]
    args.append(nc.dram_tensor("out", (GROUPS, 4, T, C), F32, kind="ExternalOutput").ap())
    tower(nc, *args)
    r = run_bass_kernel_spmd(nc, [arrays], core_ids=[0])
    return r.results[0]["out"].reshape(B, T, C)
```

```python
from contextlib import ExitStack

import numpy as np

import concourse.bass as bass
from concourse import mybir

ALU = mybir.AluOpType
ACT = mybir.ActivationFunctionType
AX = mybir.AxisListType.X
F32 = mybir.dt.float32
F16 = mybir.dt.float16
I32 = mybir.dt.int32
U8 = mybir.dt.uint8

P = 128
B, T, C = 64, 128, 64
PAIRS, GROUPS = B // 2, B // 4
G2, DG = 2, 32
BG = 4
D1, D2 = 16, 32
NH, NKV, HD = 4, 2, 16
HP = 32
NE, HID = 8, 170
NT = -(-NE * HID // P)
BIG = -1e30
LN_EPS, RMS_EPS, TOP_EPS = 1e-5, 1e-6, 1e-9

CH = 8
CV = 8
N_DVE = 64
N_POOL = 48
N_ACT = T - N_DVE - N_POOL
NP = N_POOL // CH
ND = 3

VW = DG + 1
KW = HD + 1


ORDER = [
    """dif.0 sum2.0 cmp.0 dif.1 red2.0 sum2.1 cmp.1 cmp.2 f_tr f_q f_k sum1.0 red2.1 dif.2 f_rotq ptr.0 cmp.3 f_rotk
       ptr.1 ptr.2 sum1.1 red1.0 red1.1 sgn.0 sgn.1 f_ke dif.3 sgn.2 soft_t dif.4 f_sc.0 soft_m front_stat f_sc.1
       f_sc.2 f_mask.0 soft_e sgn.3 f_mask.1 f_mask.2 f_sc.3 f_exp.0 f_exp.1 f_mask.3 f_turn.0 f_exp.2 f_turn.1
       f_val.0 f_exp.3 front_norm cmp.4 f_turn.2 f_val.1 f_turn.3 f_weigh.0 dif.5 soft_pt cmp.5 f_val.2 ptr.3 cmp.6
       f_val.3 f_weigh.1 f_weigh.2 sgn.4 f_weigh.3 soft_pv cmp.7 f_yt sgn.5 pair_add front_mm f_wo f_rms front_split""".split(),
    """ptr.0 sum2.0 ptr.1 dif.0 cmp.0 red2.0 f_x2 sum2.1 f_xs cmp.1 front_stat ptr.2 dif.1 f_route cmp.2 f_top.0
       f_h.0 f_h.1 sum1.0 red2.1 sgn.0 f_h.2 red1.0 f_h.3 f_h.4 cmp.3 f_h.5 f_h.6 sum1.1 f_top.1 f_h.7 dif.2 f_h.8
       red1.1 cmp.4 f_h.9 f_h.10 ptr.3 soft_t sgn.1 soft_m dif.3 dif.4 f_e.0 f_e.1 soft_e soft_pt sgn.2 cmp.5 soft_pv
       cmp.6 f_o.0 sgn.3 f_e.2 cmp.7 pair_add sgn.4 front_norm dif.5 f_stat+ f_o.1 sgn.5 f_o.2 front_mm front_split
       f_e.3 f_norm+ f_o.3""".split(),
]


def columns(parts):
    at, out = 0, {}
    for name, width in parts:
        out[name] = (at, at + width)
        at += width
    return out, at


WCOL, WWIDTH = columns([
    ("qk", 256), ("v", 128), ("rope", 1024), ("vf", 64), ("wo", 128), ("router", NE),
    ("w2", NT * P), ("w_mlp", 1), ("b_mlp", 1), ("ln1", 1), ("ln2", 1), ("g1", 1), ("b1", 1),
    ("g2", 1), ("b2", 1), ("g3", C), ("b3", C), ("t1", D1), ("t2", D2), ("t3", C)])
KCOL, KWIDTH = columns([
    ("ident", 128), ("cos", 128), ("sin", 128), ("causal", 128), ("rank", NE), ("alpha", 1),
    ("scale", 1), ("bias", 1), ("m1", 8), ("m2", 8), ("m3", 4), ("eps", 1),
    ("ln_eps", 4), ("rms_eps", 4), ("mean", 4)])
HCOL, HWIDTH = columns([("ident", 128), ("sign_rows", 128), ("ones", 128), ("bg", BG)])


def first_expert(t):
    return min(P * t // HID, NE - 2)


def tower(nc, coords, valid, wts, w13, kf, kh, out):
    with ExitStack() as ctx:
        def sb(name, shape, dt=F32):
            return ctx.enter_context(nc.sbuf_tensor(name, shape, dt))

        def ps(name, shape, dt=F32):
            return ctx.enter_context(nc.psum_tensor(name, shape, dt))

        def sem(name):
            return ctx.enter_context(nc.semaphore(name))

        h0_dram = nc.dram_tensor("h0_scratch", (PAIRS, T, 2 * C), F32).ap()

        W = sb("W", [P, WWIDTH])
        K = sb("K", [P, KWIDTH])
        H = sb("H", [P, HWIDTH], F16)

        def w(name):
            return W[:, WCOL[name][0]:WCOL[name][1]]

        def k(name):
            return K[:, KCOL[name][0]:KCOL[name][1]]

        def hc(name):
            return H[:, HCOL[name][0]:HCOL[name][1]]

        w1h, w1l = sb("w1h", [P, NT, P], F16), sb("w1l", [P, NT, P], F16)
        w3h, w3l = sb("w3h", [P, NT, P], F16), sb("w3l", [P, NT, P], F16)
        wrh, wrl = sb("wrh", [P, NE], F16), sb("wrl", [P, NE], F16)
        half = sb("half", [P, 4])
        ind = [sb(f"ind{s}", [P, T, T], F16) for s in range(2)]
        dif = [sb(f"dif{s}", [P, CH, T]) for s in range(ND)]
        hin = [sb(f"hin{s}", [P, 2, C]) for s in range(2)]
        h1 = sb("h1", [P, 4, C])
        stat = sb("stat", [P, 2, 6])
        mv = sb("mv", [P, 2, 2])
        ve = sb("ve", [P, 2])
        rstd = sb("rstd", [P, 2])
        xn = sb("xn", [P, 2, C])
        xT = sb("xT", [P, T])
        qk = [sb(f"qk{s}", [P, 2, T]) for s in range(2)]
        wh = sb("wh", [P, 2 * T], F16)
        wl = sb("wl", [P, 2 * T], F16)
        bd = [sb(f"bd{s}", [P, 2, T, 2, BG], F16) for s in range(2)]
        va = [sb(f"va{s}", [P, 2, G2, VW]) for s in range(2)]
        t2s = sb("t2s", [P, BG, T])
        t1s = sb("t1s", [P, BG, T])
        raw = sb("raw", [P, BG, T])
        att = sb("att", [P, BG, T])
        attT = sb("attT", [P, BG, T])
        mx = sb("mx", [P, BG])
        mb = sb("mb", [P, BG])
        nm = sb("nm", [P, BG])
        rden = sb("rden", [P, BG])
        add = sb("add", [P, 2, C])
        fstat = sb("fstat", [P, 4, 6])
        fmv = sb("fmv", [P, 4, 2])
        fv = sb("fv", [P, 4])
        fr = sb("fr", [P, 4])
        ft = sb("ft", [P, 4])
        fu = sb("fu", [P, 4])
        fq = sb("fq", [P, 4])
        fm = sb("fm", [P, 4])
        pause = sb("pause", [P, 1])
        frr = sb("frr", [P, 4])
        fx = sb("fx", [P, 4, C])
        fxr = sb("fxr", [P, 4, C])
        res = sb("res", [P, 4, C])
        fxT = sb("fxT", [P, 2, T])
        vf = sb("vf", [P, 4, NKV, KW])
        r1, r2 = sb("r1", [P, 4, T]), sb("r2", [P, 4, T])
        r3, r4 = sb("r3", [P, 4, T]), sb("r4", [P, 4, T])
        qe = sb("qe", [P, 4, T])
        ke = sb("ke", [P, 4, NH, T])
        sc = [sb(f"sc{s}", [P, NH, T]) for s in range(4)]
        fmx = [sb(f"fmx{s}", [P, NH]) for s in range(4)]
        fnm = [sb(f"fnm{s}", [P, NH]) for s in range(4)]
        fp = sc
        fpT = [r1, r2, r3, r4]
        frd = [sb(f"frd{s}", [P, NH]) for s in range(4)]
        y = sb("y", [P, 4, C])
        yT = sb("yT", [P, 2, T])
        x2 = sb("x2", [P, 4, C])
        ms = sb("ms", [P, 4])
        xf = sb("xf", [P, 4, C])
        xs = sb("xs", [P, 4, 2, C], F16)
        xsT = sb("xsT", [P, 4 * T], F16)
        lg = {n: sb("lg_" + n, [P, 4, NE]) for n in ("a", "e", "p", "eq", "c", "s1", "p2", "s2", "tp", "wt")}
        l1 = {n: sb("l1_" + n, [P, 4]) for n in ("mx", "z", "rz", "m1", "c1", "m2", "c2", "st", "de", "rd")}
        sg = [sb(f"sg{s}", [P, 512]) for s in range(2)]
        hh = sb("hh", [P, NT, 512])
        oe = [sb(f"oe{s}", [P, NE, C]) for s in range(2)]
        osum = [sb(f"osum{s}", [P, C]) for s in range(2)]
        fo = sb("fo", [P, 4, C])

        pT = ps("pT", [P, 1024])
        pA = ps("pA", [P, 512])
        pS = ps("pS", [P, 512])
        pF = [ps(f"pF{s}", [P, 512]) for s in range(4)]

        craw = ind[0][:, 0:16, :].rearrange("p a b -> p (a b)").bitcast(I32)
        vraw = ind[0][:, 16:20, :].rearrange("p a b -> p (a b)").bitcast(U8)
        cf = ind[0][:, 20:36, :].rearrange("p a b -> p (a b)").bitcast(F32)
        cT = ind[0][:, 36:52, :].rearrange("p a b -> p (a b)").bitcast(F32)
        h1T = ind[0][:, 52:68, :].rearrange("p a b -> p (a b)").bitcast(F32)
        w1bd = ind[0][:, 68:70, :].rearrange("p a b -> p (a b)").bitcast(F32)
        w2bd = ind[0][:, 70:74, :].rearrange("p a b -> p (a b)").bitcast(F32)
        w3bd = ind[0][:, 74:78, :].rearrange("p a b -> p (a b)").bitcast(F32)
        h2T = ind[1][:, 0:32, :].rearrange("p a b -> p (a b)").bitcast(F32)
        sq = [ind[1][:, 32 + 8 * i:40 + 8 * i, :].rearrange("p a b -> p (a b)").bitcast(F32) for i in range(2)]
        zn = [ind[1][:, 48 + 8 * i:56 + 8 * i, :].rearrange("p a b -> p (a b)").bitcast(F32) for i in range(2)]
        h3g = [ind[1][:, 64 + 8 * i:72 + 8 * i, :].rearrange("p a b -> p (a b)").bitcast(F32) for i in range(2)]
        h3o = [ind[1][:, 80 + 8 * i:88 + 8 * i, :].rearrange("p a b -> p (a b)").bitcast(F32) for i in range(2)]
        w13raw = hh[:, 0:6, :].rearrange("p a b -> p (a b)")
        pms = [sb(f"pms{i}", [P, 32]) for i in range(2)]
        psd = [sb(f"psd{i}", [P, 32]) for i in range(2)]
        prs = [sb(f"prs{i}", [P, 32]) for i in range(2)]
        wm = sb("wm", [P, 3])
        wn = sb("wn", [P, 3])
        wc = sb("wc", [P, D1 + D2 + C])

        names = """ld_w ld_w13 ld_k ld_c dve_pro pool_pro w_split wbd_ready c_ready
            w_ln z_mm z_sq z_ms z_sd z_rs z_zn z_tr z_hT z_gb z_st0 z_st1
            ld_a0 ld_a1 ld_r0 ld_r1 a_mv a_rstd a_xn a_tr a_xT a_mm a_qk a_v a_w a_wl a_bd
            i_dve i_ptr i_dif i_sgn t2_mm t1_mm t2_s t1_s s_tp s_raw s_rl s_m s_p s_pt s_ptT s_pv s_h1
            dve_front dve_soft dve_value pool_a act_s
            dve_rope dve_top f_rr f_res f_xf f_rd f_os pool_f f_mv f_r f_x f_xo f_tr f_xT f_v f_va f_q f_qrope f_qe f_k f_krope f_ke f_kep
            f_sc f_scm f_nm f_p f_pt f_ptT f_pv f_y f_yt f_yT f_wo f_x2 f_ms f_rq f_xs f_xst f_xsT
            f_lg f_la f_le f_wt f_h13 f_sg f_hh f_e f_oe f_out st_out""".split()
        S = {n: sem(n) for n in names}
        block = ctx.enter_context(nc.Block())

        class Chain:

            def __init__(self, eng, name, idx, per):
                self.eng, self.sem, self.idx, self.per, self.n = eng, S[name], idx, per, 0

            def step(self, ins):
                self.n += 1
                return ins.then_inc(self.sem, 1)

            def wait(self):
                self.eng.wait_ge(self.sem, self.idx * self.per + self.n)

            def link(self, ins):
                self.step(ins)
                self.wait()

            def end(self):
                assert self.n == self.per, (self.sem, self.n)

        def nth(eng, name, idx, per, n):
            eng.wait_ge(S[name], idx * per + n)

        def before(eng, name, idx, per, back=1):
            if isinstance(idx, int) and idx < back:
                return
            eng.wait_ge(S[name], idx * per + per - back * per)

        def difs(s, c):
            return dif[c % ND]

        def sequence(do, engine):
            def compare(p, s, g, what):
                for kind, n in what:
                    do(kind, p, s, g, n)

            def piece(item):
                kind, *n = item.rstrip("+").split(".")
                return kind, int(n[0]) if n else 0, item.endswith("+")

            def every():
                return ([("cmp", n) for n in range(N_DVE // CV)] + [("ptr", n) for n in range(N_ACT // 4)]
                        + [(kind, n) for n in range(NP) for kind in ("dif", "sgn")])

            for s in range(2):
                for part in ("front_stat", "front_norm", "front_mm", "front_split"):
                    do(part, s, s, 0, 0)
            compare(0, 0, 0, every())

            def group(j, first, last):
                for s in range(2):
                    p = 2 * j + s
                    for item in ORDER[s]:
                        kind, n, own = piece(item)
                        if kind in ("cmp", "ptr", "dif", "sgn"):
                            if not (last and s == 1):
                                do(kind, p + 1, 1 - s, j + s, n)
                        elif kind.startswith("front"):
                            if not last:
                                do(kind, p + 2, s, j + 1, n)
                        elif own:
                            do(kind, None, None, j, n)
                        elif kind.startswith("f_"):
                            if not first:
                                do(kind, None, None, j - 1, n)
                        else:
                            do(kind, p, s, j, n)

            group(0, True, False)
            group(1, False, False)
            with engine.Fori(2, GROUPS - 1) as j:
                group(j, False, False)
            group(GROUPS - 1, False, True)
            for s in range(2):
                for item in ORDER[s]:
                    kind, n, own = piece(item)
                    if kind.startswith("f_") and not own:
                        do(kind, None, None, GROUPS - 1, n)

        @block.sync
        def _(sp):
            sp.dma_start(craw[0:24, :], coords).then_inc(S["ld_c"], 16)
            sp.dma_start(vraw[0:24, :], valid).then_inc(S["ld_c"], 16)
            sp.dma_start(K[:], kf).then_inc(S["ld_k"], 16)
            sp.dma_start(W[:], wts).then_inc(S["ld_w"], 16)
            sp.dma_start(H[:], kh).then_inc(S["ld_k"], 16)
            sp.dma_start(w13raw[:, 0:2 * NT * P], w13).then_inc(S["ld_w13"], 16)
            for i in range(8):
                sp.wait_ge(S["z_gb"], i + 1)
                sp.dma_start(h0_dram.rearrange("(m i) t c -> i t m c", i=8)[i],
                             h3o[i % 2][:, 0:512].rearrange("p (m c) -> p m c", m=4)).then_inc(S[f"z_st{i % 2}"], 16)
            sp.wait_ge(S["z_st0"], 16 * 4)
            sp.wait_ge(S["z_st1"], 16 * 4)

            def load(p, s, g):
                before(sp, "a_xn", p, 1, 2)
                sp.dma_start(hin[s][:], h0_dram[p].rearrange("t (b c) -> t b c", b=2)).then_inc(S[f"ld_a{s}"], 16)
                before(sp, "f_xo", g, 1, 1)
                sp.dma_start(h1[:, 2 * s:2 * s + 2, :],
                             h0_dram[p].rearrange("t (b c) -> t b c", b=2)).then_inc(S[f"ld_r{s}"], 16)

            def store(g):
                nth(sp, "f_out", g, 4, 4)
                sp.dma_start(out[g].rearrange("b t c -> t b c"), fo[:]).then_inc(S["st_out"], 16)

            load(0, 0, 0)
            load(1, 1, 0)

            def residual(p, s, g):
                before(sp, "f_xo", g, 1, 1)
                sp.dma_start(h1[:, 2 * s:2 * s + 2, :],
                             h0_dram[p].rearrange("t (b c) -> t b c", b=2)).then_inc(S[f"ld_r{s}"], 16)

            def normed(p, s):
                before(sp, "a_xn", p, 1, 2)
                sp.dma_start(hin[s][:], h0_dram[p].rearrange("t (b c) -> t b c", b=2)).then_inc(S[f"ld_a{s}"], 16)

            normed(2, 0)
            normed(3, 1)

            def group(j):
                residual(2 * j, 0, j)
                residual(2 * j + 1, 1, j)
                normed(2 * j + 2, 0)
                normed(2 * j + 3, 1)
                store(j - 1)

            group(1)
            with sp.Fori(2, GROUPS - 1) as j:
                group(j)
            residual(PAIRS - 2, 0, GROUPS - 1)
            residual(PAIRS - 1, 1, GROUPS - 1)
            store(GROUPS - 2)
            store(GROUPS - 1)
            sp.wait_ge(S["st_out"], 16 * GROUPS)

        @block.tensor
        def _(pe):
            zbank = [pT[:, 0:512], pT[:, 512:1024], pF[0][:], pF[1][:]]
            tbank = [pA, pS]

            def mm(u):
                z = zbank[u % 4]
                if u >= 4:
                    pe.wait_ge(S["z_zn"], u - 3)
                if u < 2:
                    pe.wait_ge(S["c_ready"], 1)
                    pe.wait_ge(S["wbd_ready"], 1)
                    for c in range(4):
                        i = 4 * u + c
                        last = nc.tensor.matmul(z[:, 128 * c:128 * c + 128], cT[0:24, 128 * i:128 * i + 128],
                                                w1bd[0:24, :], start=True, stop=True)
                elif u < 6:
                    v = u - 2
                    pe.wait_ge(S["z_hT"], v // 2 + 1)
                    for c in range(2):
                        i = 2 * v + c
                        last = nc.tensor.matmul(z[:, 256 * c:256 * c + 256], h1T[:, 128 * i:128 * i + 128],
                                                w2bd[:, :], start=True, stop=True)
                else:
                    i = u - 6
                    pe.wait_ge(S["z_hT"], 2 + i // 2 + 1)
                    for hf in range(2):
                        last = nc.tensor.matmul(z[:, 256 * hf:256 * hf + 256],
                                                h2T[:, 1024 * hf + 128 * i:1024 * hf + 128 * i + 128],
                                                w3bd[:, :], start=True, stop=True)
                last.then_inc(S["z_mm"], 1)

            def tr(u):
                pe.wait_ge(S["z_zn"], u + 1)
                if u >= 2:
                    pe.wait_ge(S["z_hT"], u - 1)
                for c in range(4):
                    last = nc.tensor.transpose(tbank[u % 2][:, 128 * c:128 * c + 128],
                                               zn[u % 2][:, 128 * c:128 * c + 128], k("ident"))
                last.then_inc(S["z_tr"], 1)

            pe.wait_ge(S["ld_k"], 32)
            mm(0)
            mm(1)
            tr(0)
            mm(2)
            mm(3)
            tr(1)
            mm(4)
            mm(5)
            tr(2)
            mm(6)
            mm(7)
            tr(3)
            mm(8)
            mm(9)
            tr(4)
            tr(5)
            for u in range(10, 14):
                mm(u)
            pe.wait_ge(S["w_split"], 1)

            ropew = w("rope").rearrange("p (m b o) -> p m b o", m=4, b=2)

            def project(m, bank):
                dst = bank[:].rearrange("p (i b t) -> p b i t", i=2, b=2)
                for b in range(2):
                    last = nc.tensor.matmul(dst[:, b, :, :], ropew[:, m, b, :], fxT[:, :, :], start=True, stop=True)
                return last

            def do(part, p, s, g, n):
                if part == "front_norm":
                    pe.wait_ge(S["a_xn"], p + 1)
                    before(pe, "a_qk", p, 1)
                    before(pe, "a_v", p, 1)
                    nc.tensor.transpose(pA[:, 384:512], xn[:].rearrange("p b c -> p (b c)"),
                                        k("ident")).then_inc(S["a_tr"], 1)
                elif part == "front_mm":
                    pe.wait_ge(S["a_xT"], p + 1)
                    nc.tensor.matmul(pA[:, 0:128], w("qk")[:, 0:128], xT[:], start=True, stop=True)
                    nc.tensor.matmul(pA[:, 128:256], w("qk")[:, 128:256], xT[:], start=True, stop=True)
                    nc.tensor.matmul(pA[:, 256:384], xT[:], w("v"), start=True, stop=True).then_inc(S["a_mm"], 1)
                elif part == "sum2":
                    if n == 0:
                        pe.wait_ge(S["i_dve"], p + 1)
                        pe.wait_ge(S["i_ptr"], p + 1)
                        nth(pe, "i_sgn", p, NP, NP)
                        pe.wait_ge(S["a_bd"], p + 1)
                    if not (isinstance(p, int) and p == 0):
                        pe.wait_ge(S["t1_s"], 2 * p - 1 + n)
                    col, tok = 512 * n, T // 2 * n
                    nc.tensor.matmul(pT[:, col:col + 512], hc("sign_rows"),
                                     bd[s][:, 1, tok:tok + T // 2, :, :].rearrange("p a b c -> p (a b c)"),
                                     start=True, stop=False)
                    for i in range(T // 2):
                        last = nc.tensor.matmul(
                            pT[:, col + 8 * i:col + 8 * i + 8], ind[s][:, :, tok + i],
                            bd[s][:, 1, tok + i, :, :].rearrange("p b c -> p (b c)"),
                            start=False, stop=i == T // 2 - 1)
                    last.then_inc(S["t2_mm"], 1)
                elif part == "sum1":
                    nth(pe, "t2_s", p, 2, n + 1)
                    col, tok = 512 * n, T // 2 * n
                    signs = max(tok, N_DVE)
                    if signs < tok + T // 2:
                        first = 8 * (signs - tok)
                        nc.tensor.matmul(pT[:, col + first:col + 512], hc("ones"),
                                         bd[s][:, 0, signs:tok + T // 2, :, :].rearrange("p a b c -> p (a b c)"),
                                         start=True, stop=False)
                    for i in range(T // 2):
                        sign = tok + i >= signs
                        last = nc.tensor.matmul(
                            pT[:, col + 8 * i:col + 8 * i + 8], ind[s][:, tok + i, :],
                            bd[s][:, 0, tok + i, :, :].rearrange("p b c -> p (b c)"),
                            start=not sign, stop=not sign or i == T // 2 - 1)
                    last.then_inc(S["t1_mm"], 1)
                elif part == "soft_t":
                    nth(pe, "t1_s", p, 2, 2)
                    before(pe, "s_h1", p, 1)
                    for b in range(BG):
                        last = nc.tensor.transpose(pS[:, 128 * b:128 * b + 128], t1s[:, b, :], k("ident"))
                    last.then_inc(S["s_tp"], 1)
                elif part == "soft_pt":
                    pe.wait_ge(S["s_p"], p + 1)
                    pe.wait_ge(S["s_raw"], p + 1)
                    for b in range(BG):
                        last = nc.tensor.transpose(pS[:, 128 * b:128 * b + 128], att[:, b, :], k("ident"))
                    last.then_inc(S["s_pt"], 1)
                elif part == "soft_pv":
                    pe.wait_ge(S["s_ptT"], p + 1)
                    for b in range(BG):
                        last = nc.tensor.matmul(pS[:, VW * b:VW * b + VW], attT[:, b, :],
                                                va[s][:, b // G2, b % G2, :], start=True, stop=True)
                    last.then_inc(S["s_pv"], 1)
                elif part == "f_tr":
                    pe.wait_ge(S["f_x"], g + 1)
                    before(pe, "f_oe", g, 4)
                    for i in range(2):
                        last = nc.tensor.transpose(pF[2][:, 128 * i:128 * i + 128],
                                                   fxr[:, 2 * i:2 * i + 2, :].rearrange("p b c -> p (b c)"),
                                                   k("ident"))
                    last.then_inc(S["f_tr"], 1)
                elif part == "f_q":
                    pe.wait_ge(S["f_xT"], g + 1)
                    for i in range(2):
                        last = nc.tensor.matmul(pF[2][:, 256 + 64 * i:320 + 64 * i], fxT[:, i, :], w("vf"),
                                                start=True, stop=True)
                    last.then_inc(S["f_v"], 1)
                    project(0, pF[0])
                    project(1, pF[1]).then_inc(S["f_q"], 1)
                elif part == "f_k":
                    pe.wait_ge(S["f_va"], g + 1)
                    project(2, pF[2])
                    project(3, pF[3]).then_inc(S["f_k"], 1)
                elif part == "f_sc":
                    if n == 0:
                        pe.wait_ge(S["f_qe"], g + 1)
                        pe.wait_ge(S["f_ke"], g + 1)
                        pe.wait_ge(S["f_kep"], g + 1)
                        pe.wait_ge(S["f_krope"], g + 1)
                    nc.tensor.matmul(pF[n][:], qe[:, n, :], ke[:, n, :, :].rearrange("p h t -> p (h t)"),
                                     start=True, stop=True).then_inc(S["f_sc"], 1)
                elif part == "f_turn":
                    nth(pe, "f_p", g, 4, n + 1)
                    for h in range(NH):
                        last = nc.tensor.transpose(pF[n][:, 128 * h:128 * h + 128], fp[n][:, h, :], k("ident"))
                    last.then_inc(S["f_pt"], 1)
                elif part == "f_val":
                    nth(pe, "f_ptT", g, 4, n + 1)
                    for h in range(NH):
                        last = nc.tensor.matmul(pF[n][:, KW * h:KW * h + KW], fpT[n][:, h, :],
                                                vf[:, n, h * NKV // NH, :], start=True, stop=True)
                    last.then_inc(S["f_pv"], 1)
                elif part == "f_yt":
                    nth(pe, "f_y", g, 4, 4)
                    for i in range(2):
                        last = nc.tensor.transpose(pF[0][:, 128 * i:128 * i + 128],
                                                   y[:, 2 * i:2 * i + 2, :].rearrange("p b c -> p (b c)"), k("ident"))
                    last.then_inc(S["f_yt"], 1)
                elif part == "f_wo":
                    pe.wait_ge(S["f_yT"], g + 1)
                    for i in range(2):
                        last = nc.tensor.matmul(pF[0][:, 256 + 128 * i:384 + 128 * i], yT[:, i, :], w("wo"),
                                                start=True, stop=True)
                    last.then_inc(S["f_wo"], 1)
                elif part == "f_xs":
                    pe.wait_ge(S["f_xs"], g + 1)
                    for b in range(4):
                        last = nc.tensor.transpose(pF[1][:].bitcast(F16)[:, 128 * b:128 * b + 128],
                                                   xs[:, b, :, :].rearrange("p a c -> p (a c)"), hc("ident"))
                    last.then_inc(S["f_xst"], 1)
                elif part == "f_route":
                    pe.wait_ge(S["f_xsT"], g + 1)
                    for b in range(4):
                        dst = pF[2][:, NE * b:NE * b + NE]
                        nc.tensor.matmul(dst, xsT[:, 128 * b:128 * b + 128], wrh[:], start=True, stop=False)
                        last = nc.tensor.matmul(dst, xsT[:, 128 * b:128 * b + 128], wrl[:], start=False, stop=True)
                    last.then_inc(S["f_lg"], 1)
                elif part == "f_h":
                    one, three = pF[2 * (n % 2)], pF[2 * (n % 2) + 1]
                    if n == 1:
                        pe.wait_ge(S["f_la"], g + 1)
                    if n >= 2:
                        nth(pe, "f_sg", g, NT, n - 1)
                    nc.tensor.matmul(one[:], w1h[:, n, :], xsT[:], start=True, stop=False)
                    nc.tensor.matmul(one[:], w1l[:, n, :], xsT[:], start=False, stop=True)
                    if n >= 2:
                        nth(pe, "f_hh", g, NT, n - 1)
                    nc.tensor.matmul(three[:], w3h[:, n, :], xsT[:], start=True, stop=False)
                    nc.tensor.matmul(three[:], w3l[:, n, :], xsT[:], start=False, stop=True).then_inc(S["f_h13"], 1)
                elif part == "f_e":
                    if n == 0:
                        nth(pe, "f_hh", g, NT, NT)
                    for t in range(NT):
                        e0 = first_expert(t)
                        last = nc.tensor.matmul(pF[n][:, C * e0:C * e0 + 2 * C],
                                                hh[:, t, 128 * n:128 * n + 128],
                                                w("w2")[:, P * t:P * t + P], start=t == 0, stop=t == NT - 1,
                                                skip_group_check=True)
                    last.then_inc(S["f_e"], 1)

            sequence(do, pe)

        @block.scalar
        def _(act):
            zbank = [pT[:, 0:512], pT[:, 512:1024], pF[0][:], pF[1][:]]
            tbank = [pA, pS]

            def square(u):
                act.wait_ge(S["z_mm"], u + 1)
                if u >= 2:
                    act.wait_ge(S["z_ms"], u - 1)
                nc.scalar.activation(sq[u % 2][:, 0:512], zbank[u % 4], ACT.Square).then_inc(S["z_sq"], 1)

            def root(u):
                width = D1 if u < 2 else D2 if u < 6 else C
                act.wait_ge(S["z_ms"], u + 1)
                if u >= 2:
                    act.wait_ge(S["z_zn"], u - 1)
                nc.scalar.activation(psd[u % 2][:, 0:512 // width], pms[u % 2][:, 0:512 // width], ACT.Sqrt,
                                     bias=k("eps"), scale=1.0 / width).then_inc(S["z_sd"], 1)

            def evac(u):
                act.wait_ge(S["z_tr"], u + 1)
                if u < 2:
                    nc.scalar.activation(h1T[:, 512 * u:512 * u + 512], tbank[u % 2][:], ACT.Relu,
                                         bias=w("b1"), scale=w("g1")).then_inc(S["z_hT"], 1)
                else:
                    v = u - 2
                    dst = h2T[:, :].rearrange("p (h i t) -> p i h t", h=2, t=T)[:, 2 * v:2 * v + 2, :, :]
                    nc.scalar.activation(dst, tbank[u % 2][:].rearrange("p (i h t) -> p i h t", i=2, h=2), ACT.Relu,
                                         bias=w("b2"), scale=w("g2")).then_inc(S["z_hT"], 1)

            act.wait_ge(S["ld_w"], 16)
            act.wait_ge(S["ld_k"], 32)
            square(0)
            square(1)
            root(0)
            root(1)
            evac(0)
            square(2)
            square(3)
            evac(1)
            root(2)
            root(3)
            square(4)
            square(5)
            evac(2)
            root(4)
            root(5)
            square(6)
            square(7)
            evac(3)
            root(6)
            root(7)
            square(8)
            square(9)
            evac(4)
            root(8)
            root(9)
            square(10)
            square(11)
            evac(5)
            root(10)
            root(11)
            square(12)
            square(13)
            root(12)
            root(13)
            act.wait_ge(S["pool_pro"], 1)
            act.wait_ge(S["z_st0"], 16 * 4)
            act.wait_ge(S["z_st1"], 16 * 4)
            act.wait_ge(S["z_mm"], 14)

            def do(part, p, s, g, n):
                if part == "front_norm":
                    act.wait_ge(S["a_tr"], p + 1)
                    nc.scalar.activation(xT[:], pA[:, 384:512], ACT.Copy).then_inc(S["a_xT"], 1)
                elif part == "front_mm":
                    act.wait_ge(S["a_mm"], p + 1)
                    before(act, "i_dve", p, 1, 2)
                    before(act, "i_ptr", p, 1, 2)
                    before(act, "i_sgn", p, NP, 2)
                    nc.scalar.activation(qk[s][:].rearrange("p a t -> p (a t)"), pA[:, 0:256],
                                         ACT.Copy).then_inc(S["a_qk"], 1)
                    before(act, "s_pv", p, 1, 2)
                    nc.scalar.activation(va[s][:, :, :, 0:DG], pA[:, 256:384].rearrange(
                        "p (b d g) -> p b g d", b=2, g=G2), ACT.Copy).then_inc(S["a_v"], 1)
                elif part == "ptr":
                    if n == 0:
                        before(act, "t1_mm", p, 2, 2)
                        act.wait_ge(S["a_qk"], p + 1)
                    for i in range(4):
                        q = N_DVE + N_POOL + 4 * n + i
                        ins = nc.scalar.activation(ind[s][:, q, :], qk[s][:, 1, :], ACT.Sign,
                                                   bias=qk[s][:, 0, q:q + 1], scale=-1.0)
                    if n == N_ACT // 4 - 1:
                        ins.then_inc(S["i_ptr"], 1)
                elif part == "sgn":
                    before(act, "t1_mm", p, 2, 2)
                    nth(act, "i_dif", p, NP, n + 1)
                    q = N_DVE + CH * n
                    ins = nc.scalar.activation(ind[s][:, q:q + CH, :], difs(s, n)[:], ACT.Sign)
                    ins.then_inc(S["i_sgn"], 1)
                elif part == "soft_m":
                    act.wait_ge(S["s_raw"], p + 1)
                    before(act, "s_pt", p, 1)
                    nc.scalar.activation(att[:].rearrange("p b t -> p (b t)"), raw[:].rearrange("p b t -> p (b t)"),
                                         ACT.Relu, bias=w("b_mlp"), scale=k("alpha")).then_inc(S["act_s"], 1)
                elif part == "soft_e":
                    act.wait_ge(S["act_s"], p + 1)
                    act.wait_ge(S["s_m"], p + 1)
                    for b in range(BG):
                        last = nc.scalar.activation(att[:, b, :], att[:, b, :], ACT.Exp, bias=nm[:, b:b + 1])
                    last.then_inc(S["s_p"], 1)
                elif part == "soft_pt":
                    act.wait_ge(S["s_pt"], p + 1)
                    nc.scalar.activation(attT[:].rearrange("p b t -> p (b t)"), pS[:], ACT.Copy).then_inc(S["s_ptT"], 1)
                elif part == "f_tr":
                    act.wait_ge(S["f_tr"], g + 1)
                    nc.scalar.activation(fxT[:].rearrange("p i t -> p (i t)"), pF[2][:, 0:256],
                                         ACT.Copy).then_inc(S["f_xT"], 1)
                elif part == "f_q":
                    act.wait_ge(S["f_v"], g + 1)
                    nc.scalar.activation(vf[:, :, :, 0:HD], pF[2][:, 256:384].rearrange(
                        "p (b v d) -> p b v d", b=4, v=NKV), ACT.Copy).then_inc(S["f_va"], 1)
                elif part == "f_exp":
                    nth(act, "f_nm", g, 4, n + 1)
                    for h in range(NH):
                        last = nc.scalar.activation(fp[n][:, h, :], sc[n][:, h, :], ACT.Exp,
                                                    bias=fnm[n][:, h:h + 1], scale=HD ** -0.5)
                    last.then_inc(S["f_p"], 1)
                elif part == "f_turn":
                    nth(act, "f_pt", g, 4, n + 1)
                    nc.scalar.activation(fpT[n][:].rearrange("p h t -> p (h t)"), pF[n][:],
                                         ACT.Copy).then_inc(S["f_ptT"], 1)
                elif part == "f_yt":
                    act.wait_ge(S["f_yt"], g + 1)
                    nc.scalar.activation(yT[:].rearrange("p i t -> p (i t)"), pF[0][:, 0:256],
                                         ACT.Copy).then_inc(S["f_yT"], 1)
                elif part == "f_rms":
                    act.wait_ge(S["f_x2"], g + 1)
                    for b in range(4):
                        last = nc.scalar.activation(sg[0][:, 64 * b:64 * b + 64], x2[:, b, :], ACT.Square,
                                                    accum_out=ms[:, b:b + 1])
                    last.then_inc(S["f_ms"], 1)
                elif part == "f_xs":
                    act.wait_ge(S["f_xst"], g + 1)
                    nc.scalar.activation(xsT[:], pF[1][:].bitcast(F16)[:, 0:512], ACT.Copy).then_inc(S["f_xsT"], 1)
                elif part == "f_route":
                    act.wait_ge(S["f_la"], g + 1)
                    nc.scalar.activation(lg["e"][:].rearrange("p b e -> p (b e)"),
                                         lg["a"][:].rearrange("p b e -> p (b e)"), ACT.Exp).then_inc(S["f_le"], 1)
                elif part == "f_h":
                    nth(act, "f_h13", g, NT, n + 1)
                    if n >= 2:
                        nth(act, "f_hh", g, NT, n - 1)
                    elif n == 0:
                        act.wait_ge(S["f_ms"], g + 1)
                    nc.scalar.activation(sg[n % 2][:], pF[2 * (n % 2)][:], ACT.Silu).then_inc(S["f_sg"], 1)

            sequence(do, act)

        @block.gpsimd
        def _(pool):
            nc.gpsimd.memset(half[:], -0.5)
            for s in range(2):
                nc.gpsimd.memset(va[s][:], 1.0)
            nc.gpsimd.memset(vf[:], 1.0).then_inc(S["pool_pro"], 1)
            pool.wait_ge(S["ld_w"], 16)
            for i in range(8):
                pool.wait_ge(S["z_zn"], 6 + i + 1)
                if i >= 2:
                    pool.wait_ge(S[f"z_st{i % 2}"], 16 * (i // 2))
                z, g, o = zn[i % 2][:, 0:512], h3g[i % 2][:, 0:512], h3o[i % 2][:, 0:512]
                g3 = w("g3").unsqueeze(1).to_broadcast([P, 8, C])
                b3 = w("b3").unsqueeze(1).to_broadcast([P, 8, C])
                nc.gpsimd.tensor_tensor(g.rearrange("p (a c) -> p a c", c=C), z.rearrange("p (a c) -> p a c", c=C), g3,
                                        ALU.mult).then_inc(S["pool_pro"], 1)
                pool.wait_ge(S["pool_pro"], i + 2)
                nc.gpsimd.tensor_tensor(o.rearrange("p (a c) -> p a c", c=C), g.rearrange("p (a c) -> p a c", c=C), b3,
                                        ALU.add).then_inc(S["z_gb"], 1)

            latest = [0]

            def do(part, p, s, g, n):
                if part == "dif":
                    pool.wait_ge(S["a_qk"], p + 1)
                    if not (isinstance(p, int) and p * NP + n < ND):
                        pool.wait_ge(S["i_sgn"], p * NP + n + 1 - ND)
                    q = N_DVE + CH * n
                    nc.gpsimd.tensor_tensor(difs(s, n)[:], qk[s][:, 0, q:q + CH].unsqueeze(2).to_broadcast([P, CH, T]),
                                            qk[s][:, 1, :].unsqueeze(1).to_broadcast([P, CH, T]),
                                            ALU.subtract).then_inc(S["i_dif"], 1)
                    latest[:] = [p * NP + n + 1]
                elif part == "front_stat":
                    ch = Chain(pool, "pool_a", p, 1)
                    pool.wait_ge(S["a_mv"], p + 1)
                    ch.link(nc.gpsimd.tensor_tensor(ve[:], mv[:, :, 1], k("ln_eps")[:, 0:2], ALU.add))
                    ch.end()
                    nc.gpsimd.tensor_tensor(rstd[:], ve[:], half[:, 0:2], ALU.pow).then_inc(S["a_rstd"], 1)
                elif part == "front_split":
                    pool.wait_ge(S["a_w"], p + 1)
                    before(pool, "t1_mm", p, 2, 2)
                    for part2, src in ((0, wh), (1, wl)):
                        if part2 == 1:
                            pool.wait_ge(S["a_wl"], p + 1)
                        last = nc.gpsimd.tensor_tensor(
                            bd[s][:].rearrange("p a t r b -> p (a t) r b")[:, :, part2, :],
                            src[:].unsqueeze(2).to_broadcast([P, 2 * T, BG]),
                            hc("bg").unsqueeze(1).to_broadcast([P, 2 * T, BG]), ALU.mult)
                    last.then_inc(S["a_bd"], 1)
                elif part == "f_stat":
                    ch = Chain(pool, "pool_f", g, 5)
                    pool.wait_ge(S["f_mv"], g + 1)
                    var = fmv[:, :, 1]
                    ch.link(nc.gpsimd.tensor_tensor(fv[:], var, k("ln_eps"), ALU.add))
                    ch.link(nc.gpsimd.tensor_tensor(fr[:], fv[:], half[:], ALU.pow))
                    ch.link(nc.gpsimd.tensor_tensor(ft[:], fr[:], fr[:], ALU.mult))
                    ch.link(nc.gpsimd.tensor_tensor(ft[:], ft[:], var, ALU.mult))
                    ch.link(nc.gpsimd.tensor_tensor(ft[:], ft[:], k("rms_eps"), ALU.add))
                    ch.end()
                    nc.gpsimd.tensor_tensor(fu[:], ft[:], half[:], ALU.pow).then_inc(S["f_r"], 1)
                elif part == "f_norm":
                    pool.wait_ge(S["f_x"], g + 1)
                    before(pool, "f_out", g, 4)
                    nc.gpsimd.tensor_tensor(res[:], h1[:], fx[:], ALU.add).then_inc(S["f_xo"], 1)
                elif part == "f_rotq":
                    pool.wait_ge(S["f_qrope"], g + 1)
                    nc.gpsimd.tensor_tensor(qe[:], r1[:], r2[:], ALU.add).then_inc(S["f_qe"], 1)
                elif part == "f_ke":
                    pool.wait_ge(S["f_krope"], g + 1)
                    pool.wait_ge(S["i_dif"], latest[0])
                    pool.wait_ge(S["f_qe"], g + 1)
                    for h in range(2, NH):
                        rows = slice(HP * h, HP * h + HP)
                        last = nc.gpsimd.tensor_tensor(ke[rows, :, h, :], r3[rows], r4[rows], ALU.add)
                    last.then_inc(S["f_kep"], 1)
                    pool.wait_ge(S["f_kep"], g + 1)
                elif part == "f_rms":
                    pool.wait_ge(S["f_ms"], g + 1)
                    nc.gpsimd.tensor_tensor(fm[:], ms[:], k("mean"), ALU.mult).then_inc(S["f_rq"], 1)
                    nth(pool, "f_rq", g, 3, 1)
                    nc.gpsimd.tensor_tensor(fv[:], fm[:], k("rms_eps"), ALU.add).then_inc(S["f_rq"], 1)
                    nth(pool, "f_rq", g, 3, 2)
                    nc.gpsimd.tensor_tensor(fq[:], fv[:], half[:], ALU.pow).then_inc(S["f_rq"], 1)

            sequence(do, pool)

        @block.vector
        def _(dve):
            ch = Chain(dve, "dve_pro", 0, 10)
            nc.vector.memset(ke[:], 0.0)
            dve.wait_ge(S["ld_c"], 32)
            dve.wait_ge(S["ld_k"], 32)
            ch.link(nc.vector.tensor_scalar(cf[0:24, :], craw[0:24, :], k("scale")[0:24, :], -1.0, ALU.mult, ALU.add))
            nc.vector.tensor_tensor(cT[0:24, :], cf[0:24, :], vraw[0:24, :], ALU.mult).then_inc(S["c_ready"], 1)
            dve.wait_ge(S["ld_w"], 16)
            srcs = [(w("t1"), 0, D1), (w("t2"), D1, D2), (w("t3"), D1 + D2, C)]
            for i, (src, at, n) in enumerate(srcs):
                ch.step(nc.vector.tensor_reduce(wm[:, i:i + 1], src, AX, ALU.add))
            ch.wait()
            for i, (src, at, n) in enumerate(srcs):
                ch.step(nc.vector.tensor_scalar(wn[:, i:i + 1], wm[:, i:i + 1], -1.0 / n, None, ALU.mult))
            ch.wait()
            for i, (src, at, n) in enumerate(srcs):
                ch.step(nc.vector.tensor_scalar(wc[:, at:at + n], src, wn[:, i:i + 1], None, ALU.add))
            ch.wait()
            ch.end()
            for dst, mask, nb, at, n in ((w1bd, "m1", 8, 0, D1), (w2bd, "m2", 8, D1, D2), (w3bd, "m3", 4, D1 + D2, C)):
                last = nc.vector.tensor_tensor(dst[:, 0:nb * n].rearrange("p (b n) -> p b n", b=nb),
                                               wc[:, at:at + n].unsqueeze(1).to_broadcast([P, nb, n]),
                                               k(mask).unsqueeze(2).to_broadcast([P, nb, n]), ALU.mult)
            last.then_inc(S["wbd_ready"], 1)
            nc.vector.tensor_scalar(w("rope"), w("rope"), w("ln1"), None, ALU.mult)
            nc.vector.tensor_scalar(w("vf"), w("vf"), w("ln1"), None, ALU.mult)

            def mean_square(u):
                width = D1 if u < 2 else D2 if u < 6 else C
                dve.wait_ge(S["z_sq"], u + 1)
                if u >= 2:
                    dve.wait_ge(S["z_sd"], u - 1)
                nc.vector.tensor_reduce(pms[u % 2][:, 0:512 // width],
                                        sq[u % 2][:, 0:512].rearrange("p (a c) -> p a c", c=width),
                                        AX, ALU.add).then_inc(S["z_ms"], 1)

            def normalise(u):
                width = D1 if u < 2 else D2 if u < 6 else C
                n = 512 // width
                z = [pT[:, 0:512], pT[:, 512:1024], pF[0][:], pF[1][:]][u % 4]
                dve.wait_ge(S["z_sd"], u + 1)
                nc.vector.reciprocal(prs[u % 2][:, 0:n], psd[u % 2][:, 0:n]).then_inc(S["z_rs"], 1)
                dve.wait_ge(S["z_rs"], u + 1)
                if 2 <= u < 8:
                    dve.wait_ge(S["z_tr"], u - 1)
                elif u >= 8:
                    dve.wait_ge(S["z_gb"], u - 7)
                nc.vector.tensor_tensor(zn[u % 2][:, 0:512].rearrange("p (a c) -> p a c", c=width),
                                        z.rearrange("p (a c) -> p a c", c=width),
                                        prs[u % 2][:, 0:n].unsqueeze(2).to_broadcast([P, n, width]),
                                        ALU.mult).then_inc(S["z_zn"], 1)

            for u in range(0, 14, 2):
                mean_square(u)
                mean_square(u + 1)
                normalise(u)
                normalise(u + 1)
            dve.wait_ge(S["ld_w13"], 16)
            n13 = NT * P
            flat = lambda x: x[:].rearrange("p t n -> p (t n)")
            raw13 = w13raw[:, 0:2 * n13]
            nc.vector.tensor_scalar(raw13, raw13, w("ln2"), None, ALU.mult)
            nc.vector.tensor_scalar(w("router"), w("router"), w("ln2"), None, ALU.mult).then_inc(S["w_ln"], 1)
            dve.wait_ge(S["w_ln"], 1)
            nc.vector.tensor_copy(flat(w1h), raw13[:, 0:n13])
            nc.vector.tensor_copy(flat(w3h), raw13[:, n13:2 * n13])
            nc.vector.tensor_copy(wrh[:], w("router")).then_inc(S["w_ln"], 1)
            dve.wait_ge(S["w_ln"], 2)
            nc.vector.tensor_tensor(flat(w1l), raw13[:, 0:n13], flat(w1h), ALU.subtract)
            nc.vector.tensor_tensor(flat(w3l), raw13[:, n13:2 * n13], flat(w3h), ALU.subtract)
            nc.vector.tensor_tensor(wrl[:], w("router"), wrh[:], ALU.subtract).then_inc(S["w_split"], 1)
            dve.wait_ge(S["w_split"], 1)
            dve.wait_ge(S["z_st0"], 16 * 4)
            dve.wait_ge(S["z_st1"], 16 * 4)
            dve.wait_ge(S["z_mm"], 14)

            def rotate(a, b, cosine, sine):
                cos = k("cos").unsqueeze(1).to_broadcast([P, 4, T])
                sin = k("sin").unsqueeze(1).to_broadcast([P, 4, T])
                nc.vector.tensor_tensor(cosine[:], a[:].rearrange("p (b t) -> p b t", b=4), cos, ALU.mult)
                return nc.vector.tensor_tensor(sine[:], b[:].rearrange("p (b t) -> p b t", b=4), sin, ALU.mult)

            def do(part, p, s, g, n):
                if part == "front_stat":
                    ch = Chain(dve, "dve_front", p, 1)
                    nth(dve, f"ld_a{s}", g, 16, 16)
                    for b in range(2):
                        last = nc.vector.bn_stats(stat[:, b, :], hin[s][:, b, :])
                    ch.link(last)
                    ch.end()
                    nc.vector.memset(pause[:], 0.0)
                    for b in range(2):
                        last = nc.vector.bn_aggr(mv[:, b, :], stat[:, b, :])
                    last.then_inc(S["a_mv"], 1)
                elif part == "front_norm":
                    dve.wait_ge(S["a_rstd"], p + 1)
                    dve.wait_ge(S["a_mv"], p + 1)
                    before(dve, "a_tr", p, 1)
                    for b in range(2):
                        last = nc.vector.tensor_scalar(xn[:, b, :], hin[s][:, b, :], mv[:, b, 0:1], rstd[:, b:b + 1],
                                                       ALU.subtract, ALU.mult)
                    last.then_inc(S["a_xn"], 1)
                elif part == "front_split":
                    dve.wait_ge(S["a_qk"], p + 1)
                    before(dve, "a_bd", p, 1)
                    flat2 = qk[s][:].rearrange("p a t -> p (a t)")
                    nc.vector.tensor_scalar(wh[:], flat2, w("w_mlp"), None, ALU.mult).then_inc(S["a_w"], 1)
                    dve.wait_ge(S["a_w"], p + 1)
                    nc.vector.scalar_tensor_tensor(wl[:], flat2, w("w_mlp"), wh[:], ALU.mult,
                                                   ALU.subtract).then_inc(S["a_wl"], 1)
                elif part == "cmp":
                    if n == 0:
                        before(dve, "t1_mm", p, 2, 2)
                        dve.wait_ge(S["a_qk"], p + 1)
                    q = CV * n
                    ins = nc.vector.tensor_tensor(ind[s][:, q:q + CV, :],
                                                  qk[s][:, 1, :].unsqueeze(1).to_broadcast([P, CV, T]),
                                                  qk[s][:, 0, q:q + CV].unsqueeze(2).to_broadcast([P, CV, T]),
                                                  ALU.is_lt)
                    if n == N_DVE // CV - 1:
                        ins.then_inc(S["i_dve"], 1)
                elif part == "red2":
                    nth(dve, "t2_mm", p, 2, n + 1)
                    half_k, bank = slice(T // 2 * n, T // 2 * n + T // 2), slice(512 * n, 512 * n + 512)
                    nc.vector.tensor_reduce(t2s[:, :, half_k], pT[:, bank].rearrange("p (k r b) -> p b k r", r=2, b=BG),
                                            AX, ALU.add, negate=True).then_inc(S["t2_s"], 1)
                elif part == "red1":
                    nth(dve, "t1_mm", p, 2, n + 1)
                    before(dve, "s_tp", p, 1)
                    half_q, bank = slice(T // 2 * n, T // 2 * n + T // 2), slice(512 * n, 512 * n + 512)
                    nc.vector.tensor_reduce(t1s[:, :, half_q], pT[:, bank].rearrange("p (k r b) -> p b k r", r=2, b=BG),
                                            AX, ALU.add).then_inc(S["t1_s"], 1)
                elif part == "soft_m":
                    dve.wait_ge(S["s_tp"], p + 1)
                    nth(dve, "t2_s", p, 2, 2)
                    before(dve, "act_s", p, 1)
                    nc.vector.tensor_tensor(raw[:].rearrange("p b t -> p (b t)"), pS[:],
                                            t2s[:].rearrange("p b t -> p (b t)"), ALU.add).then_inc(S["s_raw"], 1)
                    dve.wait_ge(S["s_raw"], p + 1)
                    ch = Chain(dve, "dve_soft", p, 2)
                    ch.link(nc.vector.tensor_reduce(mx[:], raw[:], AX, ALU.max))
                    ch.link(nc.vector.tensor_scalar(mb[:], mx[:], k("alpha"), w("b_mlp"), ALU.mult, ALU.add))
                    ch.end()
                    before(dve, "s_p", p, 1)
                    nc.vector.tensor_scalar(nm[:], mb[:], 0.0, -1.0, ALU.max, ALU.mult).then_inc(S["s_m"], 1)
                elif part == "pair_add":
                    dve.wait_ge(S["s_pv"], p + 1)
                    pv = pS[:, 0:BG * VW].rearrange("p (b v) -> p b v", v=VW)
                    ch = Chain(dve, "dve_value", p, 2)
                    ch.link(nc.vector.reciprocal(rden[:], pv[:, :, DG]))
                    ch.link(nc.vector.tensor_tensor(add[:].rearrange("p b (d g) -> p b g d", g=G2),
                                                    pv[:, :, 0:DG].rearrange("p (b g) d -> p b g d", g=G2),
                                                    rden[:].rearrange("p (b g) -> p b g", g=G2).unsqueeze(3)
                                                    .to_broadcast([P, 2, G2, DG]), ALU.mult))
                    ch.end()
                    nth(dve, f"ld_r{s}", g, 16, 16)
                    nc.vector.tensor_tensor(h1[:, 2 * s:2 * s + 2, :], h1[:, 2 * s:2 * s + 2, :], add[:],
                                            ALU.add).then_inc(S["s_h1"], 1)
                elif part == "f_stat":
                    dve.wait_ge(S["s_h1"], g * 2 + 2)
                    ch = Chain(dve, "dve_rope", g, 1)
                    for b in range(4):
                        last = nc.vector.bn_stats(fstat[:, b, :], h1[:, b, :])
                    ch.link(last)
                    ch.end()
                    nc.vector.memset(pause[:], 0.0)
                    for b in range(4):
                        last = nc.vector.bn_aggr(fmv[:, b, :], fstat[:, b, :])
                    last.then_inc(S["f_mv"], 1)
                elif part == "f_norm":
                    dve.wait_ge(S["f_mv"], g + 1)
                    dve.wait_ge(S["f_r"], g + 1)
                    nc.vector.tensor_tensor(frr[:], fr[:], fu[:], ALU.mult).then_inc(S["f_rr"], 1)
                    dve.wait_ge(S["f_rr"], g + 1)
                    for dst, r in ((fxr, frr), (fx, fr)):
                        for b in range(4):
                            last = nc.vector.tensor_scalar(dst[:, b, :], h1[:, b, :], fmv[:, b, 0:1], r[:, b:b + 1],
                                                           ALU.subtract, ALU.mult)
                    last.then_inc(S["f_x"], 1)
                elif part == "f_rotq":
                    dve.wait_ge(S["f_q"], g + 1)
                    rotate(pF[0], pF[1], r1, r2).then_inc(S["f_qrope"], 1)
                elif part == "f_rotk":
                    dve.wait_ge(S["f_k"], g + 1)
                    rotate(pF[2], pF[3], r3, r4).then_inc(S["f_krope"], 1)
                elif part == "f_ke":
                    dve.wait_ge(S["f_krope"], g + 1)
                    for h in range(2):
                        rows = slice(HP * h, HP * h + HP)
                        last = nc.vector.tensor_tensor(ke[rows, :, h, :], r3[rows], r4[rows], ALU.add)
                    last.then_inc(S["f_ke"], 1)
                elif part == "f_mask":
                    nth(dve, "f_sc", g, 4, n + 1)
                    nc.vector.tensor_tensor(sc[n][:], pF[n][:].rearrange("p (h t) -> p h t", h=NH),
                                            k("causal").unsqueeze(1).to_broadcast([P, NH, T]),
                                            ALU.add).then_inc(S["f_scm"], 1)
                    nth(dve, "f_scm", g, 8, 2 * n + 1)
                    nc.vector.tensor_reduce(fmx[n][:], sc[n][:], AX, ALU.max).then_inc(S["f_scm"], 1)
                    nth(dve, "f_scm", g, 8, 2 * n + 2)
                    nc.vector.tensor_scalar(fnm[n][:], fmx[n][:], -HD ** -0.5, None, ALU.mult).then_inc(S["f_nm"], 1)
                elif part == "f_weigh":
                    nth(dve, "f_pv", g, 4, n + 1)
                    pv = pF[n][:, 0:NH * KW].rearrange("p (h v) -> p h v", v=KW)
                    nc.vector.reciprocal(frd[n][:], pv[:, :, HD]).then_inc(S["f_rd"], 1)
                    nth(dve, "f_rd", g, 4, n + 1)
                    nc.vector.tensor_tensor(y[:, n, :].rearrange("p (h d) -> p h d", h=NH), pv[:, :, 0:HD],
                                            frd[n][:].unsqueeze(2).to_broadcast([P, NH, HD]),
                                            ALU.mult).then_inc(S["f_y"], 1)
                elif part == "f_wo":
                    dve.wait_ge(S["f_wo"], g + 1)
                    wo = pF[0][:, 256:512].rearrange("p (b c) -> p b c", b=4)
                    nc.vector.tensor_tensor(x2[:], fx[:], wo, ALU.add).then_inc(S["f_x2"], 1)
                    dve.wait_ge(S["f_xo"], g + 1)
                    nc.vector.tensor_tensor(res[:], res[:], wo, ALU.add).then_inc(S["f_res"], 1)
                elif part == "f_x2":
                    nth(dve, "f_rq", g, 3, 3)
                    dve.wait_ge(S["f_x2"], g + 1)
                    nc.vector.tensor_tensor(xf[:], x2[:], fq[:].unsqueeze(2).to_broadcast([P, 4, C]),
                                            ALU.mult).then_inc(S["f_xf"], 1)
                elif part == "f_xs":
                    nth(dve, "f_xf", g, 2, 1)
                    before(dve, "f_xst", g, 1)
                    nc.vector.tensor_copy(xs[:, :, 0, :], xf[:]).then_inc(S["f_xf"], 1)
                    nth(dve, "f_xf", g, 2, 2)
                    nc.vector.tensor_tensor(xs[:, :, 1, :], xf[:], xs[:, :, 0, :], ALU.subtract).then_inc(S["f_xs"], 1)
                elif part == "f_route":
                    dve.wait_ge(S["f_lg"], g + 1)
                    logits = pF[2][:, 0:4 * NE].rearrange("p (b e) -> p b e", b=4)
                    ct = Chain(dve, "dve_top", g, 21)
                    ct.link(nc.vector.tensor_reduce(l1["mx"][:], logits, AX, ALU.max))
                    nc.vector.tensor_tensor(lg["a"][:], logits, l1["mx"][:].unsqueeze(2).to_broadcast([P, 4, NE]),
                                            ALU.subtract).then_inc(S["f_la"], 1)
                elif part == "f_top":
                    top2(g, n)
                elif part == "f_h":
                    nth(dve, "f_sg", g, NT, n + 1)
                    nc.vector.tensor_tensor(hh[:, n, :], sg[n % 2][:], pF[2 * (n % 2) + 1][:],
                                            ALU.mult).then_inc(S["f_hh"], 1)
                elif part == "f_o":
                    nth(dve, "f_e", g, 4, n + 1)
                    nc.vector.tensor_tensor(oe[n % 2][:], pF[n][:].rearrange("p (e c) -> p e c", e=NE),
                                            lg["wt"][:, n, :].unsqueeze(2).to_broadcast([P, NE, C]),
                                            ALU.mult).then_inc(S["f_oe"], 1)
                    nth(dve, "f_oe", g, 4, n + 1)
                    nc.vector.tensor_reduce(osum[n % 2][:], oe[n % 2][:].rearrange("p e c -> p c e"),
                                            AX, ALU.add).then_inc(S["f_os"], 1)
                    nth(dve, "f_os", g, 4, n + 1)
                    if n == 0:
                        dve.wait_ge(S["f_res"], g + 1)
                        if not (isinstance(g, int) and g == 0):
                            dve.wait_ge(S["st_out"], g * 16)
                    nc.vector.tensor_tensor(fo[:, n, :], res[:, n, :], osum[n % 2][:], ALU.add).then_inc(S["f_out"], 1)

            def top2(g, half):
                ch = Chain(dve, "dve_top", g, 21)
                ch.n = (1, 10)[half]
                v = nc.vector

                def wide(x):
                    return x[:].unsqueeze(2).to_broadcast([P, 4, NE])

                rank = k("rank").unsqueeze(1).to_broadcast([P, 4, NE])

                def largest(probs, m, c, sel):
                    ch.link(v.tensor_reduce(l1[m][:], lg[probs][:], AX, ALU.max))
                    ch.link(v.tensor_tensor(lg["eq"][:], lg[probs][:], wide(l1[m]), ALU.is_equal))
                    ch.link(v.tensor_tensor(lg["c"][:], lg["eq"][:], rank, ALU.mult))
                    ch.link(v.tensor_reduce(l1[c][:], lg["c"][:], AX, ALU.max))
                    ch.link(v.tensor_tensor(lg[sel][:], lg["c"][:], wide(l1[c]), ALU.is_equal))

                if half == 0:
                    dve.wait_ge(S["f_le"], g + 1)
                    ch.link(v.tensor_reduce(l1["z"][:], lg["e"][:], AX, ALU.add))
                    ch.link(v.reciprocal(l1["rz"][:], l1["z"][:]))
                    ch.link(v.tensor_tensor(lg["p"][:], lg["e"][:], wide(l1["rz"]), ALU.mult))
                    largest("p", "m1", "c1", "s1")
                    ch.link(v.scalar_tensor_tensor(lg["p2"][:], lg["s1"][:], -2.0, lg["p"][:], ALU.mult, ALU.add))
                    assert ch.n == 10
                    return
                largest("p2", "m2", "c2", "s2")
                ch.step(v.tensor_tensor(lg["eq"][:], lg["s1"][:], lg["s2"][:], ALU.add))
                ch.link(v.tensor_tensor(l1["st"][:], l1["m1"][:], l1["m2"][:], ALU.add))
                ch.step(v.tensor_tensor(lg["tp"][:], lg["p"][:], lg["eq"][:], ALU.mult))
                ch.link(v.tensor_scalar(l1["de"][:], l1["st"][:], 1.0, TOP_EPS, ALU.mult, ALU.add))
                ch.link(v.reciprocal(l1["rd"][:], l1["de"][:]))
                ch.link(v.tensor_tensor(lg["wt"][:], lg["tp"][:], wide(l1["rd"]), ALU.mult))
                ch.end()

            sequence(do, dve)


def _block_rows(a, n):
    r, c = a.shape
    out = np.zeros((n * r, n * c), a.dtype)
    for i in range(n):
        out[i * r:(i + 1) * r, i * c:(i + 1) * c] = a
    return out


def _pack(cols, width, parts, dtype):
    out = np.zeros((P, width), dtype)
    for name, a in parts.items():
        lo, hi = cols[name]
        out[:a.shape[0], lo:hi] = a.reshape(a.shape[0], -1)
    return out


def _tokens(a):
    return a.reshape(4, 8, 2, T).transpose(0, 2, 1, 3).reshape(8, 1, 8 * T)


def _rope_rows(wm, perm):
    heads = wm.shape[0] // HD
    rows = np.zeros((NH, HP, C), wm.dtype)
    for h in range(NH):
        rows[h, :HD] = wm.reshape(heads, HD, C)[h * heads // NH][perm]
    return rows.reshape(P, C).T


def _weights(x):
    f = lambda n: np.asarray(x[n])
    col = lambda a, n: np.tile(a, n)[:, None]
    same, swap = np.arange(HD), (np.arange(HD) + HD // 2) % HD
    rope = np.zeros((2, C, 4, 2, P), np.float32)
    for m, (name, perm) in enumerate((("L0_ffn_wq", same), ("L0_ffn_wq", swap), ("L0_ffn_wk", same),
                                      ("L0_ffn_wk", swap))):
        for b in range(2):
            rope[b, :, m, b] = _rope_rows(f(name), perm)
    w2 = np.zeros((P, NT, 2, C), np.float32)
    for e in range(NE):
        for i in range(HID):
            n = e * HID + i
            w2[n % P, n // P, e - first_expert(n // P)] = f("L0_ffn_w2")[e, :, i]
    parts = {
        "qk": np.concatenate([_block_rows(f("L0_attn_Wq").T, 2), _block_rows(f("L0_attn_Wk").T, 2)], 1),
        "v": _block_rows(f("L0_attn_Wv").T, 2),
        "rope": rope.reshape(P, -1), "vf": _block_rows(f("L0_ffn_wv").T, 2), "wo": _block_rows(f("L0_ffn_wo").T, 2),
        "router": np.tile(f("L0_ffn_router_w").T, (2, 1)), "w2": w2,
        "w_mlp": col(f("L0_attn_w_mlp"), 4), "b_mlp": col(f("L0_attn_b_mlp"), P),
        "ln1": col(f("L0_ffn_ln1_w"), 2), "ln2": col(f("L0_ffn_ln2_w"), 2),
        "g1": col(f("L0_tok_g1"), 8), "b1": col(f("L0_tok_b1"), 8), "g2": col(f("L0_tok_g2"), 4),
        "b2": col(f("L0_tok_b2"), 4), "g3": np.tile(f("L0_tok_g3"), (P, 1)), "b3": np.tile(f("L0_tok_b3"), (P, 1)),
        "t1": np.tile(f("L0_tok_W1"), (8, 1)), "t2": np.tile(f("L0_tok_W2"), (8, 1)),
        "t3": np.tile(f("L0_tok_W3"), (4, 1)),
    }
    w13 = np.zeros((2, C, 2, NT * P), np.float32)
    w13[:, :, 0, :NE * HID] = f("L0_ffn_w1").reshape(NE * HID, C).T
    w13[:, :, 1, :NE * HID] = f("L0_ffn_w3").reshape(NE * HID, C).T
    return _pack(WCOL, WWIDTH, parts, np.float32), w13.reshape(P, -1)


def _constants():
    inv_freq = 1.0 / 10000.0 ** (np.arange(0, HD, 2, dtype=np.float32) / HD)
    freqs = np.outer(np.arange(T, dtype=np.float32), inv_freq)
    emb = np.concatenate([freqs, freqs], axis=-1)
    cos, sin = np.zeros((NH, HP, T), np.float32), np.zeros((NH, HP, T), np.float32)
    cos[:, :HD] = np.cos(emb).T
    sin[:, :HD] = np.sin(emb).T * np.where(np.arange(HD) < HD // 2, -1.0, 1.0)[:, None]
    q, key = np.arange(P)[:, None], np.arange(T)[None, :]
    sizes = np.array([160, 120, 2], np.float32)
    parts = {
        "ident": np.eye(P), "cos": cos.reshape(P, T), "sin": sin.reshape(P, T),
        "causal": np.where(key <= q, 0.0, BIG), "rank": np.tile(np.arange(NE, 0, -1), (P, 1)),
        "alpha": np.where(q < N_DVE, 1.0, 0.5), "scale": np.tile((2.0 / (sizes - 1))[:, None], (8, 1)),
        "bias": np.full((P, 1), -1.0), "m1": np.arange(P)[:, None] // 3 == np.arange(8),
        "m2": q // D1 == np.arange(8), "m3": q // D2 == np.arange(4), "eps": np.full((P, 1), LN_EPS),
        "ln_eps": np.full((P, 4), LN_EPS), "rms_eps": np.full((P, 4), RMS_EPS), "mean": np.full((P, 4), 1.0 / C),
    }
    half = {"ident": np.eye(P), "sign_rows": np.ones((P, 1)) * (key >= N_DVE), "ones": np.ones((P, P)),
            "bg": q // DG == np.arange(BG)}
    return _pack(KCOL, KWIDTH, parts, np.float32), _pack(HCOL, HWIDTH, half, np.float16)


def kernel(**inputs):
    import concourse.bacc as bacc
    from concourse.bass_utils import run_bass_kernel_spmd

    tok = [np.asarray(inputs[n]) for n in ("x", "itok_BS_0_479", "mask_BS_i1_0")]
    valid = np.asarray(inputs["mask_BS_b1_0"]).view(np.uint8)
    wts, w13 = _weights(inputs)
    kf, kh = _constants()
    arrays = {
        "coords": np.concatenate([_tokens(a) for a in tok], 1).reshape(24, 8 * T),
        "valid": np.concatenate([_tokens(valid)] * 3, 1).reshape(24, 8 * T),
        "wts": wts, "w13": w13, "kf": kf, "kh": kh,
    }
    nc = bacc.Bacc("TRN2", target_bir_lowering=False, num_devices=1)
    args = [nc.dram_tensor(n, a.shape, mybir.dt.from_np(a.dtype), kind="ExternalInput").ap()
            for n, a in arrays.items()]
    args.append(nc.dram_tensor("out", (GROUPS, 4, T, C), F32, kind="ExternalOutput").ap())
    tower(nc, *args)
    r = run_bass_kernel_spmd(nc, [arrays], core_ids=[0])
    return r.results[0]["out"].reshape(B, T, C)
```

```python
from contextlib import ExitStack

import numpy as np

import concourse.bass as bass
from concourse import mybir

ALU = mybir.AluOpType
ACT = mybir.ActivationFunctionType
AX = mybir.AxisListType.X
F32 = mybir.dt.float32
F16 = mybir.dt.float16
BF16 = mybir.dt.bfloat16
I32 = mybir.dt.int32
U8 = mybir.dt.uint8

P = 128
B, T, C = 64, 128, 64
PAIRS, GROUPS = B // 2, B // 4
G2, DG = 2, 32
BG = 4
D1, D2 = 16, 32
NH, NKV, HD = 4, 2, 16
HP = 32
NE, HID = 8, 170
NT = -(-NE * HID // P)
BIG = -1e30
LN_EPS, RMS_EPS, TOP_EPS = 1e-5, 1e-6, 1e-9

CH = 8
CV = 8
N_DVE = 64
N_POOL = 48
N_ACT = T - N_DVE - N_POOL
NP = N_POOL // CH
ND = 3

VW = DG + 1
KW = HD + 1


ORDER = {
    "tensor": (
        """f_tr f_v f_q f_k sum2.0 sum2.1 sum1.0 f_sc.0 f_sc.1 f_sc.2 sum1.1 f_turn.0 f_sc.3 f_val.0 soft_t f_turn.1
           f_turn.2 f_turn.3 f_val.1 f_val.2 f_val.3 f_yt soft_pt f_wo front_norm soft_pv front_mm""".split(),
        """sum2.0 f_xs sum2.1 f_route f_h.0 f_h.1 sum1.0 f_h.2 f_h.3 f_h.4 sum1.1 front_norm f_h.5 f_h.6 f_h.7 f_h.8
           f_h.9 f_h.10 soft_t f_e.0 f_e.1 soft_pt soft_pv f_e.2 front_mm f_e.3""".split(),
    ),
    "scalar": (
        """ptr.0 ptr.1 sgn.0 sgn.1 sgn.2 f_exp.0 ptr.2 f_exp.1 f_turn.0 sgn.3 f_exp.2 f_exp.3 f_turn.1 f_turn.2
           soft_m f_turn.3 soft_e sgn.4 f_yt soft_pt ptr.3 front_norm f_rms sgn.5 front_mm front_split""".split(),
        """ptr.0 sgn.0 f_xs sgn.1 f_route f_h.0 f_h.1 f_h.2 sgn.2 f_h.3 ptr.1 f_h.4 f_h.5 f_h.6 f_h.7 front_norm
           f_h.8 ptr.2 f_h.9 f_h.10 soft_m soft_e soft_pt sgn.3 front_mm front_split sgn.4 f_tr+ f_v+ ptr.3 sgn.5""".split(),
    ),
    "gpsimd": (
        """dif.0 f_ke dif.1 dif.2 dif.3 dif.4 dif.5 front_stat""".split(),
        """f_rms dif.0 dif.1 front_stat dif.2 dif.3 dif.4 dif.5 f_s.0 f_stat+ f_norm+ f_s.1""".split(),
    ),
    "vector": (
        """f_rotk red2.0 f_qe f_ke cmp.0 cmp.1 f_max.0 red2.1 red1.0 cmp.2 f_max.1 f_max.2 cmp.3 f_max.3 red1.1
           front_stat f_weigh.0 soft_m front_norm f_weigh.1 cmp.4 f_weigh.2 f_weigh.3 cmp.5 f_wo cmp.6 cmp.7 pair_add
           f_x2 f_xs front_split""".split(),
        """red2.0 front_stat f_route red2.1 f_top.0 f_h.0 cmp.0 f_h.1 f_h.2 red1.0 cmp.1 front_norm f_h.3 f_h.4 cmp.2
           f_h.5 f_h.6 red1.1 f_h.7 f_h.8 cmp.3 f_h.9 f_h.10 soft_m f_top.1 f_o.0 f_o.1 cmp.4 cmp.5 pair_add f_stat+
           cmp.6 f_norm+ f_o.2 cmp.7 f_o.3 front_split f_rotq+""".split(),
    ),
}


def columns(parts):
    at, out = 0, {}
    for name, width in parts:
        out[name] = (at, at + width)
        at += width
    return out, at


WCOL, WWIDTH = columns([
    ("qk", 256), ("v", 128), ("rope", 1024), ("vf", 64), ("wo", 128), ("router", NE),
    ("w2", NT * P), ("w_mlp", 1), ("b_mlp", 1), ("ln1", 1), ("ln2", 1), ("g1", 1), ("b1", 1),
    ("g2", 1), ("b2", 1), ("g3", C), ("b3", C), ("t1", D1), ("t2", D2), ("t3", C)])
KCOL, KWIDTH = columns([
    ("ident", 128), ("cos", 128), ("sin", 128), ("causal", 128), ("rank", NE), ("alpha", 1),
    ("scale", 1), ("bias", 1), ("m1", 8), ("m2", 8), ("m3", 4), ("eps", 1),
    ("ln_eps", 4), ("rms_eps", 4)])
HCOL, HWIDTH = columns([("ident", 128), ("sign_rows", 128), ("ones", 128), ("bg", BG)])


def first_expert(t):
    return min(P * t // HID, NE - 2)


def tower(nc, coords, valid, wts, w13, kf, kh, out):
    with ExitStack() as ctx:
        def sb(name, shape, dt=F32):
            return ctx.enter_context(nc.sbuf_tensor(name, shape, dt))

        def ps(name, shape, dt=F32):
            return ctx.enter_context(nc.psum_tensor(name, shape, dt))

        def sem(name):
            return ctx.enter_context(nc.semaphore(name))

        h0_dram = nc.dram_tensor("h0_scratch", (PAIRS, T, 2 * C), F32).ap()

        W = sb("W", [P, WWIDTH])
        K = sb("K", [P, KWIDTH])
        H = sb("H", [P, HWIDTH], F16)

        def w(name):
            return W[:, WCOL[name][0]:WCOL[name][1]]

        def k(name):
            return K[:, KCOL[name][0]:KCOL[name][1]]

        def hc(name):
            return H[:, HCOL[name][0]:HCOL[name][1]]

        w1h, w1l = sb("w1h", [P, NT, P], F16), sb("w1l", [P, NT, P], F16)
        w3h, w3l = sb("w3h", [P, NT, P], F16), sb("w3l", [P, NT, P], F16)
        wrh, wrl = sb("wrh", [P, NE], F16), sb("wrl", [P, NE], F16)
        maskb, identb = sb("maskb", [P, T], BF16), sb("identb", [P, P], BF16)
        half = sb("half", [P, 4])
        ind = [sb(f"ind{s}", [P, T, T], F16) for s in range(2)]
        dif = [sb(f"dif{s}", [P, CH, T]) for s in range(ND)]
        hin = [sb(f"hin{s}", [P, 2, C]) for s in range(2)]
        h1 = sb("h1", [P, 4, C])
        stat = sb("stat", [P, 2, 6])
        mv = sb("mv", [P, 2, 2])
        ve = sb("ve", [P, 2])
        rstd = sb("rstd", [P, 2])
        xn = sb("xn", [P, 2, C])
        xT = sb("xT", [P, T])
        qk = [sb(f"qk{s}", [P, 2, T]) for s in range(2)]
        bd = [sb(f"bd{s}", [P, 2, T, 2, BG], F16) for s in range(2)]
        va = [sb(f"va{s}", [P, 2, G2, VW]) for s in range(2)]
        t2s = sb("t2s", [P, BG, T])
        t1s = sb("t1s", [P, BG, T])
        raw = sb("raw", [P, BG, T])
        att = sb("att", [P, BG, T])
        attT = sb("attT", [P, BG, T])
        mx = sb("mx", [P, BG])
        mb = sb("mb", [P, BG])
        nm = sb("nm", [P, BG])
        rden = sb("rden", [P, BG])
        add = sb("add", [P, 2, C])
        fstat = sb("fstat", [P, 4, 6])
        fmv = sb("fmv", [P, 4, 2])
        fv = sb("fv", [P, 4])
        fr = sb("fr", [P, 4])
        fu = sb("fu", [P, 4])
        fq = sb("fq", [P, 4])
        fm = sb("fm", [P, 4])
        pause = sb("pause", [P, 1])
        pause_p = sb("pause_p", [P, 1])
        frr = sb("frr", [P, 4])
        fx = sb("fx", [P, 4, C])
        fxr = sb("fxr", [P, 4, C])
        rx = sb("rx", [P, 4, C])
        res = sb("res", [P, 4, C])
        fxT = sb("fxT", [P, 2, T])
        vf = sb("vf", [P, 4, NKV, KW])
        r1, r2 = sb("r1", [P, 4, T]), sb("r2", [P, 4, T])
        r3, r4 = sb("r3", [P, 4, T]), sb("r4", [P, 4, T])
        qe = sb("qe", [P, 4, T])
        ke = sb("ke", [P, 4, NH, T])
        fmx = [sb(f"fmx{s}", [P, NH]) for s in range(4)]
        fnm = [sb(f"fnm{s}", [P, NH]) for s in range(4)]
        fp = [sb(f"fp{s}", [P, NH, T]) for s in range(4)]
        fpT = [r1, r2, r3, r4]
        frd = [sb(f"frd{s}", [P, NH]) for s in range(4)]
        y = sb("y", [P, 4, C])
        yT = sb("yT", [P, 2, T])
        x2 = sb("x2", [P, 4, C])
        ms = sb("ms", [P, 4])
        xf = x2
        xs = sb("xs", [P, 4, 2, C], F16)
        xsT = sb("xsT", [P, 4 * T], F16)
        lg = {n: sb("lg_" + n, [P, 4, NE]) for n in ("a", "e", "p", "eq", "c", "s1", "p2", "s2", "tp", "wt")}
        l1 = {n: sb("l1_" + n, [P, 4]) for n in ("mx", "z", "rz", "m1", "c1", "m2", "c2", "st", "de", "rd")}
        sg = [sb(f"sg{s}", [P, 512]) for s in range(2)]
        hh = sb("hh", [P, NT, 512])
        oe = [sb(f"oe{s}", [P, 2, NE, C]) for s in range(2)]
        o4, o2, o1 = sb("o4", [P, 2, 4, C]), sb("o2", [P, 2, 2, C]), sb("o1", [P, 2, C])
        fo = sb("fo", [P, 4, C])

        pT = ps("pT", [P, 1024])
        pA = ps("pA", [P, 512])
        pS = ps("pS", [P, 512])
        pF = [ps(f"pF{s}", [P, 512]) for s in range(4)]

        craw = ind[0][:, 0:16, :].rearrange("p a b -> p (a b)").bitcast(I32)
        vraw = ind[0][:, 16:20, :].rearrange("p a b -> p (a b)").bitcast(U8)
        cf = ind[0][:, 20:36, :].rearrange("p a b -> p (a b)").bitcast(F32)
        cT = ind[0][:, 36:52, :].rearrange("p a b -> p (a b)").bitcast(F32)
        h1T = ind[0][:, 52:68, :].rearrange("p a b -> p (a b)").bitcast(F32)
        w1bd = ind[0][:, 68:70, :].rearrange("p a b -> p (a b)").bitcast(F32)
        w2bd = ind[0][:, 70:74, :].rearrange("p a b -> p (a b)").bitcast(F32)
        w3bd = ind[0][:, 74:78, :].rearrange("p a b -> p (a b)").bitcast(F32)
        h2T = ind[1][:, 0:32, :].rearrange("p a b -> p (a b)").bitcast(F32)
        sq = [ind[1][:, 32 + 8 * i:40 + 8 * i, :].rearrange("p a b -> p (a b)").bitcast(F32) for i in range(2)]
        zn = [ind[1][:, 48 + 8 * i:56 + 8 * i, :].rearrange("p a b -> p (a b)").bitcast(F32) for i in range(2)]
        h3g = [ind[1][:, 64 + 8 * i:72 + 8 * i, :].rearrange("p a b -> p (a b)").bitcast(F32) for i in range(2)]
        h3o = [ind[1][:, 80 + 8 * i:88 + 8 * i, :].rearrange("p a b -> p (a b)").bitcast(F32) for i in range(2)]
        w13raw = hh[:, 0:6, :].rearrange("p a b -> p (a b)")
        pms = [sb(f"pms{i}", [P, 32]) for i in range(2)]
        psd = [sb(f"psd{i}", [P, 32]) for i in range(2)]
        prs = [sb(f"prs{i}", [P, 32]) for i in range(2)]
        wm = sb("wm", [P, 3])
        wn = sb("wn", [P, 3])
        wc = sb("wc", [P, D1 + D2 + C])

        names = """ld_w ld_e ld_h ld_w13 ld_k ld_c dve_pro pool_pro w_split wbd_ready c_ready
            w_ln z_mm z_sq z_ms z_sd z_rs z_zn z_tr z_hT z_gb0 z_gb1 dve_gb z_st0 z_st1
            ld_a0 ld_a1 ld_r0 ld_r1 a_mv a_rstd a_xn a_tr a_xT a_mm a_qk a_v a_hi a_bd
            i_dve i_ptr i_dif i_sgn t2_mm t1_mm t2_s t1_s s_tp s_raw s_m s_p s_pt s_ptT s_pv s_h1
            dve_front dve_soft dve_value pool_a act_s
            dve_rope dve_top f_res f_xf f_rd pool_x pool_o pool_done f_ve f_mv f_r f_x f_xo f_tr f_xT f_v f_va f_q f_qrope f_qe f_k f_krope f_ke f_kep
            f_sc f_max f_nm f_p f_pt f_ptT f_pv f_y f_yt f_yT f_wo f_x2 f_ms f_rq f_xs f_xst f_xsT
            f_lg f_la f_le f_h13 f_sg f_hh f_e f_oe f_out st_out""".split()
        S = {n: sem(n) for n in names}
        block = ctx.enter_context(nc.Block())

        class Chain:

            def __init__(self, eng, name, idx, per):
                self.eng, self.sem, self.idx, self.per, self.n = eng, S[name], idx, per, 0

            def step(self, ins):
                self.n += 1
                return ins.then_inc(self.sem, 1)

            def wait(self):
                self.eng.wait_ge(self.sem, self.idx * self.per + self.n)

            def link(self, ins):
                self.step(ins)
                self.wait()

            def end(self):
                assert self.n == self.per, (self.sem, self.n)

        def nth(eng, name, idx, per, n):
            eng.wait_ge(S[name], idx * per + n)

        def before(eng, name, idx, per, back=1):
            if isinstance(idx, int) and idx < back:
                return
            eng.wait_ge(S[name], idx * per + per - back * per)

        def freed(engine, p, n):
            if isinstance(p, int) and p < 2 and n == 0:
                engine.wait_ge(S["z_mm"], 14)
                if p == 1:
                    engine.wait_ge(S["z_st0"], 16 * 4)
                    engine.wait_ge(S["z_st1"], 16 * 4)

        def difs(s, c):
            return dif[c % ND]

        def sequence(do, engine, order):
            def piece(item):
                kind, *n = item.rstrip("+").split(".")
                return kind, int(n[0]) if n else 0, item.endswith("+")

            def every():
                kinds = (("cmp", N_DVE // CV, 0), ("ptr", N_ACT // 4, 0), ("dif", NP, 0), ("sgn", NP, 2))
                return [(kind, t - late) for t in range(max(N_DVE // CV, NP + 2)) for kind, count, late in kinds
                        if 0 <= t - late < count]

            for kind, n in every():
                do(kind, 0, 0, 0, n)
            do("front_split", 1, 1, 0, 0)

            def group(j, first, last):
                for s in range(2):
                    p = 2 * j + s
                    for item in order[s]:
                        kind, n, own = piece(item)
                        if kind in ("cmp", "ptr", "dif", "sgn"):
                            if not (last and s == 1):
                                do(kind, p + 1, 1 - s, j + s, n)
                        elif kind.startswith("front"):
                            if not last:
                                do(kind, p + 2, s, j + 1, n)
                        elif own:
                            do(kind, None, None, j, n)
                        elif kind.startswith("f_"):
                            if not first:
                                do(kind, None, None, j - 1, n)
                        else:
                            do(kind, p, s, j, n)

            group(0, True, False)
            group(1, False, False)
            with engine.Fori(2, GROUPS - 1) as j:
                group(j, False, False)
            group(GROUPS - 1, False, True)
            for s in range(2):
                for item in order[s]:
                    kind, n, own = piece(item)
                    if kind.startswith("f_") and not own:
                        do(kind, None, None, GROUPS - 1, n)

        @block.sync
        def _(sp):
            sp.dma_start(craw[0:24, :], coords).then_inc(S["ld_c"], 16)
            sp.dma_start(vraw[0:24, :], valid).then_inc(S["ld_c"], 16)
            sp.dma_start(K[:], kf).then_inc(S["ld_k"], 16)
            small = WCOL["w_mlp"][0]
            sp.dma_start(W[:, small:], wts[:, small:]).then_inc(S["ld_e"], 16)
            sp.dma_start(W[:, 0:small], wts[:, 0:small]).then_inc(S["ld_w"], 16)
            sp.dma_start(H[:], kh).then_inc(S["ld_h"], 16)
            sp.dma_start(w13raw[:, 0:2 * NT * P], w13).then_inc(S["ld_w13"], 16)
            def chunk(i):
                sp.wait_ge(S[f"z_gb{i % 2}"], i // 2 + 1)
                sp.dma_start(h0_dram.rearrange("(m i) t c -> i t m c", i=8)[i],
                             h3o[i % 2][:, 0:512].rearrange("p (m c) -> p m c", m=4)).then_inc(S[f"z_st{i % 2}"], 16)

            def load(p, s):
                sp.wait_ge(S[f"z_st{p}"], 16)
                sp.dma_start(hin[s][:], h0_dram[p].rearrange("t (b c) -> t b c", b=2)).then_inc(S[f"ld_a{s}"], 16)
                sp.dma_start(h1[:, 2 * s:2 * s + 2, :],
                             h0_dram[p].rearrange("t (b c) -> t b c", b=2)).then_inc(S[f"ld_r{s}"], 16)

            def store(g):
                nth(sp, "f_out", g, 2, 2)
                sp.dma_start(out[g].rearrange("b t c -> t b c"), fo[:]).then_inc(S["st_out"], 16)

            chunk(0)
            chunk(1)
            load(0, 0)
            load(1, 1)
            for i in range(2, 8):
                chunk(i)
            sp.wait_ge(S["z_st0"], 16 * 4)
            sp.wait_ge(S["z_st1"], 16 * 4)

            def residual(p, s, g):
                before(sp, "f_xo", g, 1, 1)
                before(sp, "f_x", g, 1, 1)
                sp.dma_start(h1[:, 2 * s:2 * s + 2, :],
                             h0_dram[p].rearrange("t (b c) -> t b c", b=2)).then_inc(S[f"ld_r{s}"], 16)

            def normed(p, s):
                before(sp, "a_xn", p, 1, 2)
                sp.dma_start(hin[s][:], h0_dram[p].rearrange("t (b c) -> t b c", b=2)).then_inc(S[f"ld_a{s}"], 16)

            normed(2, 0)
            normed(3, 1)

            def group(j):
                residual(2 * j, 0, j)
                residual(2 * j + 1, 1, j)
                normed(2 * j + 2, 0)
                normed(2 * j + 3, 1)
                store(j - 1)

            group(1)
            with sp.Fori(2, GROUPS - 1) as j:
                group(j)
            residual(PAIRS - 2, 0, GROUPS - 1)
            residual(PAIRS - 1, 1, GROUPS - 1)
            store(GROUPS - 2)
            store(GROUPS - 1)
            sp.wait_ge(S["st_out"], 16 * GROUPS)

        @block.tensor
        def _(pe):
            zbank = [pT[:, 0:512], pT[:, 512:1024], pF[0][:], pF[1][:]]
            tbank = [pA, pS]

            def mm(u):
                z = zbank[u % 4]
                if u >= 4:
                    pe.wait_ge(S["z_zn"], u - 3)
                if u < 2:
                    pe.wait_ge(S["c_ready"], 1)
                    pe.wait_ge(S["wbd_ready"], 1)
                    for c in range(4):
                        i = 4 * u + c
                        last = nc.tensor.matmul(z[:, 128 * c:128 * c + 128], cT[0:24, 128 * i:128 * i + 128],
                                                w1bd[0:24, :], start=True, stop=True)
                elif u < 6:
                    v = u - 2
                    pe.wait_ge(S["z_hT"], v // 2 + 1)
                    for c in range(2):
                        i = 2 * v + c
                        last = nc.tensor.matmul(z[:, 256 * c:256 * c + 256], h1T[:, 128 * i:128 * i + 128],
                                                w2bd[:, :], start=True, stop=True)
                else:
                    i = u - 6
                    pe.wait_ge(S["z_hT"], 2 + i // 2 + 1)
                    for hf in range(2):
                        last = nc.tensor.matmul(z[:, 256 * hf:256 * hf + 256],
                                                h2T[:, 1024 * hf + 128 * i:1024 * hf + 128 * i + 128],
                                                w3bd[:, :], start=True, stop=True)
                last.then_inc(S["z_mm"], 1)

            def tr(u):
                pe.wait_ge(S["z_zn"], u + 1)
                if u >= 2:
                    pe.wait_ge(S["z_hT"], u - 1)
                for c in range(4):
                    last = nc.tensor.transpose(tbank[u % 2][:, 128 * c:128 * c + 128],
                                               zn[u % 2][:, 128 * c:128 * c + 128], k("ident"))
                last.then_inc(S["z_tr"], 1)

            pe.wait_ge(S["ld_k"], 16)
            mm(0)
            mm(1)
            tr(0)
            mm(2)
            mm(3)
            tr(1)
            mm(4)
            mm(5)
            tr(2)
            mm(6)
            mm(7)
            tr(3)
            mm(8)
            mm(9)
            tr(4)
            tr(5)

            ropew = w("rope").rearrange("p (m b o) -> p m b o", m=4, b=2)

            def project(m, bank):
                dst = bank[:].rearrange("p (i b t) -> p b i t", i=2, b=2)
                for b in range(2):
                    last = nc.tensor.matmul(dst[:, b, :, :], ropew[:, m, b, :], fxT[:, :, :], start=True, stop=True)
                return last

            def do(part, p, s, g, n):
                if part == "front_norm":
                    pe.wait_ge(S["a_xn"], p + 1)
                    before(pe, "a_qk", p, 1)
                    before(pe, "a_v", p, 1)
                    nc.tensor.transpose(pA[:, 384:512], xn[:].rearrange("p b c -> p (b c)"),
                                        k("ident")).then_inc(S["a_tr"], 1)
                elif part == "front_mm":
                    pe.wait_ge(S["a_xT"], p + 1)
                    nc.tensor.matmul(pA[:, 0:128], w("qk")[:, 0:128], xT[:], start=True, stop=True)
                    nc.tensor.matmul(pA[:, 128:256], w("qk")[:, 128:256], xT[:], start=True, stop=True)
                    nc.tensor.matmul(pA[:, 256:384], xT[:], w("v"), start=True, stop=True).then_inc(S["a_mm"], 1)
                elif part == "sum2":
                    if n == 0:
                        pe.wait_ge(S["i_dve"], p + 1)
                        pe.wait_ge(S["i_ptr"], p + 1)
                        nth(pe, "i_sgn", p, NP, NP)
                        pe.wait_ge(S["a_bd"], p + 1)
                    if not (isinstance(p, int) and p == 0):
                        pe.wait_ge(S["t1_s"], 2 * p - 1 + n)
                    col, tok = 512 * n, T // 2 * n
                    nc.tensor.matmul(pT[:, col:col + 512], hc("sign_rows"),
                                     bd[s][:, 1, tok:tok + T // 2, :, :].rearrange("p a b c -> p (a b c)"),
                                     start=True, stop=False)
                    for i in range(T // 2):
                        last = nc.tensor.matmul(
                            pT[:, col + 8 * i:col + 8 * i + 8], ind[s][:, :, tok + i],
                            bd[s][:, 1, tok + i, :, :].rearrange("p b c -> p (b c)"),
                            start=False, stop=i == T // 2 - 1)
                    last.then_inc(S["t2_mm"], 1)
                elif part == "sum1":
                    nth(pe, "t2_s", p, 2, n + 1)
                    col, tok = 512 * n, T // 2 * n
                    signs = max(tok, N_DVE)
                    for i in range(T // 2):
                        sign = tok + i >= signs
                        if tok + i == signs:
                            nc.tensor.matmul(pT[:, col + 8 * i:col + 512], hc("ones"),
                                             bd[s][:, 0, signs:tok + T // 2, :, :].rearrange("p a b c -> p (a b c)"),
                                             start=True, stop=False)
                        last = nc.tensor.matmul(
                            pT[:, col + 8 * i:col + 8 * i + 8], ind[s][:, tok + i, :],
                            bd[s][:, 0, tok + i, :, :].rearrange("p b c -> p (b c)"),
                            start=not sign, stop=not sign or i == T // 2 - 1)
                    last.then_inc(S["t1_mm"], 1)
                elif part == "soft_t":
                    nth(pe, "t1_s", p, 2, 2)
                    before(pe, "s_h1", p, 1)
                    for b in range(BG):
                        last = nc.tensor.transpose(pS[:, 128 * b:128 * b + 128], t1s[:, b, :], k("ident"))
                    last.then_inc(S["s_tp"], 1)
                elif part == "soft_pt":
                    pe.wait_ge(S["s_p"], p + 1)
                    pe.wait_ge(S["s_raw"], p + 1)
                    for b in range(BG):
                        last = nc.tensor.transpose(pS[:, 128 * b:128 * b + 128], att[:, b, :], k("ident"))
                    last.then_inc(S["s_pt"], 1)
                elif part == "soft_pv":
                    pe.wait_ge(S["s_ptT"], p + 1)
                    for b in range(BG):
                        last = nc.tensor.matmul(pS[:, VW * b:VW * b + VW], attT[:, b, :],
                                                va[s][:, b // G2, b % G2, :], start=True, stop=True)
                    last.then_inc(S["s_pv"], 1)
                elif part == "f_tr":
                    pe.wait_ge(S["f_x"], g + 1)
                    for i in range(2):
                        last = nc.tensor.transpose(pF[2][:, 128 * i:128 * i + 128],
                                                   fxr[:, 2 * i:2 * i + 2, :].rearrange("p b c -> p (b c)"),
                                                   k("ident"))
                    last.then_inc(S["f_tr"], 1)
                elif part == "f_v":
                    pe.wait_ge(S["f_xT"], g + 1)
                    for i in range(2):
                        last = nc.tensor.matmul(pF[2][:, 256 + 64 * i:320 + 64 * i], fxT[:, i, :], w("vf"),
                                                start=True, stop=True)
                    last.then_inc(S["f_v"], 1)
                elif part == "f_q":
                    project(0, pF[3])
                    pe.wait_ge(S["f_va"], g + 1)
                    project(1, pF[2]).then_inc(S["f_q"], 1)
                elif part == "f_k":
                    before(pe, "f_oe", g, 4)
                    project(2, pF[0])
                    project(3, pF[1]).then_inc(S["f_k"], 1)
                elif part == "f_sc":
                    if n == 0:
                        pe.wait_ge(S["f_qe"], g + 1)
                        pe.wait_ge(S["f_ke"], g + 1)
                        pe.wait_ge(S["f_kep"], g + 1)
                        pe.wait_ge(S["f_krope"], g + 1)
                    nc.tensor.matmul(pF[n][:], qe[:, n, :], ke[:, n, :, :].rearrange("p h t -> p (h t)"),
                                     start=True, stop=False)
                    nc.tensor.matmul(pF[n][:], identb[:], maskb[:].unsqueeze(1).to_broadcast([P, NH, T]),
                                     start=False, stop=True).then_inc(S["f_sc"], 1)
                elif part == "f_turn":
                    nth(pe, "f_p", g, 4, n + 1)
                    for h in range(NH):
                        last = nc.tensor.transpose(pF[n][:, 128 * h:128 * h + 128], fp[n][:, h, :], k("ident"))
                    last.then_inc(S["f_pt"], 1)
                elif part == "f_val":
                    nth(pe, "f_ptT", g, 4, n + 1)
                    for h in range(NH):
                        last = nc.tensor.matmul(pF[n][:, KW * h:KW * h + KW], fpT[n][:, h, :],
                                                vf[:, n, h * NKV // NH, :], start=True, stop=True)
                    last.then_inc(S["f_pv"], 1)
                elif part == "f_yt":
                    nth(pe, "f_y", g, 4, 4)
                    for i in range(2):
                        last = nc.tensor.transpose(pF[0][:, 128 * i:128 * i + 128],
                                                   y[:, 2 * i:2 * i + 2, :].rearrange("p b c -> p (b c)"), k("ident"))
                    last.then_inc(S["f_yt"], 1)
                elif part == "f_wo":
                    pe.wait_ge(S["f_yT"], g + 1)
                    for i in range(2):
                        last = nc.tensor.matmul(pF[0][:, 256 + 128 * i:384 + 128 * i], yT[:, i, :], w("wo"),
                                                start=True, stop=True)
                    last.then_inc(S["f_wo"], 1)
                elif part == "f_xs":
                    pe.wait_ge(S["f_xs"], g + 1)
                    for b in range(4):
                        last = nc.tensor.transpose(pF[1][:].bitcast(F16)[:, 128 * b:128 * b + 128],
                                                   xs[:, b, :, :].rearrange("p a c -> p (a c)"), hc("ident"))
                    last.then_inc(S["f_xst"], 1)
                elif part == "f_route":
                    pe.wait_ge(S["f_xsT"], g + 1)
                    for b in range(4):
                        dst = pF[2][:, NE * b:NE * b + NE]
                        nc.tensor.matmul(dst, xsT[:, 128 * b:128 * b + 128], wrh[:], start=True, stop=False)
                        last = nc.tensor.matmul(dst, xsT[:, 128 * b:128 * b + 128], wrl[:], start=False, stop=True)
                    last.then_inc(S["f_lg"], 1)
                elif part == "f_h":
                    one, three = pF[2 * (n % 2)], pF[2 * (n % 2) + 1]
                    if n == 1:
                        pe.wait_ge(S["f_la"], g + 1)
                    if n >= 2:
                        nth(pe, "f_sg", g, NT, n - 1)
                    nc.tensor.matmul(one[:], w1h[:, n, :], xsT[:], start=True, stop=False)
                    nc.tensor.matmul(one[:], w1l[:, n, :], xsT[:], start=False, stop=True)
                    if n >= 2:
                        nth(pe, "f_hh", g, NT, n - 1)
                    nc.tensor.matmul(three[:], w3h[:, n, :], xsT[:], start=True, stop=False)
                    nc.tensor.matmul(three[:], w3l[:, n, :], xsT[:], start=False, stop=True).then_inc(S["f_h13"], 1)
                elif part == "f_e":
                    if n == 0:
                        nth(pe, "f_hh", g, NT, NT)
                    elif n >= 2:
                        nth(pe, "f_oe", g, 4, n - 1)
                    for t in range(NT):
                        e0 = first_expert(t)
                        last = nc.tensor.matmul(pF[n % 2][:, C * e0:C * e0 + 2 * C],
                                                hh[:, t, 128 * n:128 * n + 128],
                                                w("w2")[:, P * t:P * t + P], start=t == 0, stop=t == NT - 1,
                                                skip_group_check=True)
                    last.then_inc(S["f_e"], 1)

            for u in range(10, 14):
                mm(u)
            pe.wait_ge(S["ld_w"], 16)
            pe.wait_ge(S["ld_h"], 16)
            for p in range(2):
                do("front_norm", p, p, 0, 0)
                do("front_mm", p, p, 0, 0)
            pe.wait_ge(S["w_split"], 1)
            sequence(do, pe, ORDER["tensor"])

        @block.scalar
        def _(act):
            zbank = [pT[:, 0:512], pT[:, 512:1024], pF[0][:], pF[1][:]]
            tbank = [pA, pS]

            def square(u):
                act.wait_ge(S["z_mm"], u + 1)
                if u >= 2:
                    act.wait_ge(S["z_ms"], u - 1)
                nc.scalar.activation(sq[u % 2][:, 0:512], zbank[u % 4], ACT.Square).then_inc(S["z_sq"], 1)

            def root(u):
                width = D1 if u < 2 else D2 if u < 6 else C
                act.wait_ge(S["z_ms"], u + 1)
                if u >= 2:
                    act.wait_ge(S["z_zn"], u - 1)
                nc.scalar.activation(psd[u % 2][:, 0:512 // width], pms[u % 2][:, 0:512 // width], ACT.Sqrt,
                                     bias=k("eps"), scale=1.0 / width).then_inc(S["z_sd"], 1)

            def evac(u):
                act.wait_ge(S["z_tr"], u + 1)
                if u < 2:
                    nc.scalar.activation(h1T[:, 512 * u:512 * u + 512], tbank[u % 2][:], ACT.Relu,
                                         bias=w("b1"), scale=w("g1")).then_inc(S["z_hT"], 1)
                else:
                    v = u - 2
                    dst = h2T[:, :].rearrange("p (h i t) -> p i h t", h=2, t=T)[:, 2 * v:2 * v + 2, :, :]
                    nc.scalar.activation(dst, tbank[u % 2][:].rearrange("p (i h t) -> p i h t", i=2, h=2), ACT.Relu,
                                         bias=w("b2"), scale=w("g2")).then_inc(S["z_hT"], 1)

            act.wait_ge(S["ld_e"], 16)
            act.wait_ge(S["ld_k"], 16)
            square(0)
            square(1)
            root(0)
            root(1)
            evac(0)
            square(2)
            square(3)
            evac(1)
            root(2)
            root(3)
            square(4)
            square(5)
            evac(2)
            root(4)
            root(5)
            square(6)
            square(7)
            evac(3)
            root(6)
            root(7)
            square(8)
            square(9)
            evac(4)
            root(8)
            root(9)
            square(10)
            square(11)
            evac(5)
            root(10)
            root(11)
            square(12)
            square(13)
            root(12)
            root(13)
            act.wait_ge(S["pool_pro"], 1)

            def do(part, p, s, g, n):
                if part == "front_norm":
                    act.wait_ge(S["a_tr"], p + 1)
                    nc.scalar.activation(xT[:], pA[:, 384:512], ACT.Copy).then_inc(S["a_xT"], 1)
                elif part == "front_mm":
                    act.wait_ge(S["a_mm"], p + 1)
                    before(act, "i_dve", p, 1, 2)
                    before(act, "i_ptr", p, 1, 2)
                    before(act, "i_sgn", p, NP, 2)
                    nc.scalar.activation(qk[s][:].rearrange("p a t -> p (a t)"), pA[:, 0:256],
                                         ACT.Copy).then_inc(S["a_qk"], 1)
                    before(act, "s_pv", p, 1, 2)
                    nc.scalar.activation(va[s][:, :, :, 0:DG], pA[:, 256:384].rearrange(
                        "p (b d g) -> p b g d", b=2, g=G2), ACT.Copy).then_inc(S["a_v"], 1)
                elif part == "front_split":
                    act.wait_ge(S["a_qk"], p + 1)
                    before(act, "t1_mm", p, 2, 2)
                    for b in range(BG):
                        rows = slice(DG * b, DG * b + DG)
                        last = nc.scalar.activation(bd[s][rows, :, :, 0, b], qk[s][rows], ACT.Identity,
                                                    scale=w("w_mlp")[rows])
                    last.then_inc(S["a_hi"], 1)
                elif part == "ptr":
                    if n == 0:
                        before(act, "t1_mm", p, 2, 2)
                        freed(act, p, n)
                        act.wait_ge(S["a_qk"], p + 1)
                    for i in range(4):
                        q = N_DVE + N_POOL + 4 * n + i
                        ins = nc.scalar.activation(ind[s][:, q, :], qk[s][:, 1, :], ACT.Sign,
                                                   bias=qk[s][:, 0, q:q + 1], scale=-1.0)
                    if n == N_ACT // 4 - 1:
                        ins.then_inc(S["i_ptr"], 1)
                elif part == "sgn":
                    before(act, "t1_mm", p, 2, 2)
                    freed(act, p, n)
                    nth(act, "i_dif", p, NP, n + 1)
                    q = N_DVE + CH * n
                    ins = nc.scalar.activation(ind[s][:, q:q + CH, :], difs(s, n)[:], ACT.Sign)
                    ins.then_inc(S["i_sgn"], 1)
                elif part == "soft_m":
                    act.wait_ge(S["s_raw"], p + 1)
                    before(act, "s_pt", p, 1)
                    nc.scalar.activation(att[:].rearrange("p b t -> p (b t)"), raw[:].rearrange("p b t -> p (b t)"),
                                         ACT.Relu, bias=w("b_mlp"), scale=k("alpha")).then_inc(S["act_s"], 1)
                elif part == "soft_e":
                    act.wait_ge(S["act_s"], p + 1)
                    act.wait_ge(S["s_m"], p + 1)
                    for b in range(BG):
                        last = nc.scalar.activation(att[:, b, :], att[:, b, :], ACT.Exp, bias=nm[:, b:b + 1])
                    last.then_inc(S["s_p"], 1)
                elif part == "soft_pt":
                    act.wait_ge(S["s_pt"], p + 1)
                    nc.scalar.activation(attT[:].rearrange("p b t -> p (b t)"), pS[:], ACT.Copy).then_inc(S["s_ptT"], 1)
                elif part == "f_tr":
                    act.wait_ge(S["f_tr"], g + 1)
                    nc.scalar.activation(fxT[:].rearrange("p i t -> p (i t)"), pF[2][:, 0:256],
                                         ACT.Copy).then_inc(S["f_xT"], 1)
                elif part == "f_v":
                    act.wait_ge(S["f_v"], g + 1)
                    nc.scalar.activation(vf[:, :, :, 0:HD], pF[2][:, 256:384].rearrange(
                        "p (b v d) -> p b v d", b=4, v=NKV), ACT.Copy).then_inc(S["f_va"], 1)
                elif part == "f_exp":
                    nth(act, "f_nm", g, 4, n + 1)
                    for h in range(NH):
                        last = nc.scalar.activation(fp[n][:, h, :], pF[n][:, T * h:T * h + T], ACT.Exp,
                                                    bias=fnm[n][:, h:h + 1], scale=HD ** -0.5)
                    last.then_inc(S["f_p"], 1)
                elif part == "f_turn":
                    nth(act, "f_pt", g, 4, n + 1)
                    nc.scalar.activation(fpT[n][:].rearrange("p h t -> p (h t)"), pF[n][:],
                                         ACT.Copy).then_inc(S["f_ptT"], 1)
                elif part == "f_yt":
                    act.wait_ge(S["f_yt"], g + 1)
                    nc.scalar.activation(yT[:].rearrange("p i t -> p (i t)"), pF[0][:, 0:256],
                                         ACT.Copy).then_inc(S["f_yT"], 1)
                elif part == "f_rms":
                    act.wait_ge(S["f_x2"], g + 1)
                    for b in range(4):
                        last = nc.scalar.activation(sg[0][:, 64 * b:64 * b + 64], x2[:, b, :], ACT.Square,
                                                    scale=C ** -0.5, accum_out=ms[:, b:b + 1])
                    last.then_inc(S["f_ms"], 1)
                elif part == "f_xs":
                    act.wait_ge(S["f_xst"], g + 1)
                    nc.scalar.activation(xsT[:], pF[1][:].bitcast(F16)[:, 0:512], ACT.Copy).then_inc(S["f_xsT"], 1)
                elif part == "f_route":
                    act.wait_ge(S["f_la"], g + 1)
                    nc.scalar.activation(lg["e"][:].rearrange("p b e -> p (b e)"),
                                         lg["a"][:].rearrange("p b e -> p (b e)"), ACT.Exp).then_inc(S["f_le"], 1)
                elif part == "f_h":
                    nth(act, "f_h13", g, NT, n + 1)
                    if n >= 2:
                        nth(act, "f_hh", g, NT, n - 1)
                    elif n == 0:
                        act.wait_ge(S["f_ms"], g + 1)
                    nc.scalar.activation(sg[n % 2][:], pF[2 * (n % 2)][:], ACT.Silu).then_inc(S["f_sg"], 1)

            for p in range(2):
                do("front_norm", p, p, 0, 0)
                do("front_mm", p, p, 0, 0)
                if p == 0:
                    do("front_split", p, p, 0, 0)
            sequence(do, act, ORDER["scalar"])

        @block.gpsimd
        def _(pool):
            nc.gpsimd.memset(half[:], -0.5)
            for s in range(2):
                nc.gpsimd.memset(va[s][:], 1.0)
                nc.gpsimd.memset(bd[s][:], 0.0)
            nc.gpsimd.memset(vf[:], 1.0).then_inc(S["pool_pro"], 1)
            pool.wait_ge(S["ld_e"], 16)
            def shift(i):
                pool.wait_ge(S["z_zn"], 6 + i + 1)
                if i >= 2:
                    pool.wait_ge(S["z_st0"], 16 * (i // 2))
                z, g, o = (x[0][:, 0:512].rearrange("p (a c) -> p a c", c=C) for x in (zn, h3g, h3o))
                nc.gpsimd.tensor_tensor(g, z, w("g3").unsqueeze(1).to_broadcast([P, 8, C]),
                                        ALU.mult).then_inc(S["pool_pro"], 1)
                pool.wait_ge(S["pool_pro"], i // 2 + 2)
                nc.gpsimd.tensor_tensor(o, g, w("b3").unsqueeze(1).to_broadcast([P, 8, C]),
                                        ALU.add).then_inc(S["z_gb0"], 1)

            def do(part, p, s, g, n):
                if part == "dif":
                    pool.wait_ge(S["a_qk"], p + 1)
                    if not (isinstance(p, int) and p * NP + n < ND):
                        pool.wait_ge(S["i_sgn"], p * NP + n + 1 - ND)
                    q = N_DVE + CH * n
                    nc.gpsimd.tensor_tensor(difs(s, n)[:], qk[s][:, 0, q:q + CH].unsqueeze(2).to_broadcast([P, CH, T]),
                                            qk[s][:, 1, :].unsqueeze(1).to_broadcast([P, CH, T]),
                                            ALU.subtract).then_inc(S["i_dif"], 1)
                elif part == "front_stat":
                    ch = Chain(pool, "pool_a", p, 1)
                    pool.wait_ge(S["a_mv"], p + 1)
                    ch.link(nc.gpsimd.tensor_tensor(ve[:], mv[:, :, 1], k("ln_eps")[:, 0:2], ALU.add))
                    ch.end()
                    nc.gpsimd.tensor_tensor(rstd[:], ve[:], half[:, 0:2], ALU.pow).then_inc(S["a_rstd"], 1)
                elif part == "f_stat":
                    pool.wait_ge(S["f_ve"], g + 1)
                    nc.gpsimd.tensor_tensor(frr[:], fu[:], half[:], ALU.pow).then_inc(S["f_r"], 1)
                elif part == "f_norm":
                    ch = Chain(pool, "pool_x", g, 4)
                    pool.wait_ge(S["f_mv"], g + 1)
                    ch.link(nc.gpsimd.tensor_tensor(fv[:], fmv[:, :, 1], k("ln_eps"), ALU.add))
                    ch.link(nc.gpsimd.tensor_tensor(fr[:], fv[:], half[:], ALU.pow))
                    before(pool, "f_x2", g, 1)
                    ch.link(nc.gpsimd.tensor_tensor(fx[:], h1[:], fmv[:, :, 0:1].to_broadcast([P, 4, C]),
                                                    ALU.subtract))
                    ch.link(nc.gpsimd.tensor_tensor(fx[:], fx[:], fr[:].unsqueeze(2).to_broadcast([P, 4, C]),
                                                    ALU.mult))
                    ch.end()
                    before(pool, "f_res", g, 1)
                    nc.gpsimd.tensor_tensor(rx[:], h1[:], fx[:], ALU.add).then_inc(S["f_xo"], 1)
                elif part == "f_ke":
                    nc.gpsimd.memset(pause_p[:], 0.0).then_inc(S["pool_done"], 1)
                    pool.wait_ge(S["pool_done"], g + 1)
                    pool.wait_ge(S["f_krope"], g + 1)
                    for h in range(2, NH):
                        rows = slice(HP * h, HP * h + HP)
                        last = nc.gpsimd.tensor_tensor(ke[rows, :, h, :], r3[rows], r4[rows], ALU.add)
                    last.then_inc(S["f_kep"], 1)
                    pool.wait_ge(S["f_kep"], g + 1)
                elif part == "f_s":
                    nth(pool, "f_oe", g, 4, 2 * n + 2)
                    ch = Chain(pool, "pool_o", 2 * g + n, 3)
                    x = oe[n]
                    ch.link(nc.gpsimd.tensor_tensor(o4[:], x[:, :, 0:4, :], x[:, :, 4:8, :], ALU.add))
                    ch.link(nc.gpsimd.tensor_tensor(o2[:], o4[:, :, 0:2, :], o4[:, :, 2:4, :], ALU.add))
                    ch.link(nc.gpsimd.tensor_tensor(o1[:], o2[:, :, 0, :], o2[:, :, 1, :], ALU.add))
                    ch.end()
                    if n == 0:
                        pool.wait_ge(S["f_res"], g + 1)
                        if not (isinstance(g, int) and g == 0):
                            pool.wait_ge(S["st_out"], g * 16)
                    nc.gpsimd.tensor_tensor(fo[:, 2 * n:2 * n + 2, :], res[:, 2 * n:2 * n + 2, :], o1[:],
                                            ALU.add).then_inc(S["f_out"], 1)
                elif part == "f_rms":
                    pool.wait_ge(S["f_ms"], g + 1)
                    nc.gpsimd.tensor_tensor(fm[:], ms[:], k("rms_eps"), ALU.add).then_inc(S["f_rq"], 1)
                    nth(pool, "f_rq", g, 2, 1)
                    nc.gpsimd.tensor_tensor(fq[:], fm[:], half[:], ALU.pow).then_inc(S["f_rq"], 1)

            pool.wait_ge(S["ld_w"], 16)
            pool.wait_ge(S["ld_h"], 16)
            for name, norm in (("rope", "ln1"), ("vf", "ln1"), ("router", "ln2")):
                nc.gpsimd.tensor_tensor(w(name), w(name), w(norm).to_broadcast(
                    [P, WCOL[name][1] - WCOL[name][0]]), ALU.mult)
            pool.wait_ge(S["ld_w13"], 16)
            n13 = NT * P
            raw13 = w13raw[:, 0:2 * n13]
            nc.gpsimd.tensor_tensor(raw13, raw13, w("ln2").to_broadcast([P, 2 * n13]), ALU.mult).then_inc(S["w_ln"], 1)
            pool.wait_ge(S["w_ln"], 1)
            split = ((wrh[:], wrl[:], w("router")),
                     (w1h[:].rearrange("p t n -> p (t n)"), w1l[:].rearrange("p t n -> p (t n)"), raw13[:, 0:n13]),
                     (w3h[:].rearrange("p t n -> p (t n)"), w3l[:].rearrange("p t n -> p (t n)"), raw13[:, n13:]))
            for high, low, x in split:
                last = nc.gpsimd.tensor_copy(high, x)
            last.then_inc(S["w_ln"], 1)
            pool.wait_ge(S["w_ln"], 2)
            for high, low, x in split:
                last = nc.gpsimd.tensor_tensor(low, x, high, ALU.subtract)
            last.then_inc(S["w_split"], 1)
            for i in range(0, 8, 2):
                shift(i)
                if i >= 4:
                    do("front_stat", i // 2 - 2, i // 2 - 2, 0, 0)
            sequence(do, pool, ORDER["gpsimd"])

        @block.vector
        def _(dve):
            ch = Chain(dve, "dve_pro", 0, 10)
            nc.vector.memset(ke[:], 0.0)
            dve.wait_ge(S["ld_c"], 32)
            dve.wait_ge(S["ld_k"], 16)
            nc.vector.tensor_copy(maskb[:], k("causal"))
            nc.vector.tensor_copy(identb[:], k("ident"))
            ch.link(nc.vector.tensor_scalar(cf[0:24, :], craw[0:24, :], k("scale")[0:24, :], -1.0, ALU.mult, ALU.add))
            nc.vector.tensor_tensor(cT[0:24, :], cf[0:24, :], vraw[0:24, :], ALU.mult).then_inc(S["c_ready"], 1)
            dve.wait_ge(S["ld_e"], 16)
            srcs = [(w("t1"), 0, D1), (w("t2"), D1, D2), (w("t3"), D1 + D2, C)]
            for i, (src, at, n) in enumerate(srcs):
                ch.step(nc.vector.tensor_reduce(wm[:, i:i + 1], src, AX, ALU.add))
            ch.wait()
            for i, (src, at, n) in enumerate(srcs):
                ch.step(nc.vector.tensor_scalar(wn[:, i:i + 1], wm[:, i:i + 1], -1.0 / n, None, ALU.mult))
            ch.wait()
            for i, (src, at, n) in enumerate(srcs):
                ch.step(nc.vector.tensor_scalar(wc[:, at:at + n], src, wn[:, i:i + 1], None, ALU.add))
            ch.wait()
            ch.end()
            for dst, mask, nb, at, n in ((w1bd, "m1", 8, 0, D1), (w2bd, "m2", 8, D1, D2), (w3bd, "m3", 4, D1 + D2, C)):
                last = nc.vector.tensor_tensor(dst[:, 0:nb * n].rearrange("p (b n) -> p b n", b=nb),
                                               wc[:, at:at + n].unsqueeze(1).to_broadcast([P, nb, n]),
                                               k(mask).unsqueeze(2).to_broadcast([P, nb, n]), ALU.mult)
            last.then_inc(S["wbd_ready"], 1)

            def mean_square(u):
                width = D1 if u < 2 else D2 if u < 6 else C
                dve.wait_ge(S["z_sq"], u + 1)
                if u >= 2:
                    dve.wait_ge(S["z_sd"], u - 1)
                nc.vector.tensor_reduce(pms[u % 2][:, 0:512 // width],
                                        sq[u % 2][:, 0:512].rearrange("p (a c) -> p a c", c=width),
                                        AX, ALU.add).then_inc(S["z_ms"], 1)

            def normalise(u):
                width = D1 if u < 2 else D2 if u < 6 else C
                n = 512 // width
                z = [pT[:, 0:512], pT[:, 512:1024], pF[0][:], pF[1][:]][u % 4]
                dve.wait_ge(S["z_sd"], u + 1)
                nc.vector.reciprocal(prs[u % 2][:, 0:n], psd[u % 2][:, 0:n]).then_inc(S["z_rs"], 1)
                dve.wait_ge(S["z_rs"], u + 1)
                if 2 <= u < 8:
                    dve.wait_ge(S["z_tr"], u - 1)
                elif u >= 8:
                    dve.wait_ge(S[f"z_gb{u % 2}"], (u - 8) // 2 + 1)
                nc.vector.tensor_tensor(zn[u % 2][:, 0:512].rearrange("p (a c) -> p a c", c=width),
                                        z.rearrange("p (a c) -> p a c", c=width),
                                        prs[u % 2][:, 0:n].unsqueeze(2).to_broadcast([P, n, width]),
                                        ALU.mult).then_inc(S["z_zn"], 1)

            def shift(i):
                if i >= 2:
                    dve.wait_ge(S["z_st1"], 16 * (i // 2))
                z, g, o = (x[1][:, 0:512].rearrange("p (a c) -> p a c", c=C) for x in (zn, h3g, h3o))
                dve.wait_ge(S["z_zn"], 6 + i + 1)
                nc.vector.tensor_tensor(g, z, w("g3").unsqueeze(1).to_broadcast([P, 8, C]),
                                        ALU.mult).then_inc(S["dve_gb"], 1)
                dve.wait_ge(S["dve_gb"], i // 2 + 1)
                nc.vector.tensor_tensor(o, g, w("b3").unsqueeze(1).to_broadcast([P, 8, C]),
                                        ALU.add).then_inc(S["z_gb1"], 1)

            def rotate(a, b, cosine, sine):
                cos = k("cos").unsqueeze(1).to_broadcast([P, 4, T])
                sin = k("sin").unsqueeze(1).to_broadcast([P, 4, T])
                nc.vector.tensor_tensor(cosine[:], a[:].rearrange("p (b t) -> p b t", b=4), cos, ALU.mult)
                return nc.vector.tensor_tensor(sine[:], b[:].rearrange("p (b t) -> p b t", b=4), sin, ALU.mult)

            def do(part, p, s, g, n):
                if part == "front_stat":
                    ch = Chain(dve, "dve_front", p, 1)
                    nth(dve, f"ld_a{s}", g, 16, 16)
                    before(dve, "a_xn", p, 1)
                    for b in range(2):
                        last = nc.vector.bn_stats(stat[:, b, :], hin[s][:, b, :])
                    ch.link(last)
                    ch.end()
                    nc.vector.memset(pause[:], 0.0)
                    for b in range(2):
                        last = nc.vector.bn_aggr(mv[:, b, :], stat[:, b, :])
                    last.then_inc(S["a_mv"], 1)
                elif part == "front_norm":
                    dve.wait_ge(S["a_rstd"], p + 1)
                    dve.wait_ge(S["a_mv"], p + 1)
                    before(dve, "a_tr", p, 1)
                    for b in range(2):
                        last = nc.vector.tensor_scalar(xn[:, b, :], hin[s][:, b, :], mv[:, b, 0:1], rstd[:, b:b + 1],
                                                       ALU.subtract, ALU.mult)
                    last.then_inc(S["a_xn"], 1)
                elif part == "front_split":
                    dve.wait_ge(S["a_hi"], p + 1)
                    for b in range(BG):
                        rows = slice(DG * b, DG * b + DG)
                        last = nc.vector.scalar_tensor_tensor(bd[s][rows, :, :, 1, b], qk[s][rows], w("w_mlp")[rows],
                                                              bd[s][rows, :, :, 0, b], ALU.mult, ALU.subtract)
                    last.then_inc(S["a_bd"], 1)
                elif part == "cmp":
                    if n == 0:
                        before(dve, "t1_mm", p, 2, 2)
                        freed(dve, p, n)
                        dve.wait_ge(S["a_qk"], p + 1)
                    q = CV * n
                    ins = nc.vector.tensor_tensor(ind[s][:, q:q + CV, :],
                                                  qk[s][:, 1, :].unsqueeze(1).to_broadcast([P, CV, T]),
                                                  qk[s][:, 0, q:q + CV].unsqueeze(2).to_broadcast([P, CV, T]),
                                                  ALU.is_lt)
                    if n == N_DVE // CV - 1:
                        ins.then_inc(S["i_dve"], 1)
                elif part == "red2":
                    nth(dve, "t2_mm", p, 2, n + 1)
                    half_k, bank = slice(T // 2 * n, T // 2 * n + T // 2), slice(512 * n, 512 * n + 512)
                    nc.vector.tensor_reduce(t2s[:, :, half_k], pT[:, bank].rearrange("p (k r b) -> p b k r", r=2, b=BG),
                                            AX, ALU.add, negate=True).then_inc(S["t2_s"], 1)
                elif part == "red1":
                    nth(dve, "t1_mm", p, 2, n + 1)
                    before(dve, "s_tp", p, 1)
                    half_q, bank = slice(T // 2 * n, T // 2 * n + T // 2), slice(512 * n, 512 * n + 512)
                    nc.vector.tensor_reduce(t1s[:, :, half_q], pT[:, bank].rearrange("p (k r b) -> p b k r", r=2, b=BG),
                                            AX, ALU.add).then_inc(S["t1_s"], 1)
                elif part == "soft_m":
                    dve.wait_ge(S["s_tp"], p + 1)
                    nth(dve, "t2_s", p, 2, 2)
                    before(dve, "act_s", p, 1)
                    nc.vector.tensor_tensor(raw[:].rearrange("p b t -> p (b t)"), pS[:],
                                            t2s[:].rearrange("p b t -> p (b t)"), ALU.add).then_inc(S["s_raw"], 1)
                    dve.wait_ge(S["s_raw"], p + 1)
                    ch = Chain(dve, "dve_soft", p, 2)
                    ch.link(nc.vector.tensor_reduce(mx[:], raw[:], AX, ALU.max))
                    ch.link(nc.vector.tensor_scalar(mb[:], mx[:], k("alpha"), w("b_mlp"), ALU.mult, ALU.add))
                    ch.end()
                    before(dve, "s_p", p, 1)
                    nc.vector.tensor_scalar(nm[:], mb[:], 0.0, -1.0, ALU.max, ALU.mult).then_inc(S["s_m"], 1)
                elif part == "pair_add":
                    dve.wait_ge(S["s_pv"], p + 1)
                    pv = pS[:, 0:BG * VW].rearrange("p (b v) -> p b v", v=VW)
                    ch = Chain(dve, "dve_value", p, 2)
                    ch.link(nc.vector.reciprocal(rden[:], pv[:, :, DG]))
                    ch.link(nc.vector.tensor_tensor(add[:].rearrange("p b (d g) -> p b g d", g=G2),
                                                    pv[:, :, 0:DG].rearrange("p (b g) d -> p b g d", g=G2),
                                                    rden[:].rearrange("p (b g) -> p b g", g=G2).unsqueeze(3)
                                                    .to_broadcast([P, 2, G2, DG]), ALU.mult))
                    ch.end()
                    nth(dve, f"ld_r{s}", g, 16, 16)
                    nc.vector.tensor_tensor(h1[:, 2 * s:2 * s + 2, :], h1[:, 2 * s:2 * s + 2, :], add[:],
                                            ALU.add).then_inc(S["s_h1"], 1)
                elif part == "f_stat":
                    dve.wait_ge(S["s_h1"], g * 2 + 2)
                    ch = Chain(dve, "dve_rope", g, 1)
                    for b in range(4):
                        last = nc.vector.bn_stats(fstat[:, b, :], h1[:, b, :])
                    ch.link(last)
                    ch.end()
                    nc.vector.memset(pause[:], 0.0)
                    for b in range(4):
                        last = nc.vector.bn_aggr(fmv[:, b, :], fstat[:, b, :])
                    last.then_inc(S["f_mv"], 1)
                    dve.wait_ge(S["f_mv"], g + 1)
                    nc.vector.tensor_scalar(fu[:], fmv[:, :, 1], 1.0 + RMS_EPS, RMS_EPS * LN_EPS, ALU.mult,
                                            ALU.add).then_inc(S["f_ve"], 1)
                elif part == "f_norm":
                    dve.wait_ge(S["f_r"], g + 1)
                    for b in range(4):
                        last = nc.vector.tensor_scalar(fxr[:, b, :], h1[:, b, :], fmv[:, b, 0:1], frr[:, b:b + 1],
                                                       ALU.subtract, ALU.mult)
                    last.then_inc(S["f_x"], 1)
                elif part == "f_rotq":
                    dve.wait_ge(S["f_q"], g + 1)
                    rotate(pF[3], pF[2], r1, r2).then_inc(S["f_qrope"], 1)
                elif part == "f_qe":
                    dve.wait_ge(S["f_qrope"], g + 1)
                    nc.vector.tensor_tensor(qe[:], r1[:], r2[:], ALU.add).then_inc(S["f_qe"], 1)
                elif part == "f_rotk":
                    dve.wait_ge(S["f_k"], g + 1)
                    rotate(pF[0], pF[1], r3, r4).then_inc(S["f_krope"], 1)
                elif part == "f_ke":
                    dve.wait_ge(S["f_krope"], g + 1)
                    for h in range(2):
                        rows = slice(HP * h, HP * h + HP)
                        last = nc.vector.tensor_tensor(ke[rows, :, h, :], r3[rows], r4[rows], ALU.add)
                    last.then_inc(S["f_ke"], 1)
                elif part == "f_max":
                    nth(dve, "f_sc", g, 4, n + 1)
                    nc.vector.tensor_reduce(fmx[n][:], pF[n][:].rearrange("p (h t) -> p h t", h=NH),
                                            AX, ALU.max).then_inc(S["f_max"], 1)
                    nth(dve, "f_max", g, 4, n + 1)
                    nc.vector.tensor_scalar(fnm[n][:], fmx[n][:], -HD ** -0.5, None, ALU.mult).then_inc(S["f_nm"], 1)
                elif part == "f_weigh":
                    nth(dve, "f_pv", g, 4, n + 1)
                    pv = pF[n][:, 0:NH * KW].rearrange("p (h v) -> p h v", v=KW)
                    nc.vector.reciprocal(frd[n][:], pv[:, :, HD]).then_inc(S["f_rd"], 1)
                    nth(dve, "f_rd", g, 4, n + 1)
                    nc.vector.tensor_tensor(y[:, n, :].rearrange("p (h d) -> p h d", h=NH), pv[:, :, 0:HD],
                                            frd[n][:].unsqueeze(2).to_broadcast([P, NH, HD]),
                                            ALU.mult).then_inc(S["f_y"], 1)
                elif part == "f_wo":
                    dve.wait_ge(S["f_wo"], g + 1)
                    wo = pF[0][:, 256:512].rearrange("p (b c) -> p b c", b=4)
                    dve.wait_ge(S["f_xo"], g + 1)
                    nc.vector.tensor_tensor(x2[:], fx[:], wo, ALU.add).then_inc(S["f_x2"], 1)
                    before(dve, "f_out", g, 2)
                    nc.vector.tensor_tensor(res[:], rx[:], wo, ALU.add).then_inc(S["f_res"], 1)
                elif part == "f_x2":
                    nth(dve, "f_rq", g, 2, 2)
                    dve.wait_ge(S["f_x2"], g + 1)
                    nc.vector.tensor_tensor(xf[:], x2[:], fq[:].unsqueeze(2).to_broadcast([P, 4, C]),
                                            ALU.mult).then_inc(S["f_xf"], 1)
                elif part == "f_xs":
                    nth(dve, "f_xf", g, 2, 1)
                    before(dve, "f_xst", g, 1)
                    nc.vector.tensor_copy(xs[:, :, 0, :], xf[:]).then_inc(S["f_xf"], 1)
                    nth(dve, "f_xf", g, 2, 2)
                    nc.vector.tensor_tensor(xs[:, :, 1, :], xf[:], xs[:, :, 0, :], ALU.subtract).then_inc(S["f_xs"], 1)
                elif part == "f_route":
                    dve.wait_ge(S["f_lg"], g + 1)
                    logits = pF[2][:, 0:4 * NE].rearrange("p (b e) -> p b e", b=4)
                    ct = Chain(dve, "dve_top", g, 21)
                    ct.link(nc.vector.tensor_reduce(l1["mx"][:], logits, AX, ALU.max))
                    nc.vector.tensor_tensor(lg["a"][:], logits, l1["mx"][:].unsqueeze(2).to_broadcast([P, 4, NE]),
                                            ALU.subtract).then_inc(S["f_la"], 1)
                elif part == "f_top":
                    top2(g, n)
                elif part == "f_h":
                    nth(dve, "f_sg", g, NT, n + 1)
                    nc.vector.tensor_tensor(hh[:, n, :], sg[n % 2][:], pF[2 * (n % 2) + 1][:],
                                            ALU.mult).then_inc(S["f_hh"], 1)
                elif part == "f_o":
                    nth(dve, "f_e", g, 4, n + 1)
                    before(dve, "f_out", g, 2)
                    nc.vector.tensor_tensor(oe[n // 2][:, n % 2], pF[n % 2][:].rearrange("p (e c) -> p e c", e=NE),
                                            lg["wt"][:, n, :].unsqueeze(2).to_broadcast([P, NE, C]),
                                            ALU.mult).then_inc(S["f_oe"], 1)

            def top2(g, half):
                ch = Chain(dve, "dve_top", g, 21)
                ch.n = (1, 10)[half]
                v = nc.vector

                def wide(x):
                    return x[:].unsqueeze(2).to_broadcast([P, 4, NE])

                rank = k("rank").unsqueeze(1).to_broadcast([P, 4, NE])

                def largest(probs, m, c, sel):
                    ch.link(v.tensor_reduce(l1[m][:], lg[probs][:], AX, ALU.max))
                    ch.link(v.tensor_tensor(lg["eq"][:], lg[probs][:], wide(l1[m]), ALU.is_equal))
                    ch.link(v.tensor_tensor(lg["c"][:], lg["eq"][:], rank, ALU.mult))
                    ch.link(v.tensor_reduce(l1[c][:], lg["c"][:], AX, ALU.max))
                    ch.link(v.tensor_tensor(lg[sel][:], lg["c"][:], wide(l1[c]), ALU.is_equal))

                if half == 0:
                    dve.wait_ge(S["f_le"], g + 1)
                    ch.link(v.tensor_reduce(l1["z"][:], lg["e"][:], AX, ALU.add))
                    ch.link(v.reciprocal(l1["rz"][:], l1["z"][:]))
                    ch.link(v.tensor_tensor(lg["p"][:], lg["e"][:], wide(l1["rz"]), ALU.mult))
                    largest("p", "m1", "c1", "s1")
                    ch.link(v.scalar_tensor_tensor(lg["p2"][:], lg["s1"][:], -2.0, lg["p"][:], ALU.mult, ALU.add))
                    assert ch.n == 10
                    return
                largest("p2", "m2", "c2", "s2")
                ch.step(v.tensor_tensor(lg["eq"][:], lg["s1"][:], lg["s2"][:], ALU.add))
                ch.link(v.tensor_tensor(l1["st"][:], l1["m1"][:], l1["m2"][:], ALU.add))
                ch.step(v.tensor_tensor(lg["tp"][:], lg["p"][:], lg["eq"][:], ALU.mult))
                ch.link(v.tensor_scalar(l1["de"][:], l1["st"][:], 1.0, TOP_EPS, ALU.mult, ALU.add))
                ch.link(v.reciprocal(l1["rd"][:], l1["de"][:]))
                ch.link(v.tensor_tensor(lg["wt"][:], lg["tp"][:], wide(l1["rd"]), ALU.mult))
                ch.end()

            for u in (0, 2, 4, 6):
                mean_square(u)
                mean_square(u + 1)
                if u < 6:
                    normalise(u)
                    normalise(u + 1)
            for u in (6, 8, 10, 12):
                if u < 12:
                    mean_square(u + 2)
                    mean_square(u + 3)
                normalise(u)
                normalise(u + 1)
                shift(u - 5)
                if u == 8:
                    do("front_stat", 0, 0, 0, 0)
                elif u == 10:
                    do("front_norm", 0, 0, 0, 0)
                    do("front_stat", 1, 1, 0, 0)
            do("front_norm", 1, 1, 0, 0)
            do("front_split", 0, 0, 0, 0)
            sequence(do, dve, ORDER["vector"])


def _block_rows(a, n):
    r, c = a.shape
    out = np.zeros((n * r, n * c), a.dtype)
    for i in range(n):
        out[i * r:(i + 1) * r, i * c:(i + 1) * c] = a
    return out


def _pack(cols, width, parts, dtype):
    out = np.zeros((P, width), dtype)
    for name, a in parts.items():
        lo, hi = cols[name]
        out[:a.shape[0], lo:hi] = a.reshape(a.shape[0], -1)
    return out


def _tokens(a):
    return a.reshape(4, 8, 2, T).transpose(0, 2, 1, 3).reshape(8, 1, 8 * T)


def _rope_rows(wm, perm):
    heads = wm.shape[0] // HD
    rows = np.zeros((NH, HP, C), wm.dtype)
    for h in range(NH):
        rows[h, :HD] = wm.reshape(heads, HD, C)[h * heads // NH][perm]
    return rows.reshape(P, C).T


def _weights(x):
    f = lambda n: np.asarray(x[n])
    col = lambda a, n: np.tile(a, n)[:, None]
    same, swap = np.arange(HD), (np.arange(HD) + HD // 2) % HD
    rope = np.zeros((2, C, 4, 2, P), np.float32)
    for m, (name, perm) in enumerate((("L0_ffn_wq", same), ("L0_ffn_wq", swap), ("L0_ffn_wk", same),
                                      ("L0_ffn_wk", swap))):
        for b in range(2):
            rope[b, :, m, b] = _rope_rows(f(name), perm)
    w2 = np.zeros((P, NT, 2, C), np.float32)
    for e in range(NE):
        for i in range(HID):
            n = e * HID + i
            w2[n % P, n // P, e - first_expert(n // P)] = f("L0_ffn_w2")[e, :, i]
    parts = {
        "qk": np.concatenate([_block_rows(f("L0_attn_Wq").T, 2), _block_rows(f("L0_attn_Wk").T, 2)], 1),
        "v": _block_rows(f("L0_attn_Wv").T, 2),
        "rope": rope.reshape(P, -1), "vf": _block_rows(f("L0_ffn_wv").T, 2), "wo": _block_rows(f("L0_ffn_wo").T, 2),
        "router": np.tile(f("L0_ffn_router_w").T, (2, 1)), "w2": w2,
        "w_mlp": col(f("L0_attn_w_mlp"), 4), "b_mlp": col(f("L0_attn_b_mlp"), P),
        "ln1": col(f("L0_ffn_ln1_w"), 2), "ln2": col(f("L0_ffn_ln2_w"), 2),
        "g1": col(f("L0_tok_g1"), 8), "b1": col(f("L0_tok_b1"), 8), "g2": col(f("L0_tok_g2"), 4),
        "b2": col(f("L0_tok_b2"), 4), "g3": np.tile(f("L0_tok_g3"), (P, 1)), "b3": np.tile(f("L0_tok_b3"), (P, 1)),
        "t1": np.tile(f("L0_tok_W1"), (8, 1)), "t2": np.tile(f("L0_tok_W2"), (8, 1)),
        "t3": np.tile(f("L0_tok_W3"), (4, 1)),
    }
    w13 = np.zeros((2, C, 2, NT * P), np.float32)
    w13[:, :, 0, :NE * HID] = f("L0_ffn_w1").reshape(NE * HID, C).T
    w13[:, :, 1, :NE * HID] = f("L0_ffn_w3").reshape(NE * HID, C).T
    return _pack(WCOL, WWIDTH, parts, np.float32), w13.reshape(P, -1)


def _constants():
    inv_freq = 1.0 / 10000.0 ** (np.arange(0, HD, 2, dtype=np.float32) / HD)
    freqs = np.outer(np.arange(T, dtype=np.float32), inv_freq)
    emb = np.concatenate([freqs, freqs], axis=-1)
    cos, sin = np.zeros((NH, HP, T), np.float32), np.zeros((NH, HP, T), np.float32)
    cos[:, :HD] = np.cos(emb).T
    sin[:, :HD] = np.sin(emb).T * np.where(np.arange(HD) < HD // 2, -1.0, 1.0)[:, None]
    q, key = np.arange(P)[:, None], np.arange(T)[None, :]
    sizes = np.array([160, 120, 2], np.float32)
    parts = {
        "ident": np.eye(P), "cos": cos.reshape(P, T), "sin": sin.reshape(P, T),
        "causal": np.where(key <= q, 0.0, BIG), "rank": np.tile(np.arange(NE, 0, -1), (P, 1)),
        "alpha": np.where(q < N_DVE, 1.0, 0.5), "scale": np.tile((2.0 / (sizes - 1))[:, None], (8, 1)),
        "bias": np.full((P, 1), -1.0), "m1": np.arange(P)[:, None] // 3 == np.arange(8),
        "m2": q // D1 == np.arange(8), "m3": q // D2 == np.arange(4), "eps": np.full((P, 1), LN_EPS),
        "ln_eps": np.full((P, 4), LN_EPS), "rms_eps": np.full((P, 4), RMS_EPS),
    }
    half = {"ident": np.eye(P), "sign_rows": np.ones((P, 1)) * (key >= N_DVE), "ones": np.ones((P, P)),
            "bg": q // DG == np.arange(BG)}
    return _pack(KCOL, KWIDTH, parts, np.float32), _pack(HCOL, HWIDTH, half, np.float16)


def kernel(**inputs):
    import concourse.bacc as bacc
    from concourse.bass_utils import run_bass_kernel_spmd

    tok = [np.asarray(inputs[n]) for n in ("x", "itok_BS_0_479", "mask_BS_i1_0")]
    valid = np.asarray(inputs["mask_BS_b1_0"]).view(np.uint8)
    wts, w13 = _weights(inputs)
    kf, kh = _constants()
    arrays = {
        "coords": np.concatenate([_tokens(a) for a in tok], 1).reshape(24, 8 * T),
        "valid": np.concatenate([_tokens(valid)] * 3, 1).reshape(24, 8 * T),
        "wts": wts, "w13": w13, "kf": kf, "kh": kh,
    }
    nc = bacc.Bacc("TRN2", target_bir_lowering=False, num_devices=1)
    args = [nc.dram_tensor(n, a.shape, mybir.dt.from_np(a.dtype), kind="ExternalInput").ap()
            for n, a in arrays.items()]
    args.append(nc.dram_tensor("out", (GROUPS, 4, T, C), F32, kind="ExternalOutput").ap())
    tower(nc, *args)
    r = run_bass_kernel_spmd(nc, [arrays], core_ids=[0])
    return r.results[0]["out"].reshape(B, T, C)
```
